# Optimizing a Trainium2 kernel written in Bass

```python
import numpy as np
import jax
import jax.numpy as jnp

def _softmax(x, axis=-1):
    return jax.nn.softmax(x, axis=axis)

def _gelu(x):
    return jax.nn.gelu(x, approximate=True)

def _silu(x):
    return jax.nn.silu(x)

def _sigmoid(x):
    return jax.nn.sigmoid(x)

def _layernorm(x, axis=-1, eps=1e-05):
    m = jnp.mean(x, axis=axis, keepdims=True)
    v = jnp.var(x, axis=axis, keepdims=True)
    return (x - m) / jnp.sqrt(v + eps)

def _scatter_add(tgt, idx, src, axis=0):
    return tgt.at[idx].add(src)

def _segment_sum(src, seg, n):
    return jax.ops.segment_sum(src, seg, n)
kernel_name = 'mk_gnn_resnorm_d2_gnn_r64_f189a7'

def setup_inputs(seed: int=0):
    np.random.seed(seed)
    _w = jnp.asarray

    def _rec_inputs():
        import jax
        import jax.numpy as jnp
        _gk = jax.random.key(seed)
        x = -0.0003713 + 1 * jax.random.normal(jax.random.fold_in(_gk, 1), (50000, 256), jnp.float32)
        src = jax.random.randint(jax.random.fold_in(_gk, 2), (12500,), 0, 50000, jnp.int32)
        dst = jax.random.randint(jax.random.fold_in(_gk, 3), (12500,), 0, 50000, jnp.int32)
        _o = jnp.argsort(dst, stable=True)
        src = src[_o]
        dst = dst[_o]
        edge_attr_256 = 0.000133148 + 1.00009 * jax.random.normal(jax.random.fold_in(_gk, 12), (12500, 256), jnp.float32)
        edge_attr_256_n2 = 0.000133148 + 1.00009 * jax.random.normal(jax.random.fold_in(_gk, 13), (12500, 256), jnp.float32)
        edge_type_2 = jax.random.randint(jax.random.fold_in(_gk, 15), (12500,), 0, 2, jnp.int32)
        return (x, src, dst, edge_attr_256, edge_attr_256_n2, edge_type_2)
    x, src, dst, edge_attr_256, edge_attr_256_n2, edge_type_2 = _rec_inputs()

    def _L0_gnn_setup():
        import jax, jax.numpy as jnp
        import numpy as np
        N, E, H = (50000, 6250, 256)
        EPS = 1e-05

        def _bn(h, g, b):
            mean = h.mean(0)
            var = h.var(0)
            return (h - mean) * jax.lax.rsqrt(var + EPS) * g + b
        key = jax.random.key(seed)
        ks = jax.random.split(key, 12)
        s = 1.0 / np.sqrt(H)
        return {'x': jax.random.normal(ks[0], (N, H), jnp.float32), 'edge_index': jax.random.randint(ks[1], (2, E), 0, N, jnp.int32), 'edge_attr': jax.random.normal(ks[2], (E, H), jnp.float32), 'bases': jax.random.normal(ks[3], (E, H), jnp.float32), 'W_pre': jax.random.normal(ks[4], (H, H), jnp.float32) * s, 'b_pre': jnp.zeros((H,), jnp.float32), 'W1': jax.random.normal(ks[5], (H, H), jnp.float32) * s, 'b1': jnp.zeros((H,), jnp.float32), 'g1': jnp.ones((H,), jnp.float32), 'be1': jnp.zeros((H,), jnp.float32), 'W2': jax.random.normal(ks[6], (H, H), jnp.float32) * s, 'b2': jnp.zeros((H,), jnp.float32), 'g2': jnp.ones((H,), jnp.float32), 'be2': jnp.zeros((H,), jnp.float32)}
    _L0_gnn_all = _L0_gnn_setup()
    _L0_gnn_in = {k: v for k, v in _L0_gnn_all.items() if k in ('W_pre', 'b_pre', 'W1', 'b1', 'g1', 'be1', 'W2', 'b2', 'g2', 'be2')}
    del _L0_gnn_all

    def _L1_gnn_setup():
        import jax, jax.numpy as jnp
        import numpy as np
        N_NODES = 10000
        N_EDGES = 5000
        D = 256
        D_OUT = 256
        NUM_REL = 2
        key = jax.random.key(seed)
        ks = jax.random.split(key, 16)
        s = 1.0 / np.sqrt(D)
        inp = {}
        inp['feat'] = jax.random.normal(ks[0], (N_NODES, D), dtype=jnp.float32)
        inp['src'] = jax.random.randint(ks[1], (N_EDGES,), 0, N_NODES, dtype=jnp.int32)
        inp['dst'] = jax.random.randint(ks[2], (N_EDGES,), 0, N_NODES, dtype=jnp.int32)
        inp['rel'] = jax.random.randint(ks[3], (N_EDGES,), 0, NUM_REL, dtype=jnp.int32)
        inp['W_rel'] = jax.random.normal(ks[4], (NUM_REL, D, D), dtype=jnp.float32) * s
        inp['b_rel'] = jax.random.normal(ks[5], (NUM_REL, D), dtype=jnp.float32) * s
        inp['W_ih'] = jax.random.normal(ks[6], (4 * D, D), dtype=jnp.float32) * s
        inp['b_ih'] = jax.random.normal(ks[7], (4 * D,), dtype=jnp.float32) * s
        inp['b_hh'] = jax.random.normal(ks[8], (4 * D,), dtype=jnp.float32) * s
        h = D // 2
        inp['W1'] = jax.random.normal(ks[9], (h, D), dtype=jnp.float32) * s
        inp['b1'] = jax.random.normal(ks[10], (h,), dtype=jnp.float32) * s
        inp['W2'] = jax.random.normal(ks[11], (h, h), dtype=jnp.float32) * (1.0 / np.sqrt(h))
        inp['b2'] = jax.random.normal(ks[12], (h,), dtype=jnp.float32) * (1.0 / np.sqrt(h))
        inp['W3'] = jax.random.normal(ks[13], (D_OUT, h), dtype=jnp.float32) * (1.0 / np.sqrt(h))
        inp['b3'] = jax.random.normal(ks[14], (D_OUT,), dtype=jnp.float32) * (1.0 / np.sqrt(h))
        return inp
    _L1_gnn_all = _L1_gnn_setup()
    _L1_gnn_in = {k: v for k, v in _L1_gnn_all.items() if k in ('W_rel', 'b_rel', 'W_ih', 'b_ih', 'b_hh', 'W1', 'b1', 'W2', 'b2', 'W3', 'b3')}
    del _L1_gnn_all
    return {'x': x, 'src': src, 'dst': dst, 'edge_attr_256': edge_attr_256, 'edge_attr_256_n2': edge_attr_256_n2, 'edge_type_2': edge_type_2, 'L0_gnn_W_pre': _L0_gnn_in['W_pre'], 'L0_gnn_b_pre': _L0_gnn_in['b_pre'], 'L0_gnn_W1': _L0_gnn_in['W1'], 'L0_gnn_b1': _L0_gnn_in['b1'], 'L0_gnn_g1': _L0_gnn_in['g1'], 'L0_gnn_be1': _L0_gnn_in['be1'], 'L0_gnn_W2': _L0_gnn_in['W2'], 'L0_gnn_b2': _L0_gnn_in['b2'], 'L0_gnn_g2': _L0_gnn_in['g2'], 'L0_gnn_be2': _L0_gnn_in['be2'], 'L1_gnn_W_rel': _L1_gnn_in['W_rel'], 'L1_gnn_b_rel': _L1_gnn_in['b_rel'], 'L1_gnn_W_ih': _L1_gnn_in['W_ih'], 'L1_gnn_b_ih': _L1_gnn_in['b_ih'], 'L1_gnn_b_hh': _L1_gnn_in['b_hh'], 'L1_gnn_W1': _L1_gnn_in['W1'], 'L1_gnn_b1': _L1_gnn_in['b1'], 'L1_gnn_W2': _L1_gnn_in['W2'], 'L1_gnn_b2': _L1_gnn_in['b2'], 'L1_gnn_W3': _L1_gnn_in['W3'], 'L1_gnn_b3': _L1_gnn_in['b3']}

def reference(x, src, dst, edge_attr_256, edge_attr_256_n2, edge_type_2, L0_gnn_W_pre, L0_gnn_b_pre, L0_gnn_W1, L0_gnn_b1, L0_gnn_g1, L0_gnn_be1, L0_gnn_W2, L0_gnn_b2, L0_gnn_g2, L0_gnn_be2, L1_gnn_W_rel, L1_gnn_b_rel, L1_gnn_W_ih, L1_gnn_b_ih, L1_gnn_b_hh, L1_gnn_W1, L1_gnn_b1, L1_gnn_W2, L1_gnn_b2, L1_gnn_W3, L1_gnn_b3):
    import jax
    import jax.numpy as jnp

    def _L0_gnn_ref(x, edge_index, edge_attr, bases, W_pre, b_pre, W1, b1, g1, be1, W2, b2, g2, be2):
        import jax, jax.numpy as jnp
        import numpy as np
        N, E, H = (50000, 6250, 256)
        EPS = 1e-05

        def _bn(h, g, b):
            mean = h.mean(0)
            var = h.var(0)
            return (h - mean) * jax.lax.rsqrt(var + EPS) * g + b
        src_idx, dst_idx = (edge_index[0], edge_index[1])
        edge_feat = jax.nn.gelu((x[src_idx] + edge_attr) @ W_pre + b_pre, approximate=False) * bases
        aggr = jax.ops.segment_sum(edge_feat, dst_idx, num_segments=N)
        y = x + aggr
        h = jnp.maximum(_bn(y @ W1 + b1, g1, be1), 0.0)
        h = jnp.maximum(_bn(h @ W2 + b2, g2, be2), 0.0)
        return y + h

    def _L1_gnn_ref(feat, src, dst, rel, W_rel, b_rel, W_ih, b_ih, b_hh, W1, b1, W2, b2, W3, b3):
        import jax, jax.numpy as jnp
        import numpy as np
        N_NODES = 10000
        N_EDGES = 5000
        D = 256
        D_OUT = 256
        NUM_REL = 2
        n_nodes = feat.shape[0]
        S = feat[src]

        def edge_nn(x, W, b):
            h = jax.nn.relu(x @ W.T + b)
            return jax.nn.relu(h @ W.T + b)
        msgs = jnp.zeros_like(S)
        for r in range(W_rel.shape[0]):
            msgs = jnp.where((rel == r)[:, None], edge_nn(S, W_rel[r], b_rel[r]), msgs)
        agg = jax.ops.segment_sum(msgs, dst, num_segments=n_nodes)
        gates = agg @ W_ih.T + b_ih + b_hh
        i, f, g, o = jnp.split(gates, 4, axis=-1)
        c = jax.nn.sigmoid(i) * jnp.tanh(g)
        hn = jax.nn.sigmoid(o) * jnp.tanh(c)
        x = jax.nn.relu(hn @ W1.T + b1)
        x = jax.nn.relu(x @ W2.T + b2)
        return x @ W3.T + b3
    edge_index = jnp.stack([src, dst])
    x = _layernorm(x + _L0_gnn_ref(x, edge_index, edge_attr_256, edge_attr_256_n2, L0_gnn_W_pre, L0_gnn_b_pre, L0_gnn_W1, L0_gnn_b1, L0_gnn_g1, L0_gnn_be1, L0_gnn_W2, L0_gnn_b2, L0_gnn_g2, L0_gnn_be2), axis=-1)
    x = _layernorm(x + _L1_gnn_ref(x, src, dst, edge_type_2, L1_gnn_W_rel, L1_gnn_b_rel, L1_gnn_W_ih, L1_gnn_b_ih, L1_gnn_b_hh, L1_gnn_W1, L1_gnn_b1, L1_gnn_W2, L1_gnn_b2, L1_gnn_W3, L1_gnn_b3), axis=-1)
    return x

_drawn_inputs = setup_inputs


def setup_inputs(seed=0):
    import zlib

    import numpy as np

    out = dict(_drawn_inputs(seed))
    spreads = {'L0_gnn_b_pre': (0.0, 0.423),
     'L0_gnn_b1': (0.0, 0.8),
     'L0_gnn_g1': (1.0, 0.2),
     'L0_gnn_be1': (0.0, 0.317),
     'L0_gnn_b2': (0.0, 0.8),
     'L0_gnn_g2': (1.0, 0.2),
     'L0_gnn_be2': (0.0, 0.1)}
    factors = {'L1_gnn_W_rel': 3.206,
     'L1_gnn_b_rel': 8.0,
     'L1_gnn_W_ih': 2.732,
     'L1_gnn_b_ih': 8.0,
     'L1_gnn_b_hh': 8.0,
     'L1_gnn_W1': 2.715}
    for name, (base, spread) in spreads.items():
        noise = np.random.default_rng([zlib.crc32(name.encode()), seed]).standard_normal(out[name].shape)
        drawn = base * np.exp(spread * noise) if base else spread * noise
        out[name] = jnp.asarray(drawn.astype(out[name].dtype))
    for name, factor in factors.items():
        out[name] = (out[name] * factor).astype(out[name].dtype)
    return out
```

```python
from contextlib import ExitStack, contextmanager

import numpy as np

import concourse.bass as bass
from concourse import mybir

F32 = mybir.dt.float32
F32R = mybir.dt.float32r
I32 = mybir.dt.int32
ALU = mybir.AluOpType
ACT = mybir.ActivationFunctionType

P = 128
F = 256
C = F // P
J = 4
B = J * P
EPS = 1e-5
NO_NODE = -5.0

REL, IH, M1, M2, M3, NBLK = 0, 8, 20, 22, 23, 25
GATES = 3
GATE_ROWS = (0, 2, 3)


class Shapes:
    def __init__(self, nodes, edges):
        self.N, self.E = nodes, edges
        self.NB = -(-nodes // B)
        self.NP = self.NB // 2
        self.last_node = nodes - B
        self.dup = (self.NB * B - nodes) // J
        self.ET = -(-edges // P)
        self.EB = -(-self.ET // J)
        self.tail_tiles = self.ET - J * (self.EB - 1)
        self.tail_edges = edges - (self.EB - 1) * B
        self.tail_rows = edges - (self.ET - 1) * P
        self.TC = J * self.EB
        assert self.NB % 2 == 0 and self.NP % 2 == 1 and self.EB % 2 == 1 and self.EB >= 5
        assert self.ET == 2 * self.NP and (self.NB * B - nodes) % J == 0


def mm3(pe, out, lhs, rhs, first, last):
    pe.matmul(out, lhs[0], rhs[0], start=first, stop=False)
    pe.matmul(out, lhs[0], rhs[1], start=False, stop=False)
    return pe.matmul(out, lhs[1], rhs[0], start=False, stop=last)


@contextmanager
def stage_semaphores(nc):
    used = []
    yield used
    nc.clear_and_free_semaphores(used)
    nc.all_engine_barrier()


def wait(engine, semaphore, value):
    if not (isinstance(value, int) and value <= 0):
        engine.wait_ge(semaphore, value)


def halves(i):
    return ((2 * i, 0), (2 * i + 1, 1))


def setup(nc, A, K, S):
    with ExitStack() as c:
        used = c.enter_context(stage_semaphores(nc))

        def sb(name, shape, dt=F32):
            return c.enter_context(nc.sbuf_tensor(name, shape, dt))

        def sem(name):
            used.append(nc.alloc_semaphore(name))
            return used[-1]

        raw0 = sb("raw0", [P, 3, C, F])
        raw_rel = sb("raw_rel", [P, 2, C, F])
        raw_ih = sb("raw_ih", [P, GATES * C, F])
        raw_m1 = sb("raw_m1", [P, F])
        raw_m2 = sb("raw_m2", [P, P])
        raw_m3 = sb("raw_m3", [P, C, P])
        rows = sb("rows", [2, 2, F])
        b_ih = sb("b_ih", [P, GATES * C])
        b_hh = sb("b_hh", [P, GATES * C])
        dst_i = sb("dst_i", [P, S.TC], I32)
        nxt_i = sb("nxt_i", [P, S.TC], I32)
        slot = sb("slot", [P, S.TC], I32)
        slot_f = sb("slot_f", [P, S.TC])
        differs = sb("differs", [P, S.TC])
        pick = sb("pick", [P, S.TC])
        last_row = sb("last_row", [P, P])
        gate = sb("gate", [P, GATES, C])
        cell = sb("cell", [P, C])
        cell_t = sb("cell_t", [P, C])
        hid = sb("hid", [P, C])
        hid_h, hid_l = sb("hid_h", [P, C, P], F32R), sb("hid_l", [P, C, P], F32R)
        a1, a1h, a1l = sb("a1", [P, P]), sb("a1h", [P, P], F32R), sb("a1l", [P, P], F32R)
        a2, a2h, a2l = sb("a2", [P, P]), sb("a2h", [P, P], F32R), sb("a2l", [P, P], F32R)
        wt = c.enter_context(nc.psum_tensor("wt", [P, 28, P], F32))
        small = c.enter_context(nc.psum_tensor("small", [P, 512], F32))

        tables_clear, loaded, tables_loaded = sem("tables_clear"), sem("loaded"), sem("tables_loaded")
        zeroed, consts, step, transposed = sem("zeroed"), sem("consts"), sem("step"), sem("transposed")
        gates_on, mlp_done, relu_done, weights_split = (sem("gates_on"), sem("mlp_done"), sem("relu_done"),
                                                        sem("weights_split"))
        product = sem("product")
        block = c.enter_context(nc.Block())

        loads = []

        @block.sync
        def _(sp):
            sp.dma_start(A["y"][0:S.N, :], A["x"]).then_inc(K.copied, 16)
            sp.dma_start(A["y"][S.N:S.N + S.ET * P, :], A["x"][0:S.ET * P, :]).then_inc(K.copied, 16)

            def load(dst, src):
                loads.append(sp.dma_start(dst, src).then_inc(loaded, 16))

            for n, name in enumerate(("W_pre", "W1", "W2")):
                load(raw0[:, n], A[name].rearrange("(c p) o -> p c o", p=P))
            load(raw_rel[:], A["W_rel"].rearrange("r (o p) i -> p r o i", p=P))
            for n, g in enumerate(GATE_ROWS):
                load(raw_ih[:, n * C:(n + 1) * C], A["W_ih"][g * F:(g + 1) * F, :].rearrange("(o p) i -> p o i", p=P))
            load(raw_m1[:], A["M_W1"])
            load(raw_m2[:], A["M_W2"])
            load(raw_m3[:], A["M_W3"].rearrange("(o p) i -> p o i", p=P))
            load(rows[:, 0, :], A["b_pre"].rearrange("(a f) -> a f", a=1).to_broadcast([2, F]))
            load(rows[0:2, 1, :], A["b_rel"])
            load(K.b3[:], A["M_b3"].rearrange("(a f) -> a f", a=1).to_broadcast([P, F]))
            with nc.allow_non_contiguous_dma(reason="vectors and indices to columns"):
                for n, g in enumerate(GATE_ROWS):
                    for dst, src in ((b_ih, "b_ih"), (b_hh, "b_hh")):
                        load(dst[:, n * C:(n + 1) * C], A[src][g * F:(g + 1) * F].rearrange("(c p) -> p c", p=P))
                for n in range(2):
                    load(K.rel_b[:, n * C:(n + 1) * C], A["b_rel"][n, :].rearrange("(c p) -> p c", p=P))
                load(K.m_b[:, 0:1], A["M_b1"].rearrange("(c p) -> p c", p=P))
                load(K.m_b[:, 1:2], A["M_b2"].rearrange("(c p) -> p c", p=P))
                for n, name in enumerate(("b1", "g1", "be1", "b2", "g2", "be2")):
                    load(K.bn[:, n], A[name].rearrange("(c p) -> p c", p=P))
                full = (S.ET - 1) * P
                sp.wait_ge(tables_clear, 3)
                for table, src, ahead in ((K.src, "src", 0), (dst_i, "dst", 0), (nxt_i, "dst", 1)):
                    sp.dma_start(table[:, 0:S.ET - 1],
                                 A[src][ahead:full + ahead].rearrange("(t p) -> p t", p=P)).then_inc(tables_loaded, 16)
                    rest = S.tail_rows - ahead
                    sp.dma_start(table[0:rest, S.ET - 1:S.ET],
                                 A[src][full + ahead:S.E].rearrange("(p t) -> p t", t=1)).then_inc(tables_loaded, 16)
            sp.wait_ge(loaded, 16 * len(loads))
            sp.wait_ge(tables_loaded, 96)

        n_loads = len(loads)

        @block.gpsimd
        def _(pool):
            pool.memset(K.src[:], 0).then_inc(tables_clear, 1)
            pool.memset(dst_i[:], -1).then_inc(tables_clear, 1)
            pool.memset(nxt_i[:], -1).then_inc(tables_clear, 1)
            pool.iota(slot[:], pattern=[[P, S.TC]], base=S.N, channel_multiplier=1).then_inc(consts, 1)
            pool.iota(K.part_i[:], pattern=[[0, 1]], base=0, channel_multiplier=1).then_inc(consts, 1)
            pool.memset(K.minus_half[:], -0.5).then_inc(consts, 1)
            pool.memset(K.ident[:], 0.0).then_inc(zeroed, 1)
            pool.memset(last_row[:], 0.0).then_inc(zeroed, 1)
            pool.wait_ge(zeroed, 2)
            pool.affine_select(out=K.ident[:], in_=K.ident[:], compare_op=ALU.not_equal, fill=1.0, base=0,
                               pattern=[[-1, P]], channel_multiplier=1).then_inc(consts, 1)
            pool.affine_select(out=last_row[:], in_=last_row[:], compare_op=ALU.not_equal, fill=1.0, base=1 - P,
                               pattern=[[0, P]], channel_multiplier=1).then_inc(consts, 1)

        @block.tensor
        def _(pe):
            pe.wait_ge(consts, 5)
            pe.wait_ge(loaded, 16 * n_loads)
            for r in range(2):
                for ic in range(C):
                    for oc in range(C):
                        pe.transpose(wt[:, REL + (r * C + ic) * C + oc], raw_rel[:, r, oc, ic * P:(ic + 1) * P], K.ident[:])
            for ic in range(C):
                for oc in range(GATES * C):
                    pe.transpose(wt[:, IH + ic * GATES * C + oc], raw_ih[:, oc, ic * P:(ic + 1) * P], K.ident[:])
                pe.transpose(wt[:, M1 + ic], raw_m1[:, ic * P:(ic + 1) * P], K.ident[:])
            pe.transpose(wt[:, M2], raw_m2[:], K.ident[:])
            for oc in range(C):
                last = pe.transpose(wt[:, M3 + oc], raw_m3[:, oc], K.ident[:])
            last.then_inc(transposed, 1)
            pe.wait_ge(step, 1)
            pe.matmul(small[:, 0:S.TC - 1], last_row[:], K.dst_f[:, 0:S.TC - 1], start=True, stop=True).then_inc(product, 1)
            pe.wait_ge(step, 5)
            pe.wait_ge(weights_split, 2)
            pe.wait_ge(mlp_done, 1)
            for ic in range(C):
                last = mm3(pe, small[:, 0:P], (K.wl_h[:, M1 + ic], K.wl_l[:, M1 + ic]), (hid_h[:, ic], hid_l[:, ic]),
                           ic == 0, ic == C - 1)
            last.then_inc(product, 1)
            pe.wait_ge(mlp_done, 2)
            mm3(pe, small[:, 0:P], (K.wl_h[:, M2], K.wl_l[:, M2]), (a1h[:], a1l[:]), True, True).then_inc(product, 1)
            pe.wait_ge(mlp_done, 3)
            mm3(pe, small[:, 0:F], (a2h[:], a2l[:]), (w3(K.wl_h), w3(K.wl_l)), True, True).then_inc(product, 1)

        @block.scalar
        def _(act):
            act.wait_ge(step, 3)
            for n, func in ((0, ACT.Sigmoid), (1, ACT.Tanh), (2, ACT.Sigmoid)):
                act.activation(gate[:, n], K.gate_b[:, n * C:(n + 1) * C], func).then_inc(gates_on, 1)
            act.wait_ge(step, 4)
            act.activation(cell_t[:], cell[:], ACT.Tanh).then_inc(gates_on, 1)
            act.wait_ge(product, 2)
            act.activation(a1[:], small[:, 0:P], ACT.Relu, bias=K.m_b[:, 0:1]).then_inc(relu_done, 1)
            act.wait_ge(product, 3)
            act.activation(a2[:], small[:, 0:P], ACT.Relu, bias=K.m_b[:, 1:2]).then_inc(relu_done, 1)

        @block.vector
        def _(dve):
            t = 0
            link = sem("dve_link")

            def then(ins):
                nonlocal t
                t += 1
                ins.then_inc(link, 1)
                dve.wait_ge(link, t)

            dve.wait_ge(consts, 5)
            dve.wait_ge(tables_loaded, 96)
            dve.memset(K.ones[:].bitcast(F32), 1.0)
            dve.memset(K.prev_row[:, 0:1], NO_NODE)
            dve.memset(K.prev[:, 0:1], NO_NODE)
            dve.tensor_copy(K.part[:], K.part_i[:])
            dve.tensor_copy(slot_f[:], slot[:])
            dve.tensor_scalar(out=K.dst_gather[:], in0=dst_i[:], scalar1=0, scalar2=None, op0=ALU.max)
            dve.tensor_copy(K.dst_f[:], dst_i[:]).then_inc(step, 1)
            dve.wait_ge(step, 1)
            then(dve.tensor_tensor(out=differs[:], in0=dst_i[:], in1=nxt_i[:], op=ALU.not_equal))
            then(dve.tensor_tensor(out=pick[:], in0=K.dst_f[:], in1=slot_f[:], op=ALU.subtract))
            then(dve.tensor_tensor(out=pick[:], in0=pick[:], in1=differs[:], op=ALU.mult))
            then(dve.tensor_tensor(out=K.target[:], in0=pick[:], in1=slot_f[:], op=ALU.add))
            dve.wait_ge(product, 1)
            dve.tensor_copy(K.prev[:, 1:S.TC], small[:, 0:S.TC - 1]).then_inc(step, 1)
            then(dve.tensor_scalar(out=K.is_last[:], in0=K.part[:], scalar1=float(P - 1), scalar2=None, op0=ALU.is_equal))
            then(dve.tensor_scalar(out=pick[:, 0:S.TC - 1], in0=K.dst_f[:, 0:S.TC - 1], scalar1=NO_NODE,
                                   scalar2=K.is_last[:, 0:1], op0=ALU.subtract, op1=ALU.mult))
            then(dve.tensor_scalar(out=K.prev_row[:, 1:S.TC], in0=pick[:, 0:S.TC - 1], scalar1=NO_NODE, scalar2=None,
                                   op0=ALU.add))
            dve.wait_ge(loaded, 16 * n_loads)
            dve.tensor_tensor(out=K.gate_b[:], in0=b_ih[:], in1=b_hh[:], op=ALU.add).then_inc(step, 1)
            then(dve.tensor_copy(K.w0_h[:], raw0[:]))
            then(dve.tensor_tensor(out=K.w0_l[:], in0=raw0[:], in1=K.w0_h[:].bitcast(F32), op=ALU.subtract))
            then(dve.tensor_copy(K.rows_h[:], rows[:]))
            then(dve.tensor_tensor(out=K.rows_l[:], in0=rows[:], in1=K.rows_h[:].bitcast(F32), op=ALU.subtract))
            dve.wait_ge(transposed, 1)
            dve.tensor_copy(K.wl_h[:], wt[:, 0:NBLK]).then_inc(weights_split, 1)
            dve.wait_ge(weights_split, 1)
            dve.tensor_tensor(out=K.wl_l[:], in0=wt[:, 0:NBLK], in1=K.wl_h[:].bitcast(F32), op=ALU.subtract).then_inc(weights_split, 1)
            dve.wait_ge(gates_on, 3)
            dve.tensor_tensor(out=cell[:], in0=gate[:, 0], in1=gate[:, 1], op=ALU.mult).then_inc(step, 1)
            dve.wait_ge(gates_on, 4)
            dve.tensor_tensor(out=hid[:], in0=gate[:, 2], in1=cell_t[:], op=ALU.mult).then_inc(step, 1)
            dve.wait_ge(step, 5)
            wide = hid[:].rearrange("p (c o) -> p c o", o=1).to_broadcast([P, C, P])
            then(dve.tensor_copy(hid_h[:], wide))
            dve.tensor_tensor(out=hid_l[:], in0=wide, in1=hid_h[:].bitcast(F32), op=ALU.subtract).then_inc(mlp_done, 1)
            for n, (a, h, l) in enumerate(((a1, a1h, a1l), (a2, a2h, a2l))):
                dve.wait_ge(relu_done, n + 1)
                then(dve.tensor_copy(h[:], a[:]))
                dve.tensor_tensor(out=l[:], in0=a[:], in1=h[:].bitcast(F32), op=ALU.subtract).then_inc(mlp_done, 1)
            dve.wait_ge(product, 4)
            then(dve.tensor_tensor(out=K.base[:], in0=small[:, 0:F], in1=K.b3[:], op=ALU.add))


def w3(w):
    return w[:, M3:M3 + C].rearrange("p b o -> p (b o)")


def rel_w(w, r, ic):
    return w[:, REL + (r * C + ic) * C:REL + (r * C + ic + 1) * C].rearrange("p b o -> p (b o)")


def edges0(nc, A, K, S):
    with ExitStack() as c:
        used = c.enter_context(stage_semaphores(nc))

        def sb(name, shape, dt=F32):
            return c.enter_context(nc.sbuf_tensor(name, shape, dt))

        def sem(name):
            used.append(nc.alloc_semaphore(name))
            return used[-1]

        attr = sb("attr", [P, 2, J, F])
        bases = sb("bases", [P, 2, J, F])
        dst_row = sb("dst_row", [P, 2, B], I32)
        got = sb("got", [P, 2, J, F])
        idx = sb("idx0", [P, 2, J], I32)
        e_in = sb("e_in", [P, 2, J, F])
        e_h, e_l = sb("e_h", [P, 2, C, B], F32R), sb("e_l", [P, 2, C, B], F32R)
        gelu = sb("gelu", [P, 2, J, F])
        msg = sb("msg", [P, 2, J, F])
        same = sb("same", [P, 2, J, P])
        cont = sb("cont", [P, 2, J, P])
        sums = sb("sums", [P, 2, J, F])
        pT = [c.enter_context(nc.psum_tensor(f"pT{n}", [P, C, B], F32)) for n in range(2)]
        pU = c.enter_context(nc.psum_tensor("pU", [P, J, F], F32))
        pS = [c.enter_context(nc.psum_tensor(f"pS{n}", [P, 512], F32)) for n in range(2)]

        in_full = [sem("e0_in_full0"), sem("e0_in_full1")]
        got_full = [sem("e0_got_full0"), sem("e0_got_full1")]
        stored = [sem("e0_stored0"), sem("e0_stored1")]
        idx_ready, past, added, turned, hi_done, lo_done = (sem("e0_idx_ready"), sem("e0_past"), sem("e0_added"),
                                                            sem("e0_turned"), sem("e0_hi"), sem("e0_lo"))
        u_done, gelu_done, msg_done, masks, pairs, tile_sum, tile_out = (
            sem("e0_u"), sem("e0_gelu"), sem("e0_msg"), sem("e0_masks"), sem("e0_pairs"), sem("e0_tile_sum"),
            sem("e0_tile_out"))
        first_sum, tail_full = sem("e0_first_sum"), sem("e0_tail_full")
        block = c.enter_context(nc.Block())
        LAST = S.EB - 1

        def tiles(k):
            return S.tail_tiles if isinstance(k, int) and k == LAST else J

        @block.sync
        def _(sp):
            attr_v = A["attr"][0:LAST * B, :].rearrange("(b j p) f -> b p j f", j=J, p=P)
            bases_v = A["bases"][0:LAST * B, :].rearrange("(b j p) f -> b p j f", j=J, p=P)
            dst_v = A["dst"][0:LAST * B].rearrange("(b e) -> b e", e=B)

            def load(k, b):
                if isinstance(k, int) and k == LAST:
                    sp.wait_ge(msg_done, k - 1)
                    sp.wait_ge(masks, k - 1)
                    t = S.tail_tiles - 1
                    lo = LAST * B
                    for dst, src in ((attr, A["attr"]), (bases, A["bases"])):
                        sp.dma_start(dst[0:S.tail_rows, b, t], src[lo + t * P:S.E, :]).then_inc(tail_full, 16)
                    sp.wait_ge(tail_full, 32)
                    for dst, src in ((attr, A["attr"]), (bases, A["bases"])):
                        sp.dma_start(dst[:, b, 0:t], src[lo:lo + t * P, :].rearrange("(j p) f -> p j f", p=P)).then_inc(in_full[b], 16)
                    sp.dma_start(dst_row[:, b, 0:S.tail_edges],
                                 A["dst"][lo:S.E].rearrange("(a e) -> a e", a=1).to_broadcast([P, S.tail_edges])).then_inc(in_full[b], 16)
                else:
                    sp.dma_start(attr[:, b], attr_v[bass.ds(k, 1)].rearrange("o p j f -> (o p) j f")).then_inc(in_full[b], 16)
                    sp.dma_start(bases[:, b], bases_v[bass.ds(k, 1)].rearrange("o p j f -> (o p) j f")).then_inc(in_full[b], 16)
                    sp.dma_start(dst_row[:, b], dst_v[bass.ds(k, 1)].to_broadcast([P, B])).then_inc(in_full[b], 16)

            def store(k, b):
                n = tiles(k)
                sp.wait_ge(tile_out, J * k + n)
                sp.dma_start(A["sums"][bass.ds(k * B, n * P), :].rearrange("(j p) f -> p j f", p=P),
                             sums[:, b, 0:n]).then_inc(stored[b], 16)

            load(0, 0)
            load(1, 1)
            with sp.Fori(0, LAST // 2 - 1) as i:
                for k, b in halves(i):
                    row = sp.snap(k * B)
                    nxt = sp.snap(k + 2)
                    sp.wait_ge(tile_out, J * k + J)
                    sp.dma_start(A["sums"][bass.ds(row, B), :].rearrange("(j p) f -> p j f", p=P),
                                 sums[:, b]).then_inc(stored[b], 16)
                    sp.wait_ge(msg_done, k + 1)
                    sp.wait_ge(masks, k + 1)
                    load(nxt, b)
            k = LAST - 2
            store(k, 0)
            load(LAST, 0)
            store(k + 1, 1)
            store(LAST, 0)
            sp.wait_ge(stored[0], 16 * (LAST // 2 + 1))
            sp.wait_ge(stored[1], 16 * (LAST // 2))

        @block.gpsimd
        def _(pool):
            bound = pool.to_reg(S.N - 1)

            def gather(k, b, first=False):
                if not first:
                    pool.wait_ge(added, k - 1)
                    pool.sem_inc(past, 1)
                pool.tensor_copy(idx[:, b], K.src[:, bass.ds(k * J, J)]).then_inc(idx_ready, 1)
                pool.wait_ge(idx_ready, k + 1)
                pool.sem_inc(past, 1)
                for j in range(J):
                    pool.indirect_dma_start(
                        out=got[:, b, j], out_offset=None, in_=A["x"],
                        in_offset=bass.IndirectOffsetOnAxis(ap=idx[:, b, j:j + 1], axis=0),
                        bounds_check=bound, oob_is_err=False).then_inc(got_full[b], 16)

            gather(0, 0, True)
            gather(1, 1, True)
            with pool.Fori(1, LAST // 2) as i:
                for k, b in halves(i):
                    gather(k, b)
            gather(LAST, 0)

        @block.tensor
        def _(pe):
            def turn(k, b):
                pe.wait_ge(added, k + 1)
                pe.wait_ge(lo_done, k)
                for cc in range(C):
                    for j in range(J):
                        last = pe.transpose(pT[b][:, cc, j * P:(j + 1) * P], e_in[:, b, j, cc * P:(cc + 1) * P], K.ident[:])
                last.then_inc(turned, 1)

            def dense(k, b):
                pe.wait_ge(lo_done, k + 1)
                wait(pe, gelu_done, k)
                for j in range(J):
                    pe.matmul(pU[:, j], K.ones[0:1, :], K.rows_h[0:1, 0, :], start=True, stop=False)
                    pe.matmul(pU[:, j], K.ones[0:1, :], K.rows_l[0:1, 0, :], start=False, stop=False)
                    for cc in range(C):
                        cols = slice(j * P, (j + 1) * P)
                        last = mm3(pe, pU[:, j], (e_h[:, b, cc, cols], e_l[:, b, cc, cols]),
                                   (K.w0_h[:, 0, cc], K.w0_l[:, 0, cc]), False, cc == C - 1)
                last.then_inc(u_done, 1)

            def segments(k, b, first=False):
                for j in range(tiles(k)):
                    t = J * k + j
                    s = j % 2
                    before = (b, j - 1) if j else (1 - b, J - 1)
                    if j == 0:
                        pe.wait_ge(msg_done, k + 1)
                        pe.wait_ge(masks, k + 1)
                    if not (first and j < 2):
                        pe.wait_ge(tile_out, t - 1)
                    pe.matmul(pS[s][:, 0:F], same[:, b, j], msg[:, b, j], start=True, stop=False)
                    if first and j == 0:
                        pe.wait_ge(first_sum, 1)
                    else:
                        pe.wait_ge(tile_out, t)
                    pe.matmul(pS[s][:, 0:F], cont[96:128, b, j], sums[96:128, before[0], before[1]],
                              start=False, stop=True).then_inc(tile_sum, 1)

            pe.wait_ge(added, 1)
            for cc in range(C):
                for j in range(J):
                    last = pe.transpose(pT[0][:, cc, j * P:(j + 1) * P], e_in[:, 0, j, cc * P:(cc + 1) * P], K.ident[:])
            last.then_inc(turned, 1)
            pe.wait_ge(first_sum, 1)
            dense(0, 0)
            for k, b in ((0, 0), (1, 1)):
                turn(k + 1, 1 - b)
                segments(k, b, k == 0)
                dense(k + 1, 1 - b)
            with pe.Fori(1, LAST // 2) as i:
                for k, b in halves(i):
                    turn(k + 1, 1 - b)
                    segments(k, b)
                    dense(k + 1, 1 - b)
            segments(LAST, 0)

        @block.scalar
        def _(act):
            def hi(k, b):
                act.wait_ge(turned, k + 1)
                act.wait_ge(u_done, k)
                act.activation(e_h[:, b], pT[b][:], ACT.Copy).then_inc(hi_done, 1)

            def gelus(k, b):
                act.wait_ge(u_done, k + 1)
                act.wait_ge(msg_done, k)
                act.activation(gelu[:, b], pU[:], ACT.Gelu).then_inc(gelu_done, 1)

            def out(k, b, first=False):
                for j in range(tiles(k)):
                    act.wait_ge(tile_sum, J * k + j + 1)
                    if j == 0 and not first:
                        act.wait_ge(stored[b], (k - b) * 8)
                    act.activation(sums[:, b, j], pS[j % 2][:, 0:F], ACT.Copy).then_inc(tile_out, 1)

            act.wait_ge(turned, 1)
            act.activation(e_h[:, 0], pT[0][:], ACT.Copy).then_inc(hi_done, 1)
            for k, b in ((0, 0), (1, 1)):
                if k:
                    gelus(k, b)
                else:
                    act.wait_ge(u_done, 1)
                    act.activation(gelu[:, 0], pU[:], ACT.Gelu).then_inc(gelu_done, 1)
                hi(k + 1, 1 - b)
                out(k, b, True)
            with act.Fori(1, LAST // 2) as i:
                for k, b in halves(i):
                    gelus(k, b)
                    hi(k + 1, 1 - b)
                    out(k, b)
            gelus(LAST, 0)
            out(LAST, 0)

        @block.vector
        def _(dve):
            def add(k, b):
                dve.wait_ge(in_full[b], in_sum(k, b))
                dve.wait_ge(got_full[b], 16 * J * ((k - b) // 2 + 1) if isinstance(k, int) else (k - b) * 32 + 64)
                dve.tensor_tensor(out=e_in[:, b], in0=got[:, b], in1=attr[:, b], op=ALU.add).then_inc(added, 1)

            def in_sum(k, b):
                if isinstance(k, int):
                    return 48 * ((k - b) // 2 + 1)
                return (k - b) * 24 + 48

            def message(k, b):
                dve.wait_ge(gelu_done, k + 1)
                dve.tensor_tensor(out=msg[:, b], in0=gelu[:, b], in1=bases[:, b], op=ALU.mult).then_inc(msg_done, 1)

            def lo(k, b):
                dve.wait_ge(hi_done, k + 1)
                dve.tensor_tensor(out=e_l[:, b], in0=pT[b][:], in1=e_h[:, b].bitcast(F32), op=ALU.subtract).then_inc(lo_done, 1)

            def mask(k, b, first=False):
                if not first:
                    dve.wait_ge(tile_out, J * k - J)
                rows = dst_row[:, b].rearrange("p (j e) -> p j e", j=J)
                for out, key in ((same, K.dst_f), (cont, K.prev_row)):
                    cols = key[:, bass.ds(k * J, J)].rearrange("p (j o) -> p j o", o=1).to_broadcast([P, J, P])
                    last = dve.tensor_tensor(out=out[:, b], in0=rows, in1=cols, op=ALU.is_equal)
                last.then_inc(masks, 1)

            dve.memset(sums[:, 1, J - 1], 0.0).then_inc(first_sum, 1)
            add(0, 0)
            lo(0, 0)
            mask(0, 0, True)
            for k, b in ((0, 0), (1, 1)):
                add(k + 1, 1 - b)
                message(k, b)
                mask(k + 1, 1 - b, k == 0)
                lo(k + 1, 1 - b)
            with dve.Fori(1, LAST // 2) as i:
                for k, b in halves(i):
                    add(k + 1, 1 - b)
                    message(k, b)
                    mask(k + 1, 1 - b)
                    lo(k + 1, 1 - b)
            message(LAST, 0)



def scatter0(nc, A, K, S):
    with ExitStack() as c:
        used = c.enter_context(stage_semaphores(nc))

        def sem(name):
            used.append(nc.alloc_semaphore(name))
            return used[-1]

        rows = c.enter_context(nc.sbuf_tensor("sc_rows", [P, 2, 2, F], F32))
        idx = c.enter_context(nc.sbuf_tensor("sc_idx", [P, 2, 2], I32))
        full, done = [sem("sc_full0"), sem("sc_full1")], [sem("sc_done0"), sem("sc_done1")]
        idx_ready, past = sem("sc_idx_ready"), sem("sc_past")
        block = c.enter_context(nc.Block())
        steps = S.ET // 2

        @block.sync
        def _(sp):
            view = A["sums"][0:S.ET * P, :].rearrange("(s j p) f -> s p j f", j=2, p=P)

            def load(s, b):
                sp.dma_start(rows[:, b], view[bass.ds(s, 1)].rearrange("o p j f -> (o p) j f")).then_inc(full[b], 16)

            load(0, 0)
            load(1, 1)
            with sp.Fori(0, (steps - 3) // 2) as i:
                for s, b in halves(i):
                    ahead = sp.snap(s + 2)
                    sp.wait_ge(done[b], 16 * (s - b) + 32)
                    load(ahead, b)
            s = steps - 3
            sp.wait_ge(done[0], 16 * s + 32)
            load(steps - 1, 0)
            sp.wait_ge(done[1], 16 * (s + 1 - 1) + 32)
            sp.wait_ge(done[0], 16 * (steps - 1) + 32)

        @block.gpsimd
        def _(pool):
            pool.wait_ge(K.copied, 32)

            def scatter(s, b, first=False):
                if not first:
                    pool.wait_ge(done[b], 16 * (s - b))
                    pool.sem_inc(past, 1)
                pool.tensor_copy(idx[:, b], K.target[:, bass.ds(s * 2, 2)]).then_inc(idx_ready, 1)
                pool.wait_ge(full[b], 8 * (s - b) + 16)
                pool.sem_inc(past, 1)
                pool.wait_ge(idx_ready, s + 1)
                pool.sem_inc(past, 1)
                for j in range(2):
                    pool.indirect_dma_start(
                        out=A["y"], out_offset=bass.IndirectOffsetOnAxis(ap=idx[:, b, j:j + 1], axis=0),
                        in_=rows[:, b, j], in_offset=None, compute_op=ALU.add).then_inc(done[b], 16)

            scatter(0, 0, True)
            scatter(1, 1, True)
            with pool.Fori(1, steps // 2) as i:
                for s, b in halves(i):
                    scatter(s, b)
            scatter(steps - 1, 0)


def node_rows(t, S):
    full = t[0:(S.NB - 1) * B, :].rearrange("(n p j) f -> n p (j f)", p=P, j=J)

    def at(k):
        if isinstance(k, int) and k == S.NB - 1:
            return t[S.last_node:S.N, :].rearrange("(p j) f -> p (j f)", j=J)
        return full[bass.ds(k, 1)].rearrange("o p f -> (o p) f")
    return at


def quarters(i):
    return tuple((4 * i + q, q) for q in range(4))


def stream(sp, S, steps):
    loops = (S.NB - 2) // 4 - 1
    with sp.Fori(0, loops) as i:
        for k, q in quarters(i):
            steps(k, q)
    for k in range(4 * loops, S.NB):
        steps(k, k % 4)


def bn_stats_of(dve, out, psum, tail, S):
    if tail:
        psum = psum.rearrange("p (j q) -> p j q", j=J)[:, :, S.dup:P]
    return dve.bn_stats(out, psum)


def bn_coefficients(nc, sem, sb, K, which, stats, name):
    mv, var, rstd, coef, tmp = (sb(f"{name}_mv", [P, C, 2]), sb(f"{name}_var", [P, C]), sb(f"{name}_rstd", [P, C]),
                                sb(f"{name}_coef", [P, 2, C]), sb(f"{name}_tmp", [P, 2, C]))
    step, var_ready, rstd_ready, ready = (sem(f"{name}_step"), sem(f"{name}_var_ready"), sem(f"{name}_rstd_ready"),
                                          sem(f"{name}_ready"))
    b, g, be = (K.bn[:, 3 * which + n] for n in range(3))

    def on_vector(dve):
        for cc in range(C):
            last = dve.bn_aggr(mv[:, cc], stats[:, cc].rearrange("p n s -> p (n s)"))
        last.then_inc(step, 1)
        dve.wait_ge(step, 1)
        dve.tensor_scalar(out=var[:], in0=mv[:, :, 1], scalar1=EPS, scalar2=None, op0=ALU.add).then_inc(var_ready, 1)
        dve.tensor_tensor(out=tmp[:, 0], in0=mv[:, :, 0], in1=b, op=ALU.add).then_inc(step, 1)
        dve.wait_ge(step, 2)
        dve.tensor_tensor(out=tmp[:, 1], in0=b, in1=tmp[:, 0], op=ALU.subtract)
        dve.wait_ge(rstd_ready, 1)
        dve.tensor_tensor(out=coef[:, 0], in0=g, in1=rstd[:], op=ALU.mult).then_inc(step, 1)
        dve.wait_ge(step, 3)
        dve.tensor_tensor(out=tmp[:, 0], in0=tmp[:, 1], in1=coef[:, 0], op=ALU.mult).then_inc(step, 1)
        dve.wait_ge(step, 4)
        dve.tensor_tensor(out=coef[:, 1], in0=tmp[:, 0], in1=be, op=ALU.add).then_inc(ready, 1)

    def on_pool(pool):
        pool.wait_ge(var_ready, 1)
        pool.tensor_tensor(out=rstd[:], in0=var[:], in1=K.minus_half[:, 0:C], op=ALU.pow).then_inc(rstd_ready, 1)

    return coef, ready, on_vector, on_pool


def dense1(nc, A, K, S):
    with ExitStack() as c:
        used = c.enter_context(stage_semaphores(nc))

        def sb(name, shape, dt=F32):
            return c.enter_context(nc.sbuf_tensor(name, shape, dt))

        def sem(name):
            used.append(nc.alloc_semaphore(name))
            return used[-1]

        y = sb("d1_y", [P, 4, J * F])
        y_h, y_l = sb("d1_y_h", [P, 2, C, B], F32R), sb("d1_y_l", [P, 2, C, B], F32R)
        h = sb("d1_h", [P, 4, C * B])
        pT = [c.enter_context(nc.psum_tensor(f"d1_pT{n}", [P, C, B], F32)) for n in range(2)]
        pH = [c.enter_context(nc.psum_tensor(f"d1_pH{n}", [P, C, B], F32)) for n in range(2)]
        full, stored = [sem(f"d1_full{n}") for n in range(4)], [sem(f"d1_stored{n}") for n in range(4)]
        turned, hi_done, lo_done, product, stats_done, h_done, past = (
            sem("d1_turned"), sem("d1_hi"), sem("d1_lo"), sem("d1_product"), sem("d1_stats"), sem("d1_h_done"),
            sem("d1_past"))
        block = c.enter_context(nc.Block())
        loops = (S.NB - 2) // 4

        @block.sync
        def _(sp):
            rows = node_rows(A["y"], S)
            for q in range(4):
                sp.dma_start(y[:, q], rows(q)).then_inc(full[q], 16)

            def step(k, q):
                at = k if isinstance(k, int) else sp.snap(k)
                ahead = k + 4 if isinstance(k, int) else sp.snap(k + 4)
                sp.wait_ge(h_done, k + 3)
                sp.dma_start(A["h1"][bass.ds(at, 1)].rearrange("o p f -> (o p) f"), h[:, q]).then_inc(stored[q], 16)
                if not (isinstance(k, int) and k + 4 >= S.NB):
                    sp.dma_start(y[:, q], rows(ahead)).then_inc(full[q], 16)

            stream(sp, S, step)
            for q in range(4):
                sp.wait_ge(stored[q], 16 * ((S.NB - 1 - q) // 4 + 1))

        @block.tensor
        def _(pe):
            pe.sem_inc(product, 1)

            def turn(k, q):
                b = q % 2
                pe.wait_ge(full[q], 4 * (k - q) + 16)
                wait(pe, lo_done, k)
                for cc in range(C):
                    for j in range(J):
                        at = j * F + cc * P
                        last = pe.transpose(pT[b][:, cc, j * P:(j + 1) * P], y[:, q, at:at + P], K.ident[:])
                last.then_inc(turned, 1)

            def multiply(k, q):
                b = q % 2
                pe.wait_ge(lo_done, k + 1)
                pe.wait_ge(h_done, k + 1)
                for oc in range(C):
                    for ic in range(C):
                        cols = slice(oc * P, (oc + 1) * P)
                        last = mm3(pe, pH[b][:, oc], (K.w0_h[:, 1, ic, cols], K.w0_l[:, 1, ic, cols]),
                                   (y_h[:, b, ic], y_l[:, b, ic]), ic == 0, ic == C - 1)
                last.then_inc(product, 1)

            turn(0, 0)
            with pe.Fori(0, loops) as i:
                for k, q in quarters(i):
                    turn(k + 1, q + 1 if q < 3 else 0)
                    multiply(k, q)
            k = S.NB - 2
            turn(k + 1, 1)
            multiply(k, 0)
            multiply(k + 1, 1)

        @block.scalar
        def _(act):
            act.sem_inc(h_done, 2)

            def hi(k, b):
                act.wait_ge(turned, k + 1)
                wait(act, product, k)
                act.activation(y_h[:, b], pT[b][:], ACT.Copy).then_inc(hi_done, 1)

            def out(k, q):
                act.wait_ge(stats_done, k + 1)
                wait(act, stored[q], 4 * (k - q))
                act.activation(h[:, q].rearrange("p (c n) -> p c n", c=C), pH[q % 2][:], ACT.Copy).then_inc(h_done, 1)

            hi(0, 0)
            for k, q in quarters(0):
                hi(k + 1, (q + 1) % 2)
                out(k, q)
            with act.Fori(1, loops) as i:
                for k, q in quarters(i):
                    hi(k + 1, (q + 1) % 2)
                    out(k, q)
            hi(S.NB - 1, 1)
            out(S.NB - 2, 0)
            out(S.NB - 1, 1)

        @block.vector
        def _(dve):
            def lo(k, b):
                dve.wait_ge(hi_done, k + 1)
                dve.tensor_tensor(out=y_l[:, b], in0=pT[b][:], in1=y_h[:, b].bitcast(F32), op=ALU.subtract).then_inc(lo_done, 1)

            def stats(k, b, tail=False):
                dve.wait_ge(product, k + 2)
                dve.sem_inc(past, 1)
                for cc in range(C):
                    out = K.stats[:, cc, bass.ds(k, 1)].rearrange("p o s -> p (o s)")
                    last = bn_stats_of(dve, out, pH[b][:, cc], tail, S)
                last.then_inc(stats_done, 1)

            lo(0, 0)
            with dve.Fori(0, loops) as i:
                for k, q in quarters(i):
                    lo(k + 1, (q + 1) % 2)
                    stats(k, q % 2)
            lo(S.NB - 1, 1)
            stats(S.NB - 2, 0)
            stats(S.NB - 1, 1, True)


def dense2(nc, A, K, S):
    with ExitStack() as c:
        used = c.enter_context(stage_semaphores(nc))

        def sb(name, shape, dt=F32):
            return c.enter_context(nc.sbuf_tensor(name, shape, dt))

        def sem(name):
            used.append(nc.alloc_semaphore(name))
            return used[-1]

        h1 = sb("d2_h1", [P, 4, C * B])
        r = sb("d2_r", [P, 2, C, B])
        r_h, r_l = sb("d2_r_h", [P, 2, C, B], F32R), sb("d2_r_l", [P, 2, C, B], F32R)
        h = sb("d2_h", [P, 4, C * B])
        sums = sb("d2_sums", [P, 4, F])
        half = sb("d2_half", [P, 4, F])
        idx = sb("d2_idx", [P, 4], I32)
        pH = [c.enter_context(nc.psum_tensor(f"d2_pH{n}", [P, C, B], F32)) for n in range(2)]
        full, stored = [sem(f"d2_full{n}") for n in range(4)], [sem(f"d2_stored{n}") for n in range(4)]
        sum_full, added = [sem(f"d2_sum_full{n}") for n in range(4)], [sem(f"d2_added{n}") for n in range(4)]
        relu_done, hi_done, lo_done, product, stats_done, h_done, dve_past, pool_past, halved = (
            sem("d2_relu"), sem("d2_hi"), sem("d2_lo"), sem("d2_product"), sem("d2_stats"), sem("d2_h_done"),
            sem("d2_dve_past"), sem("d2_pool_past"), sem("d2_halved"))
        coef, coef_ready, coef_vector, coef_pool = bn_coefficients(nc, sem, sb, K, 0, K.stats, "bn1")
        block = c.enter_context(nc.Block())
        loops = (S.NB - 2) // 4

        @block.sync
        def _(sp):
            def load(k, q):
                sp.dma_start(h1[:, q], A["h1"][bass.ds(k, 1)].rearrange("o p f -> (o p) f")).then_inc(full[q], 16)
                sp.dma_start(sums[:, q], A["sums"][0:S.ET * P, :].rearrange("(t p) f -> t p f", p=P)[bass.ds(k, 1)]
                             .rearrange("o p f -> (o p) f")).then_inc(sum_full[q], 16)

            for q in range(4):
                load(q, q)

            def step(k, q):
                at = k if isinstance(k, int) else sp.snap(k)
                ahead = k + 4 if isinstance(k, int) else sp.snap(k + 4)
                sp.wait_ge(h_done, k + 3)
                sp.dma_start(A["h2"][bass.ds(at, 1)].rearrange("o p f -> (o p) f"), h[:, q]).then_inc(stored[q], 16)
                if not (isinstance(k, int) and k + 4 >= S.NB):
                    sp.wait_ge(halved, k + 1)
                    load(ahead, q)

            stream(sp, S, step)
            for q in range(4):
                sp.wait_ge(stored[q], 16 * ((S.NB - 1 - q) // 4 + 1))

        @block.tensor
        def _(pe):
            pe.sem_inc(product, 1)

            def multiply(k, b):
                pe.wait_ge(lo_done, k + 1)
                pe.wait_ge(h_done, k + 1)
                for oc in range(C):
                    for ic in range(C):
                        cols = slice(oc * P, (oc + 1) * P)
                        last = mm3(pe, pH[b][:, oc], (K.w0_h[:, 2, ic, cols], K.w0_l[:, 2, ic, cols]),
                                   (r_h[:, b, ic], r_l[:, b, ic]), ic == 0, ic == C - 1)
                last.then_inc(product, 1)

            with pe.Fori(0, S.NB // 2) as i:
                for k, b in halves(i):
                    multiply(k, b)

        @block.scalar
        def _(act):
            act.sem_inc(h_done, 2)
            act.wait_ge(coef_ready, 1)

            def relu(k, q):
                act.wait_ge(full[q], 4 * (k - q) + 16)
                wait(act, lo_done, k - 1)
                for cc in range(C):
                    last = act.activation(r[:, q % 2, cc], h1[:, q, cc * B:(cc + 1) * B], ACT.Relu,
                                          bias=coef[:, 1, cc:cc + 1], scale=coef[:, 0, cc:cc + 1])
                last.then_inc(relu_done, 1)

            def out(k, q):
                act.wait_ge(stats_done, k + 1)
                wait(act, stored[q], 4 * (k - q))
                act.activation(h[:, q].rearrange("p (c n) -> p c n", c=C), pH[q % 2][:], ACT.Copy).then_inc(h_done, 1)

            relu(0, 0)
            relu(1, 1)
            for k, q in quarters(0):
                relu(k + 2, (q + 2) % 4)
                out(k, q)
            with act.Fori(1, loops) as i:
                for k, q in quarters(i):
                    relu(k + 2, (q + 2) % 4)
                    out(k, q)
            out(S.NB - 2, 0)
            out(S.NB - 1, 1)

        @block.gpsimd
        def _(pool):
            coef_pool(pool)

            def hi(k, b):
                pool.wait_ge(relu_done, k + 1)
                pool.sem_inc(pool_past, 1)
                if not (isinstance(k, int) and k < 2):
                    pool.wait_ge(product, k)
                    pool.sem_inc(pool_past, 1)
                pool.tensor_copy(r_h[:, b], r[:, b]).then_inc(hi_done, 1)

            def subtract_half(k, q):
                if not (isinstance(k, int) and k < 4):
                    pool.wait_ge(added[q], 4 * (k - q))
                    pool.sem_inc(pool_past, 1)
                pool.wait_ge(sum_full[q], 4 * (k - q) + 16)
                pool.sem_inc(pool_past, 1)
                pool.tensor_copy(idx[:, q:q + 1], K.target[:, bass.ds(k, 1)])
                pool.tensor_scalar(out=half[:, q], in0=sums[:, q], scalar1=-0.5, scalar2=None, op0=ALU.mult).then_inc(halved, 1)
                pool.wait_ge(halved, k + 1)
                pool.sem_inc(pool_past, 1)
                pool.indirect_dma_start(
                    out=A["y"], out_offset=bass.IndirectOffsetOnAxis(ap=idx[:, q:q + 1], axis=0),
                    in_=half[:, q], in_offset=None, compute_op=ALU.add).then_inc(added[q], 16)

            hi(0, 0)
            hi(1, 1)
            subtract_half(0, 0)
            subtract_half(1, 1)
            for k, q in quarters(0):
                hi(k + 2, q % 2)
                subtract_half(k + 2, (q + 2) % 4)
            with pool.Fori(1, loops) as i:
                for k, q in quarters(i):
                    hi(k + 2, q % 2)
                    subtract_half(k + 2, (q + 2) % 4)
            for q in range(4):
                pool.wait_ge(added[q], 16 * ((S.NB - 1 - q) // 4 + 1))

        @block.vector
        def _(dve):
            coef_vector(dve)

            def lo(k, b):
                dve.wait_ge(hi_done, k + 1)
                dve.tensor_tensor(out=r_l[:, b], in0=r[:, b], in1=r_h[:, b].bitcast(F32), op=ALU.subtract).then_inc(lo_done, 1)

            def stats(k, b, tail=False):
                dve.wait_ge(product, k + 2)
                dve.sem_inc(dve_past, 1)
                for cc in range(C):
                    out = K.stats2[:, cc, bass.ds(k, 1)].rearrange("p o s -> p (o s)")
                    last = bn_stats_of(dve, out, pH[b][:, cc], tail, S)
                last.then_inc(stats_done, 1)

            lo(0, 0)
            with dve.Fori(0, loops) as i:
                for k, q in quarters(i):
                    lo(k + 1, (q + 1) % 2)
                    stats(k, q % 2)
            lo(S.NB - 1, 1)
            stats(S.NB - 2, 0)
            stats(S.NB - 1, 1, True)


def row_stats(dve, stats, rows, done):
    for j in range(J):
        last = dve.bn_stats(stats[:, j], rows[:, j])
    last.then_inc(done, 1)


def row_moments(dve, mv, stats, past, done):
    dve.sem_inc(past, 1)
    for j in range(J):
        last = dve.bn_aggr(mv[:, j], stats[:, j])
    last.then_inc(done, 1)


def dense3(nc, A, K, S):
    with ExitStack() as c:
        used = c.enter_context(stage_semaphores(nc))

        def sb(name, shape, dt=F32):
            return c.enter_context(nc.sbuf_tensor(name, shape, dt))

        def sem(name):
            used.append(nc.alloc_semaphore(name))
            return used[-1]

        h2 = sb("d3_h2", [P, 4, C * B])
        y = sb("d3_y", [P, 4, J * F])
        r = sb("d3_r", [P, 2, C, B])
        s = sb("d3_s", [P, 2, J, F])
        x1 = sb("d3_x1", [P, 4, J, F])
        u = sb("d3_u", [P, 2, J, F])
        o = sb("d3_o", [P, 4, J, F])
        st1, st2 = sb("d3_st1", [P, 2, J, 6]), sb("d3_st2", [P, 2, J, 6])
        mv1, mv2 = sb("d3_mv1", [P, 2, J, 2]), sb("d3_mv2", [P, 2, J, 2])
        v1, v2 = sb("d3_v1", [P, 2, J]), sb("d3_v2", [P, 2, J])
        rs1, rs2 = sb("d3_rs1", [P, 2, J]), sb("d3_rs2", [P, 2, J])
        nm, nb = sb("d3_nm", [P, 2, J]), sb("d3_nb", [P, 2, J])
        pN = [c.enter_context(nc.psum_tensor(f"d3_pN{n}", [P, J, F], F32)) for n in range(2)]
        full, x1_out, o_out = ([sem(f"d3_full{n}") for n in range(4)], [sem(f"d3_x1_out{n}") for n in range(4)],
                               [sem(f"d3_o_out{n}") for n in range(4)])
        relu_done, turned, s_done, st1_done, mv1_done, v1_done, rs1_done, x1_done = (
            sem("d3_relu"), sem("d3_turned"), sem("d3_s_done"), sem("d3_st1_done"), sem("d3_mv1_done"),
            sem("d3_v1_done"), sem("d3_rs1_done"), sem("d3_x1_done"))
        dve_past = sem("d3_dve_past")
        u_done, st2_done, mv2_done, v2_done, rs2_done, nb_done, o_done, past = (
            sem("d3_u_done"), sem("d3_st2_done"), sem("d3_mv2_done"), sem("d3_v2_done"), sem("d3_rs2_done"),
            sem("d3_nb_done"), sem("d3_o_done"), sem("d3_past"))
        coef, coef_ready, coef_vector, coef_pool = bn_coefficients(nc, sem, sb, K, 1, K.stats2, "bn2")
        block = c.enter_context(nc.Block())
        loops = (S.NB - 2) // 4

        @block.sync
        def _(sp):
            rows = node_rows(A["y"], S)
            x1_rows, out_rows = node_rows(A["x1"], S), node_rows(A["out"], S)

            def load(k, q, at):
                sp.dma_start(h2[:, q], A["h2"][bass.ds(at, 1)].rearrange("o p f -> (o p) f")).then_inc(full[q], 16)
                sp.dma_start(y[:, q], rows(at)).then_inc(full[q], 16)

            for q in range(4):
                load(q, q, q)

            def step(k, q):
                tail = isinstance(k, int) and k == S.NB - 1
                fresh = slice(S.dup, P) if tail else slice(0, P)
                at = k if isinstance(k, int) else sp.snap(k)
                ahead = k + 4 if isinstance(k, int) else sp.snap(k + 4)
                sp.wait_ge(x1_done, k + 1)
                sp.dma_start(x1_rows(at)[fresh], x1[fresh, q].rearrange("p j f -> p (j f)")).then_inc(x1_out[q], 16)
                sp.wait_ge(o_done, k + 1)
                sp.dma_start(out_rows(at)[fresh], o[fresh, q].rearrange("p j f -> p (j f)")).then_inc(o_out[q], 16)
                if not (isinstance(k, int) and k + 4 >= S.NB):
                    load(ahead, q, ahead)

            stream(sp, S, step)
            for q in range(4):
                sp.wait_ge(x1_out[q], 16 * ((S.NB - 1 - q) // 4 + 1))
                sp.wait_ge(o_out[q], 16 * ((S.NB - 1 - q) // 4 + 1))

        @block.tensor
        def _(pe):
            def turn(k, b):
                pe.wait_ge(relu_done, k + 1)
                wait(pe, s_done, k - 1)
                for j in range(J):
                    for cc in range(C):
                        last = pe.transpose(pN[b][:, j, cc * P:(cc + 1) * P], r[:, b, cc, j * P:(j + 1) * P], K.ident[:])
                last.then_inc(turned, 1)

            turn(0, 0)
            turn(1, 1)
            with pe.Fori(0, (S.NB - 2) // 2) as i:
                for k, b in halves(i):
                    turn(k + 2, b)

        @block.scalar
        def _(act):
            act.wait_ge(coef_ready, 1)

            def relu(k, q):
                act.wait_ge(full[q], 8 * (k - q) + 32)
                wait(act, turned, k - 1)
                for cc in range(C):
                    last = act.activation(r[:, q % 2, cc], h2[:, q, cc * B:(cc + 1) * B], ACT.Relu,
                                          bias=coef[:, 1, cc:cc + 1], scale=coef[:, 0, cc:cc + 1])
                last.then_inc(relu_done, 1)

            def normed(k, q):
                b = q % 2
                act.wait_ge(nb_done, k + 1)
                wait(act, o_out[q], 4 * (k - q))
                for j in range(J):
                    last = act.activation(o[:, q, j], u[:, b, j], ACT.Identity, bias=nb[:, b, j:j + 1],
                                          scale=rs2[:, b, j:j + 1])
                last.then_inc(o_done, 1)

            relu(0, 0)
            relu(1, 1)
            for k, q in quarters(0):
                relu(k + 2, (q + 2) % 4)
                normed(k, q)
            with act.Fori(1, loops) as i:
                for k, q in quarters(i):
                    relu(k + 2, (q + 2) % 4)
                    normed(k, q)
            normed(S.NB - 2, 0)
            normed(S.NB - 1, 1)

        @block.gpsimd
        def _(pool):
            coef_pool(pool)

            def rstd(k, b, mv, mv_done, v, v_done, rs, rs_done):
                pool.wait_ge(mv_done, k + 1)
                pool.sem_inc(past, 1)
                pool.tensor_scalar(out=v[:, b], in0=mv[:, b, :, 1], scalar1=EPS, scalar2=None, op0=ALU.add).then_inc(v_done, 1)
                pool.wait_ge(v_done, k + 1)
                pool.tensor_tensor(out=rs[:, b], in0=v[:, b], in1=K.minus_half[:, 0:J], op=ALU.pow).then_inc(rs_done, 1)

            def first(k, q):
                rstd(k, q % 2, mv1, mv1_done, v1, v1_done, rs1, rs1_done)

            def second(k, q):
                b = q % 2
                pool.wait_ge(mv2_done, k + 1)
                pool.sem_inc(past, 1)
                pool.tensor_scalar(out=nm[:, b], in0=mv2[:, b, :, 0], scalar1=-1.0, scalar2=None, op0=ALU.mult)
                rstd(k, b, mv2, mv2_done, v2, v2_done, rs2, rs2_done)
                pool.wait_ge(rs2_done, k + 1)
                pool.tensor_tensor(out=nb[:, b], in0=nm[:, b], in1=rs2[:, b], op=ALU.mult).then_inc(nb_done, 1)

            def add_base(k, q):
                pool.wait_ge(x1_done, k + 1)
                wide = K.base[:].rearrange("p (o f) -> p o f", o=1).to_broadcast([P, J, F])
                pool.tensor_tensor(out=u[:, q % 2], in0=x1[:, q], in1=wide, op=ALU.add).then_inc(u_done, 1)

            def step(k, q, ahead=True):
                second(k, q)
                if ahead:
                    first(k + 1, (q + 1) % 4)
                    pool.wait_ge(o_done, k)
                    add_base(k + 1, (q + 1) % 4)

            first(0, 0)
            add_base(0, 0)
            second(0, 0)
            first(1, 1)
            add_base(1, 1)
            for k in (1, 2, 3):
                step(k, k)
            with pool.Fori(1, loops) as i:
                for k, q in quarters(i):
                    step(k, q)
            step(S.NB - 2, 0)
            step(S.NB - 1, 1, False)

        @block.vector
        def _(dve):
            coef_vector(dve)

            def add(k, q):
                b = q % 2
                dve.wait_ge(turned, k + 1)
                dve.scalar_tensor_tensor(out=s[:, b], in0=y[:, q].rearrange("p (j f) -> p j f", j=J), scalar=2.0,
                                         in1=pN[b][:], op0=ALU.mult, op1=ALU.add).then_inc(s_done, 1)
                dve.wait_ge(s_done, k + 1)
                row_stats(dve, st1[:, b], s[:, b], st1_done)

            def moments1(k, q):
                b = q % 2
                dve.wait_ge(st1_done, k + 1)
                row_moments(dve, mv1[:, b], st1[:, b], dve_past, mv1_done)

            def second(k, q):
                b = q % 2
                dve.wait_ge(u_done, k + 1)
                row_stats(dve, st2[:, b], u[:, b], st2_done)
                dve.wait_ge(st2_done, k + 1)
                row_moments(dve, mv2[:, b], st2[:, b], dve_past, mv2_done)

            def normed(k, q):
                b = q % 2
                dve.wait_ge(rs1_done, k + 1)
                wait(dve, x1_out[q], 4 * (k - q))
                for j in range(J):
                    last = dve.tensor_scalar(out=x1[:, q, j], in0=s[:, b, j], scalar1=mv1[:, b, j, 0:1],
                                             scalar2=rs1[:, b, j:j + 1], op0=ALU.subtract, op1=ALU.mult)
                last.then_inc(x1_done, 1)

            def step(k, q, ahead=True):
                if ahead:
                    add(k + 1, (q + 1) % 4)
                    moments1(k + 1, (q + 1) % 4)
                second(k, q)
                if ahead:
                    normed(k + 1, (q + 1) % 4)

            add(0, 0)
            moments1(0, 0)
            normed(0, 0)
            for k, q in quarters(0):
                step(k, q)
            with dve.Fori(1, loops) as i:
                for k, q in quarters(i):
                    step(k, q)
            step(S.NB - 2, 0)
            step(S.NB - 1, 1, False)


def edges1(nc, A, K, S):
    with ExitStack() as c:
        used = c.enter_context(stage_semaphores(nc))

        def sb(name, shape, dt=F32):
            return c.enter_context(nc.sbuf_tensor(name, shape, dt))

        def sem(name):
            used.append(nc.alloc_semaphore("e1_" + name))
            return used[-1]

        def part(name, shape):
            return sb(name + "_h", shape, F32R), sb(name + "_l", shape, F32R)

        xs, xd = sb("e1_xs", [P, 2, J, F]), sb("e1_xd", [P, 2, J, F])
        idx = sb("e1_idx", [P, 3, 2, J], I32)
        dst_row, rel_row = sb("e1_dst_row", [P, 2, B], I32), sb("e1_rel_row", [P, 2, B], I32)
        has_rel = sb("e1_has_rel", [P, 2, 2, B])
        has_k = sb("e1_has_k", [2, 2, B], F32R)
        same, cont = sb("e1_same", [P, 2, J, P]), sb("e1_cont", [P, 2, J, P])
        xt = part("e1_xt", [P, C, B])
        hid = [sb(f"e1_hid{r}", [P, C, B]) for r in range(2)]
        hidp = [part(f"e1_hidp{r}", [P, C, B]) for r in range(2)]
        msg = sb("e1_msg", [P, J, F])
        agg = sb("e1_agg", [P, C, B])
        aggp = part("e1_aggp", [P, C, B])
        gate = [sb(f"e1_gate{g}", [P, C, B]) for g in range(GATES)]
        cell, cell_t, hn = sb("e1_cell", [P, C, B]), sb("e1_cell_t", [P, C, B]), sb("e1_hn", [P, C, B])
        hnp = part("e1_hnp", [P, C, B])
        m1, m2 = sb("e1_m1", [P, B]), sb("e1_m2", [P, B])
        m1p, m2p = part("e1_m1p", [P, B]), part("e1_m2p", [P, B])
        u = sb("e1_u", [P, J, F])
        st, mv = sb("e1_st", [P, J, 6]), sb("e1_mv", [P, J, 2])
        v, rs = sb("e1_v", [P, J]), sb("e1_rs", [P, J])
        o = sb("e1_o", [P, 2, J, F])
        pX = c.enter_context(nc.psum_tensor("pX", [P, C, B], F32))
        pR = c.enter_context(nc.psum_tensor("pR", [P, C, B], F32))
        pG = c.enter_context(nc.psum_tensor("pG", [P, C, B], F32))
        pM = c.enter_context(nc.psum_tensor("pM", [P, J, F], F32))

        rows_full, xs_full, xd_full, o_out = ([sem(f"{n}{b}") for b in range(2)] for n in
                                              ("rows_full", "xs_full", "xd_full", "o_out"))
        idx_src, idx_dst, idx_out, past, dve_past, agg_clear = (
            sem(n) for n in ("idx_src", "idx_dst", "idx_out", "past", "dve_past", "agg_clear"))
        masked, turned, xt_hi, xt_lo = (sem(n) for n in ("masked", "turned", "xt_hi", "xt_lo"))
        rel_done, relu_done, mult_done, hid_hi, hid_lo = (sem(n) for n in
                                                          ("rel_done", "relu_done", "mult_done", "hid_hi", "hid_lo"))
        m_done, msg_done, sum_done, carried, agg_hi, agg_lo = (
            sem(n) for n in ("m_done", "msg_done", "sum_done", "carried", "agg_hi", "agg_lo"))
        gate_done, gate_on, cell_done, cell_on, hn_done, hn_hi, hn_lo = (
            sem(n) for n in ("gate_done", "gate_on", "cell_done", "cell_on", "hn_done", "hn_hi", "hn_lo"))
        m1_done, m1_on, m1_hi, m1_lo, m2_done, m2_on, m2_hi, m2_lo = (
            sem(n) for n in ("m1_done", "m1_on", "m1_hi", "m1_lo", "m2_done", "m2_on", "m2_hi", "m2_lo"))
        y_done, biased, u_done, st_done, mv_done, v_done, rs_done, o_done = (
            sem(n) for n in ("y_done", "biased", "u_done", "st_done", "mv_done", "v_done", "rs_done", "o_done"))
        block = c.enter_context(nc.Block())
        EB = S.EB

        def real(k):
            return not isinstance(k, int) or 0 <= k < EB

        def steps(engine, step):
            for k in (-2, -1, 0):
                step(k, k % 2)
            with engine.Fori(0, (EB - 3) // 2) as i:
                step(2 * i + 1, 1)
                step(2 * i + 2, 0)
            for k in (EB - 2, EB - 1, EB):
                step(k, k % 2)

        @block.sync
        def _(sp):
            full = (EB - 1) * B

            def load(k, b):
                at = k if isinstance(k, int) else sp.snap(k)
                wait(sp, masked, k - 1)
                for t, src in ((dst_row, "dst"), (rel_row, "rel")):
                    sp.dma_start(t[:, b], A[src][0:full].rearrange("(b e) -> b e", e=B)[bass.ds(at, 1)]
                                 .to_broadcast([P, B])).then_inc(rows_full[b], 16)

            load(0, 0)
            load(1, 1)
            with sp.Fori(1, (EB - 1) // 2) as i:
                for k, b in halves(i):
                    load(k, b)
            sp.wait_ge(masked, EB - 2)
            for t, src in ((dst_row, "dst"), (rel_row, "rel")):
                sp.dma_start(t[:, 0, 0:S.tail_edges], A[src][full:S.E].rearrange("(a e) -> a e", a=1)
                             .to_broadcast([P, S.tail_edges])).then_inc(rows_full[0], 16)

        @block.gpsimd
        def _(pool):
            last_node = pool.to_reg(S.N - 1)

            def fetch(b, into, which, full):
                for j in range(J):
                    pool.indirect_dma_start(
                        out=into[:, b, j], out_offset=None, in_=A["x1"],
                        in_offset=bass.IndirectOffsetOnAxis(ap=idx[:, which, b, j:j + 1], axis=0),
                        bounds_check=last_node, oob_is_err=False).then_inc(full[b], 16)

            def mult(k, b, r):
                pool.wait_ge(relu_done, 2 * k + r + 1)
                wide = has_rel[:, b, r].rearrange("p (o n) -> p o n", o=1).to_broadcast([P, C, B])
                pool.tensor_tensor(out=hid[r][:], in0=hid[r][:], in1=wide, op=ALU.mult).then_inc(mult_done, 1)

            def step(k, b):
                if real(k + 1):
                    pool.wait_ge(masked, k + 2)
                    pool.sem_inc(past, 1)
                    mult(k + 1, 1 - b, 0)
                if real(k - 1):
                    pool.wait_ge(mv_done, k)
                    pool.sem_inc(past, 1)
                    pool.tensor_scalar(out=v[:], in0=mv[:, :, 1], scalar1=EPS, scalar2=None, op0=ALU.add).then_inc(v_done, 1)
                    pool.wait_ge(v_done, k)
                    pool.tensor_tensor(out=rs[:], in0=v[:], in1=K.minus_half[:, 0:J], op=ALU.pow).then_inc(rs_done, 1)
                if real(k + 2):
                    if not (isinstance(k, int) and k < 0):
                        pool.wait_ge(turned, k + 1)
                        pool.sem_inc(past, 1)
                    pool.tensor_copy(idx[:, 0, b], K.src[:, bass.ds((k + 2) * J, J)]).then_inc(idx_src, 1)
                    pool.wait_ge(idx_src, k + 3)
                    pool.sem_inc(past, 1)
                    fetch(b, xs, 0, xs_full)
                if real(k + 1):
                    mult(k + 1, 1 - b, 1)
                    if not (isinstance(k, int) and k < 1):
                        pool.wait_ge(u_done, k)
                        pool.sem_inc(past, 1)
                    pool.tensor_copy(idx[:, 1, 1 - b], K.dst_gather[:, bass.ds((k + 1) * J, J)]).then_inc(idx_dst, 1)
                    pool.wait_ge(idx_dst, k + 2)
                    pool.sem_inc(past, 1)
                    fetch(1 - b, xd, 1, xd_full)
                if real(k - 1):
                    if not (isinstance(k, int) and k < 3):
                        pool.wait_ge(o_out[1 - b], (k - 1 - (1 - b)) * 32)
                        pool.sem_inc(past, 1)
                    pool.tensor_copy(idx[:, 2, 1 - b], K.target[:, bass.ds((k - 1) * J, J)]).then_inc(idx_out, 1)
                    pool.wait_ge(idx_out, k)
                    pool.sem_inc(past, 1)
                    pool.wait_ge(o_done, k)
                    pool.sem_inc(past, 1)
                    for j in range(J):
                        pool.indirect_dma_start(
                            out=A["out"], out_offset=bass.IndirectOffsetOnAxis(ap=idx[:, 2, 1 - b, j:j + 1], axis=0),
                            in_=o[:, 1 - b, j], in_offset=None, bounds_check=last_node,
                            oob_is_err=False).then_inc(o_out[1 - b], 16)
                if real(k):
                    pool.wait_ge(xd_full[b], 32 * (k - b) + 64)
                    pool.sem_inc(past, 1)
                    wide = K.b3[:].rearrange("p (o f) -> p o f", o=1).to_broadcast([P, J, F])
                    pool.tensor_tensor(out=xd[:, b], in0=xd[:, b], in1=wide, op=ALU.add).then_inc(biased, 1)

            steps(pool, step)
            for b in range(2):
                pool.wait_ge(o_out[b], 64 * ((EB - 1 - b) // 2 + 1))

        @block.tensor
        def _(pe):
            def turn(k, b):
                pe.wait_ge(xs_full[b], 32 * (k - b) + 64)
                wait(pe, carried, (k - 1) * J)
                for cc in range(C):
                    for j in range(J):
                        last = pe.transpose(pX[:, cc, j * P:(j + 1) * P], xs[:, b, j, cc * P:(cc + 1) * P], K.ident[:])
                last.then_inc(turned, 1)

            def relation(k, r):
                pe.wait_ge(xt_lo, k + 1)
                wait(pe, relu_done, 2 * k + r)
                for oc in range(C):
                    for ic in range(C):
                        blk = REL + (r * C + ic) * C + oc
                        last = mm3(pe, pR[:, oc], (K.wl_h[:, blk], K.wl_l[:, blk]), (xt[0][:, ic], xt[1][:, ic]),
                                   ic == 0, ic == C - 1)
                last.then_inc(rel_done, 1)

            def second_layer(k, b):
                pe.wait_ge(hid_lo, 2 * k + 2)
                wait(pe, u_done, k - 1)
                for j in range(J):
                    cols = slice(j * P, (j + 1) * P)
                    pe.matmul(pM[:, j], has_k[:, b, cols], K.rows_h[:, 1], start=True, stop=False)
                    pe.matmul(pM[:, j], has_k[:, b, cols], K.rows_l[:, 1], start=False, stop=False)
                    for r in range(2):
                        for ic in range(C):
                            last = mm3(pe, pM[:, j], (hidp[r][0][:, ic, cols], hidp[r][1][:, ic, cols]),
                                       (rel_w(K.wl_h, r, ic), rel_w(K.wl_l, r, ic)), False, r == 1 and ic == C - 1)
                last.then_inc(m_done, 1)

            def segment_sums(k, b):
                pe.wait_ge(msg_done, k + 1)
                pe.wait_ge(xt_lo, min(k + 2, EB) if isinstance(k, int) else k + 2)
                for j in range(J):
                    for cc in range(C):
                        last = pe.matmul(pX[:, cc, j * P:(j + 1) * P], msg[:, j, cc * P:(cc + 1) * P], same[:, b, j],
                                         start=True, stop=True)
                last.then_inc(sum_done, 1)

            def gates(k, g):
                pe.wait_ge(agg_lo, k + 1)
                if g == 0:
                    wait(pe, m2_on, k)
                else:
                    pe.wait_ge(gate_on, GATES * k + g)
                for oc in range(C):
                    for ic in range(C):
                        blk = IH + ic * GATES * C + g * C + oc
                        last = mm3(pe, pG[:, oc], (K.wl_h[:, blk], K.wl_l[:, blk]), (aggp[0][:, ic], aggp[1][:, ic]),
                                   ic == 0, ic == C - 1)
                last.then_inc(gate_done, 1)

            def mlp1(k):
                pe.wait_ge(hn_lo, k + 1)
                pe.wait_ge(gate_on, GATES * k + GATES)
                for ic in range(C):
                    last = mm3(pe, pG[:, 0], (K.wl_h[:, M1 + ic], K.wl_l[:, M1 + ic]), (hnp[0][:, ic], hnp[1][:, ic]),
                               ic == 0, ic == C - 1)
                last.then_inc(m1_done, 1)

            def mlp2(k):
                pe.wait_ge(m1_lo, k + 1)
                mm3(pe, pG[:, 1], (K.wl_h[:, M2], K.wl_l[:, M2]), (m1p[0][:], m1p[1][:]), True, True).then_inc(m2_done, 1)

            def mlp3(k):
                pe.wait_ge(m2_lo, k + 1)
                pe.wait_ge(msg_done, min(k + 2, EB) if isinstance(k, int) else k + 2)
                for j in range(J):
                    cols = slice(j * P, (j + 1) * P)
                    last = mm3(pe, pM[:, j], (m2p[0][:, cols], m2p[1][:, cols]), (w3(K.wl_h), w3(K.wl_l)), True, True)
                last.then_inc(y_done, 1)

            def step(k, b):
                if real(k + 1):
                    relation(k + 1, 0)
                if real(k - 1):
                    mlp3(k - 1)
                if real(k):
                    gates(k, 0)
                if real(k + 1):
                    relation(k + 1, 1)
                if real(k):
                    gates(k, 1)
                if real(k + 2):
                    turn(k + 2, b)
                if real(k):
                    gates(k, 2)
                if real(k + 1):
                    second_layer(k + 1, 1 - b)
                if real(k):
                    mlp1(k)
                if real(k + 1):
                    segment_sums(k + 1, 1 - b)
                if real(k):
                    mlp2(k)

            steps(pe, step)

        @block.scalar
        def _(act):
            def relation(k, r):
                act.wait_ge(rel_done, 2 * k + r + 1)
                wait(act, m_done, k)
                for cc in range(C):
                    last = act.activation(hid[r][:, cc], pR[:, cc], ACT.Relu, bias=K.rel_b[:, r * C + cc:r * C + cc + 1])
                last.then_inc(relu_done, 1)

            def relation_hi(k, r):
                act.wait_ge(mult_done, 2 * k + r + 1)
                act.activation(hidp[r][0][:], hid[r][:], ACT.Copy).then_inc(hid_hi, 1)

            def gates(k, g, func):
                act.wait_ge(gate_done, GATES * k + g + 1)
                for cc in range(C):
                    last = act.activation(gate[g][:, cc], pG[:, cc], func, bias=K.gate_b[:, g * C + cc:g * C + cc + 1])
                last.then_inc(gate_on, 1)

            def step(k, b):
                if real(k + 1):
                    relation(k + 1, 0)
                    relation_hi(k + 1, 0)
                if real(k):
                    gates(k, 0, ACT.Sigmoid)
                if real(k + 1):
                    relation(k + 1, 1)
                if real(k):
                    gates(k, 1, ACT.Tanh)
                if real(k + 1):
                    relation_hi(k + 1, 1)
                if real(k):
                    act.wait_ge(cell_done, k + 1)
                    act.activation(cell_t[:], cell[:], ACT.Tanh).then_inc(cell_on, 1)
                if real(k + 2):
                    act.wait_ge(turned, k + 3)
                    wait(act, rel_done, 2 * k + 4)
                    act.activation(xt[0][:], pX[:], ACT.Copy).then_inc(xt_hi, 1)
                if real(k):
                    gates(k, 2, ACT.Sigmoid)
                    act.wait_ge(hn_done, k + 1)
                    act.activation(hnp[0][:], hn[:], ACT.Copy).then_inc(hn_hi, 1)
                if real(k + 1):
                    act.wait_ge(m_done, k + 2)
                    wait(act, sum_done, k + 1)
                    act.activation(msg[:], pM[:], ACT.Relu).then_inc(msg_done, 1)
                if real(k):
                    act.wait_ge(m1_done, k + 1)
                    act.activation(m1[:], pG[:, 0], ACT.Relu, bias=K.m_b[:, 0:1]).then_inc(m1_on, 1)
                    act.wait_ge(m1_on, k + 1)
                    act.activation(m1p[0][:], m1[:], ACT.Copy).then_inc(m1_hi, 1)
                    act.wait_ge(m2_done, k + 1)
                    wait(act, y_done, k)
                    act.activation(m2[:], pG[:, 1], ACT.Relu, bias=K.m_b[:, 1:2]).then_inc(m2_on, 1)
                    act.wait_ge(m2_on, k + 1)
                    act.activation(m2p[0][:], m2[:], ACT.Copy).then_inc(m2_hi, 1)
                if real(k + 1):
                    act.wait_ge(carried, J * k + 2 * J)
                    act.activation(aggp[0][:], agg[:], ACT.Copy).then_inc(agg_hi, 1)

            steps(act, step)

        @block.vector
        def _(dve):
            def low(parts, whole, hi_done, lo_done, count):
                dve.wait_ge(hi_done, count)
                dve.tensor_tensor(out=parts[1][:], in0=whole, in1=parts[0][:].bitcast(F32), op=ALU.subtract).then_inc(lo_done, 1)

            def masks(k, b):
                dve.wait_ge(rows_full[b], 16 * (k - b) + 32)
                wait(dve, mult_done, 2 * k - 2)
                wait(dve, sum_done, k - 1)
                rows = dst_row[:, b].rearrange("p (j e) -> p j e", j=J)
                for out, key in ((same, K.dst_f), (cont, K.prev)):
                    cols = key[:, bass.ds(k * J, J)].rearrange("p (j o) -> p j o", o=1).to_broadcast([P, J, P])
                    dve.tensor_tensor(out=out[:, b], in0=rows, in1=cols, op=ALU.is_equal)
                for r in range(2):
                    dve.tensor_scalar(out=has_rel[:, b, r], in0=rel_row[:, b], scalar1=float(r), scalar2=None, op0=ALU.is_equal)
                dve.tensor_scalar(out=has_k[:, b], in0=rel_row[0:2, b], scalar1=K.part[0:2, 0:1], scalar2=None,
                                  op0=ALU.is_equal).then_inc(masked, 1)

            def carry(k, b):
                dve.wait_ge(sum_done, k + 1)
                wait(dve, agg_lo, k)
                for j in range(J):
                    wait(dve, carried, J * k + j)
                    before = j * P - 1 if j else B - 1
                    for cc in range(C):
                        cols = slice(j * P, (j + 1) * P)
                        last = dve.scalar_tensor_tensor(out=agg[:, cc, cols], in0=cont[:, b, j],
                                                        scalar=agg[:, cc, before:before + 1], in1=pX[:, cc, cols],
                                                        op0=ALU.mult, op1=ALU.add)
                    last.then_inc(carried, 1)

            def step(k, b):
                if real(k - 1):
                    dve.wait_ge(y_done, k)
                    dve.wait_ge(biased, k)
                    wait(dve, o_done, k - 1)
                    dve.tensor_tensor(out=u[:], in0=pM[:], in1=xd[:, 1 - b], op=ALU.add).then_inc(u_done, 1)
                    dve.wait_ge(u_done, k)
                    row_stats(dve, st, u, st_done)
                if real(k + 1):
                    low(hidp[0], hid[0][:], hid_hi, hid_lo, 2 * k + 3)
                if real(k - 1):
                    dve.wait_ge(st_done, k)
                    row_moments(dve, mv, st, dve_past, mv_done)
                if real(k + 2):
                    masks(k + 2, b)
                if real(k - 1):
                    dve.wait_ge(rs_done, k)
                    if not (isinstance(k, int) and k < 3):
                        dve.wait_ge(o_out[1 - b], (k - 1 - (1 - b)) * 32)
                    for j in range(J):
                        last = dve.tensor_scalar(out=o[:, 1 - b, j], in0=u[:, j], scalar1=mv[:, j, 0:1],
                                                 scalar2=rs[:, j:j + 1], op0=ALU.subtract, op1=ALU.mult)
                    last.then_inc(o_done, 1)
                if real(k):
                    dve.wait_ge(gate_on, GATES * k + 2)
                    dve.tensor_tensor(out=cell[:], in0=gate[0][:], in1=gate[1][:], op=ALU.mult).then_inc(cell_done, 1)
                if real(k + 1):
                    low(hidp[1], hid[1][:], hid_hi, hid_lo, 2 * k + 4)
                if real(k + 2):
                    low(xt, pX[:], xt_hi, xt_lo, k + 3)
                if real(k):
                    dve.wait_ge(gate_on, GATES * k + GATES)
                    dve.wait_ge(cell_on, k + 1)
                    dve.tensor_tensor(out=hn[:], in0=gate[2][:], in1=cell_t[:], op=ALU.mult).then_inc(hn_done, 1)
                    low(hnp, hn[:], hn_hi, hn_lo, k + 1)
                    low(m1p, m1[:], m1_hi, m1_lo, k + 1)
                if real(k + 1):
                    carry(k + 1, 1 - b)
                if real(k):
                    low(m2p, m2[:], m2_hi, m2_lo, k + 1)
                if real(k + 1):
                    low(aggp, agg[:], agg_hi, agg_lo, k + 2)

            dve.memset(agg[:], 0.0).then_inc(agg_clear, 1)
            dve.wait_ge(agg_clear, 1)
            steps(dve, step)


class Persistent:

    def __init__(self, nc, c, S):
        def sb(name, shape, dt=F32):
            return c.enter_context(nc.sbuf_tensor("k_" + name, shape, dt))

        self.ident = sb("ident", [P, P])
        self.ones = sb("ones", [P, P], F32R)
        self.w0_h, self.w0_l = sb("w0_h", [P, 3, C, F], F32R), sb("w0_l", [P, 3, C, F], F32R)
        self.wl_h, self.wl_l = sb("wl_h", [P, NBLK, P], F32R), sb("wl_l", [P, NBLK, P], F32R)
        self.rows_h, self.rows_l = sb("rows_h", [2, 2, F], F32R), sb("rows_l", [2, 2, F], F32R)
        self.src, self.dst_gather = sb("src", [P, S.TC], I32), sb("dst_gather", [P, S.TC], I32)
        self.target = sb("target", [P, S.TC], I32)
        self.dst_f = sb("dst_f", [P, S.TC])
        self.prev, self.prev_row = sb("prev", [P, S.TC]), sb("prev_row", [P, S.TC])
        self.part_i, self.part, self.is_last = sb("part_i", [P, 1], I32), sb("part", [P, 1]), sb("is_last", [P, 1])
        self.minus_half = sb("minus_half", [P, J])
        self.rel_b, self.m_b, self.gate_b = sb("rel_b", [P, 2 * C]), sb("m_b", [P, 2]), sb("gate_b", [P, GATES * C])
        self.bn = sb("bn", [P, 6, C])
        self.b3, self.base = sb("b3", [P, F]), sb("base", [P, F])
        self.stats, self.stats2 = sb("stats", [P, C, S.NB, 6]), sb("stats2", [P, C, S.NB, 6])
        self.copied = c.enter_context(nc.semaphore("copied"))


def build(nc, A, nodes, edges):
    S = Shapes(nodes, edges)
    for name, shape in (("y", (S.N + S.ET * P, F)), ("x1", (S.N, F)), ("sums", (S.TC * P, F)),
                        ("h1", (S.NB, P, C * B)), ("h2", (S.NB, P, C * B))):
        A[name] = nc.dram_tensor(f"scratch_{name}", shape, F32, kind="Internal").ap()
    with ExitStack() as c:
        K = Persistent(nc, c, S)
        for stage in (setup, edges0, scatter0, dense1, dense2, dense3, edges1):
            stage(nc, A, K, S)


_INS = {"x": "x", "src": "src", "dst": "dst", "attr": "edge_attr_256", "bases": "edge_attr_256_n2",
        "rel": "edge_type_2", "W_pre": "L0_gnn_W_pre", "b_pre": "L0_gnn_b_pre", "W1": "L0_gnn_W1", "b1": "L0_gnn_b1",
        "g1": "L0_gnn_g1", "be1": "L0_gnn_be1", "W2": "L0_gnn_W2", "b2": "L0_gnn_b2", "g2": "L0_gnn_g2",
        "be2": "L0_gnn_be2", "W_rel": "L1_gnn_W_rel", "b_rel": "L1_gnn_b_rel", "W_ih": "L1_gnn_W_ih",
        "b_ih": "L1_gnn_b_ih", "b_hh": "L1_gnn_b_hh", "M_W1": "L1_gnn_W1", "M_b1": "L1_gnn_b1", "M_W2": "L1_gnn_W2",
        "M_b2": "L1_gnn_b2", "M_W3": "L1_gnn_W3", "M_b3": "L1_gnn_b3"}


def kernel(**inputs):
    import concourse.bacc as bacc
    from concourse.bass_utils import run_bass_kernel_spmd

    nc = bacc.Bacc("TRN2", target_bir_lowering=False, num_devices=1)
    arrays, A = {}, {}
    for short, name in _INS.items():
        a = np.ascontiguousarray(inputs[name])
        arrays[f"in_{name}"] = a
        A[short] = nc.dram_tensor(f"in_{name}", a.shape, mybir.dt.from_np(a.dtype), kind="ExternalInput").ap()
    nodes, edges = inputs["x"].shape[0], inputs["src"].shape[0]
    A["out"] = nc.dram_tensor("out_0", (nodes, F), F32, kind="ExternalOutput").ap()
    build(nc, A, nodes, edges)
    return run_bass_kernel_spmd(nc, [arrays], core_ids=[0]).results[0]["out_0"]
```

```python
from contextlib import ExitStack, contextmanager

import numpy as np

import concourse.bass as bass
from concourse import mybir

F32 = mybir.dt.float32
F32R = mybir.dt.float32r
I32 = mybir.dt.int32
ALU = mybir.AluOpType
ACT = mybir.ActivationFunctionType

P = 128
F = 256
C = F // P
J = 4
B = J * P
EPS = 1e-5
NO_NODE = -5.0

REL, IH, M1, M2, M3, NBLK = 0, 8, 20, 22, 23, 25
GATES = 3
GATE_ROWS = (0, 2, 3)


class Shapes:
    def __init__(self, nodes, edges):
        self.N, self.E = nodes, edges
        self.NB = -(-nodes // B)
        self.NP = self.NB // 2
        self.last_node = nodes - B
        self.dup = (self.NB * B - nodes) // J
        self.ET = -(-edges // P)
        self.EB = -(-self.ET // J)
        self.tail_tiles = self.ET - J * (self.EB - 1)
        self.tail_edges = edges - (self.EB - 1) * B
        self.tail_rows = edges - (self.ET - 1) * P
        self.TC = J * self.EB
        self.piece = nodes // (self.EB + 3)
        assert self.NB % 2 == 0 and self.NP % 2 == 1 and self.EB % 2 == 1 and self.EB >= 5
        assert self.ET == 2 * self.NP and (self.NB * B - nodes) % J == 0


def mm3(pe, out, lhs, rhs, first, last):
    pe.matmul(out, lhs[0], rhs[0], start=first, stop=False)
    pe.matmul(out, lhs[0], rhs[1], start=False, stop=False)
    return pe.matmul(out, lhs[1], rhs[0], start=False, stop=last)


@contextmanager
def stage_semaphores(nc):
    used = []
    yield used
    nc.clear_and_free_semaphores(used)
    nc.all_engine_barrier()


def wait(engine, semaphore, value):
    if not (isinstance(value, int) and value <= 0):
        engine.wait_ge(semaphore, value)


def halves(i):
    return ((2 * i, 0), (2 * i + 1, 1))


def quarters(i):
    return tuple((4 * i + q, q) for q in range(4))


def batch_steps(engine, n, step, ahead):
    loops = (n - ahead) // 4
    for k in range(-3, 4):
        step(k, k % 4)
    with engine.Fori(1, loops) as i:
        for k, q in quarters(i):
            step(k, q)
    for k in range(4 * loops, n + 1):
        step(k, k % 4)


def batch_of(n):
    return lambda k: not isinstance(k, int) or 0 <= k < n


def setup(nc, A, K, S):
    with ExitStack() as c:
        used = c.enter_context(stage_semaphores(nc))

        def sb(name, shape, dt=F32):
            return c.enter_context(nc.sbuf_tensor(name, shape, dt))

        def sem(name):
            used.append(nc.alloc_semaphore(name))
            return used[-1]

        raw0 = sb("raw0", [P, 3, C, F])
        raw_rel = sb("raw_rel", [P, 2, C, F])
        raw_ih = sb("raw_ih", [P, GATES * C, F])
        raw_m1 = sb("raw_m1", [P, F])
        raw_m2 = sb("raw_m2", [P, P])
        raw_m3 = sb("raw_m3", [P, C, P])
        rows = sb("rows", [2, 2, F])
        b_ih = sb("b_ih", [P, GATES * C])
        b_hh = sb("b_hh", [P, GATES * C])
        dst_i = sb("dst_i", [P, S.TC], I32)
        nxt_i = sb("nxt_i", [P, S.TC], I32)
        slot = sb("slot", [P, S.TC], I32)
        slot_f = sb("slot_f", [P, S.TC])
        differs = sb("differs", [P, S.TC])
        pick = sb("pick", [P, S.TC])
        last_row = sb("last_row", [P, P])
        gate = sb("gate", [P, GATES, C])
        cell = sb("cell", [P, C])
        cell_t = sb("cell_t", [P, C])
        hid = sb("hid", [P, C])
        hid_h, hid_l = sb("hid_h", [P, C, P], F32R), sb("hid_l", [P, C, P], F32R)
        a1, a1h, a1l = sb("a1", [P, P]), sb("a1h", [P, P], F32R), sb("a1l", [P, P], F32R)
        a2, a2h, a2l = sb("a2", [P, P]), sb("a2h", [P, P], F32R), sb("a2l", [P, P], F32R)
        wt = c.enter_context(nc.psum_tensor("wt", [P, 28, P], F32))
        small = c.enter_context(nc.psum_tensor("small", [P, 512], F32))

        tables_clear, loaded, tables_loaded = sem("tables_clear"), sem("loaded"), sem("tables_loaded")
        zeroed, consts, step, transposed = sem("zeroed"), sem("consts"), sem("step"), sem("transposed")
        gates_on, mlp_done, relu_done, weights_split = (sem("gates_on"), sem("mlp_done"), sem("relu_done"),
                                                        sem("weights_split"))
        product = sem("product")
        block = c.enter_context(nc.Block())

        loads = []

        @block.sync
        def _(sp):
            def load(dst, src):
                loads.append(sp.dma_start(dst, src).then_inc(loaded, 16))

            for n, name in enumerate(("W_pre", "W1", "W2")):
                load(raw0[:, n], A[name].rearrange("(c p) o -> p c o", p=P))
            load(raw_rel[:], A["W_rel"].rearrange("r (o p) i -> p r o i", p=P))
            for n, g in enumerate(GATE_ROWS):
                load(raw_ih[:, n * C:(n + 1) * C], A["W_ih"][g * F:(g + 1) * F, :].rearrange("(o p) i -> p o i", p=P))
            load(raw_m1[:], A["M_W1"])
            load(raw_m2[:], A["M_W2"])
            load(raw_m3[:], A["M_W3"].rearrange("(o p) i -> p o i", p=P))
            load(rows[:, 0, :], A["b_pre"].rearrange("(a f) -> a f", a=1).to_broadcast([2, F]))
            load(rows[0:2, 1, :], A["b_rel"])
            load(K.b3[:], A["M_b3"].rearrange("(a f) -> a f", a=1).to_broadcast([P, F]))
            with nc.allow_non_contiguous_dma(reason="vectors and indices to columns"):
                for n, g in enumerate(GATE_ROWS):
                    for dst, src in ((b_ih, "b_ih"), (b_hh, "b_hh")):
                        load(dst[:, n * C:(n + 1) * C], A[src][g * F:(g + 1) * F].rearrange("(c p) -> p c", p=P))
                for n in range(2):
                    load(K.rel_b[:, n * C:(n + 1) * C], A["b_rel"][n, :].rearrange("(c p) -> p c", p=P))
                load(K.m_b[:, 0:1], A["M_b1"].rearrange("(c p) -> p c", p=P))
                load(K.m_b[:, 1:2], A["M_b2"].rearrange("(c p) -> p c", p=P))
                for n, name in enumerate(("b1", "g1", "be1", "b2", "g2", "be2")):
                    load(K.bn[:, n], A[name].rearrange("(c p) -> p c", p=P))
                full = (S.ET - 1) * P
                sp.wait_ge(tables_clear, 3)
                for table, src, ahead in ((K.src, "src", 0), (dst_i, "dst", 0), (nxt_i, "dst", 1)):
                    sp.dma_start(table[:, 0:S.ET - 1],
                                 A[src][ahead:full + ahead].rearrange("(t p) -> p t", p=P)).then_inc(tables_loaded, 16)
                    rest = S.tail_rows - ahead
                    sp.dma_start(table[0:rest, S.ET - 1:S.ET],
                                 A[src][full + ahead:S.E].rearrange("(p t) -> p t", t=1)).then_inc(tables_loaded, 16)
            sp.dma_start(A["y"][S.EB * S.piece:S.N, :], A["x"][S.EB * S.piece:S.N, :]).then_inc(K.copied, 16)
            sp.wait_ge(loaded, 16 * len(loads))
            sp.wait_ge(tables_loaded, 96)

        n_loads = len(loads)

        @block.gpsimd
        def _(pool):
            pool.memset(K.src[:], 0).then_inc(tables_clear, 1)
            pool.memset(dst_i[:], -1).then_inc(tables_clear, 1)
            pool.memset(nxt_i[:], -1).then_inc(tables_clear, 1)
            pool.iota(slot[:], pattern=[[P, S.TC]], base=S.N, channel_multiplier=1).then_inc(consts, 1)
            pool.iota(K.part_i[:], pattern=[[0, 1]], base=0, channel_multiplier=1).then_inc(consts, 1)
            pool.memset(K.minus_half[:], -0.5).then_inc(consts, 1)
            pool.memset(K.ident[:], 0.0).then_inc(zeroed, 1)
            pool.memset(last_row[:], 0.0).then_inc(zeroed, 1)
            pool.wait_ge(zeroed, 2)
            pool.affine_select(out=K.ident[:], in_=K.ident[:], compare_op=ALU.not_equal, fill=1.0, base=0,
                               pattern=[[-1, P]], channel_multiplier=1).then_inc(consts, 1)
            pool.affine_select(out=last_row[:], in_=last_row[:], compare_op=ALU.not_equal, fill=1.0, base=1 - P,
                               pattern=[[0, P]], channel_multiplier=1).then_inc(consts, 1)

        @block.tensor
        def _(pe):
            pe.wait_ge(consts, 5)
            pe.wait_ge(loaded, 16 * n_loads)
            for r in range(2):
                for ic in range(C):
                    for oc in range(C):
                        pe.transpose(wt[:, REL + (r * C + ic) * C + oc], raw_rel[:, r, oc, ic * P:(ic + 1) * P], K.ident[:])
            for ic in range(C):
                for oc in range(GATES * C):
                    pe.transpose(wt[:, IH + ic * GATES * C + oc], raw_ih[:, oc, ic * P:(ic + 1) * P], K.ident[:])
                pe.transpose(wt[:, M1 + ic], raw_m1[:, ic * P:(ic + 1) * P], K.ident[:])
            pe.transpose(wt[:, M2], raw_m2[:], K.ident[:])
            for oc in range(C):
                last = pe.transpose(wt[:, M3 + oc], raw_m3[:, oc], K.ident[:])
            last.then_inc(transposed, 1)
            pe.wait_ge(step, 1)
            pe.matmul(small[:, 0:S.TC - 1], last_row[:], K.dst_f[:, 0:S.TC - 1], start=True, stop=True).then_inc(product, 1)
            pe.wait_ge(step, 5)
            pe.wait_ge(weights_split, 2)
            pe.wait_ge(mlp_done, 1)
            for ic in range(C):
                last = mm3(pe, small[:, 0:P], (K.wl_h[:, M1 + ic], K.wl_l[:, M1 + ic]), (hid_h[:, ic], hid_l[:, ic]),
                           ic == 0, ic == C - 1)
            last.then_inc(product, 1)
            pe.wait_ge(mlp_done, 2)
            mm3(pe, small[:, 0:P], (K.wl_h[:, M2], K.wl_l[:, M2]), (a1h[:], a1l[:]), True, True).then_inc(product, 1)
            pe.wait_ge(mlp_done, 3)
            mm3(pe, small[:, 0:F], (a2h[:], a2l[:]), (w3(K.wl_h), w3(K.wl_l)), True, True).then_inc(product, 1)

        @block.scalar
        def _(act):
            act.wait_ge(step, 3)
            for n, func in ((0, ACT.Sigmoid), (1, ACT.Tanh), (2, ACT.Sigmoid)):
                act.activation(gate[:, n], K.gate_b[:, n * C:(n + 1) * C], func).then_inc(gates_on, 1)
            act.wait_ge(step, 4)
            act.activation(cell_t[:], cell[:], ACT.Tanh).then_inc(gates_on, 1)
            act.wait_ge(product, 2)
            act.activation(a1[:], small[:, 0:P], ACT.Relu, bias=K.m_b[:, 0:1]).then_inc(relu_done, 1)
            act.wait_ge(product, 3)
            act.activation(a2[:], small[:, 0:P], ACT.Relu, bias=K.m_b[:, 1:2]).then_inc(relu_done, 1)

        @block.vector
        def _(dve):
            t = 0
            link = sem("dve_link")

            def then(ins):
                nonlocal t
                t += 1
                ins.then_inc(link, 1)
                dve.wait_ge(link, t)

            dve.wait_ge(consts, 5)
            dve.wait_ge(tables_loaded, 96)
            dve.memset(K.ones[:].bitcast(F32), 1.0)
            dve.memset(K.prev_row[:, 0:1], NO_NODE)
            dve.memset(K.prev[:, 0:1], NO_NODE)
            dve.tensor_copy(K.part[:], K.part_i[:])
            dve.tensor_copy(slot_f[:], slot[:])
            dve.tensor_scalar(out=K.dst_gather[:], in0=dst_i[:], scalar1=0, scalar2=None, op0=ALU.max)
            dve.tensor_copy(K.dst_f[:], dst_i[:]).then_inc(step, 1)
            dve.wait_ge(step, 1)
            then(dve.tensor_tensor(out=differs[:], in0=dst_i[:], in1=nxt_i[:], op=ALU.not_equal))
            then(dve.tensor_tensor(out=pick[:], in0=K.dst_f[:], in1=slot_f[:], op=ALU.subtract))
            then(dve.tensor_tensor(out=pick[:], in0=pick[:], in1=differs[:], op=ALU.mult))
            then(dve.tensor_tensor(out=K.target[:], in0=pick[:], in1=slot_f[:], op=ALU.add))
            dve.wait_ge(product, 1)
            dve.tensor_copy(K.prev[:, 1:S.TC], small[:, 0:S.TC - 1]).then_inc(step, 1)
            then(dve.tensor_scalar(out=K.is_last[:], in0=K.part[:], scalar1=float(P - 1), scalar2=None, op0=ALU.is_equal))
            then(dve.tensor_scalar(out=pick[:, 0:S.TC - 1], in0=K.dst_f[:, 0:S.TC - 1], scalar1=NO_NODE,
                                   scalar2=K.is_last[:, 0:1], op0=ALU.subtract, op1=ALU.mult))
            then(dve.tensor_scalar(out=K.prev_row[:, 1:S.TC], in0=pick[:, 0:S.TC - 1], scalar1=NO_NODE, scalar2=None,
                                   op0=ALU.add))
            dve.wait_ge(loaded, 16 * n_loads)
            dve.tensor_tensor(out=K.gate_b[:], in0=b_ih[:], in1=b_hh[:], op=ALU.add).then_inc(step, 1)
            then(dve.tensor_copy(K.w0_h[:], raw0[:]))
            then(dve.tensor_tensor(out=K.w0_l[:], in0=raw0[:], in1=K.w0_h[:].bitcast(F32), op=ALU.subtract))
            then(dve.tensor_copy(K.rows_h[:], rows[:]))
            then(dve.tensor_tensor(out=K.rows_l[:], in0=rows[:], in1=K.rows_h[:].bitcast(F32), op=ALU.subtract))
            dve.wait_ge(transposed, 1)
            dve.tensor_copy(K.wl_h[:], wt[:, 0:NBLK]).then_inc(weights_split, 1)
            dve.wait_ge(weights_split, 1)
            dve.tensor_tensor(out=K.wl_l[:], in0=wt[:, 0:NBLK], in1=K.wl_h[:].bitcast(F32), op=ALU.subtract).then_inc(weights_split, 1)
            dve.wait_ge(gates_on, 3)
            dve.tensor_tensor(out=cell[:], in0=gate[:, 0], in1=gate[:, 1], op=ALU.mult).then_inc(step, 1)
            dve.wait_ge(gates_on, 4)
            dve.tensor_tensor(out=hid[:], in0=gate[:, 2], in1=cell_t[:], op=ALU.mult).then_inc(step, 1)
            dve.wait_ge(step, 5)
            wide = hid[:].rearrange("p (c o) -> p c o", o=1).to_broadcast([P, C, P])
            then(dve.tensor_copy(hid_h[:], wide))
            dve.tensor_tensor(out=hid_l[:], in0=wide, in1=hid_h[:].bitcast(F32), op=ALU.subtract).then_inc(mlp_done, 1)
            for n, (a, h, l) in enumerate(((a1, a1h, a1l), (a2, a2h, a2l))):
                dve.wait_ge(relu_done, n + 1)
                then(dve.tensor_copy(h[:], a[:]))
                dve.tensor_tensor(out=l[:], in0=a[:], in1=h[:].bitcast(F32), op=ALU.subtract).then_inc(mlp_done, 1)
            dve.wait_ge(product, 4)
            then(dve.tensor_tensor(out=K.base[:], in0=small[:, 0:F], in1=K.b3[:], op=ALU.add))


def w3(w):
    return w[:, M3:M3 + C].rearrange("p b o -> p (b o)")


def rel_w(w, r, ic):
    return w[:, REL + (r * C + ic) * C:REL + (r * C + ic + 1) * C].rearrange("p b o -> p (b o)")


def edges0(nc, A, K, S):
    with ExitStack() as c:
        used = c.enter_context(stage_semaphores(nc))

        def sb(name, shape, dt=F32):
            return c.enter_context(nc.sbuf_tensor(name, shape, dt))

        def sem(name):
            used.append(nc.alloc_semaphore(name))
            return used[-1]

        attr = sb("attr", [P, 4, J, F])
        bases = sb("bases", [P, 4, J, F])
        dst_row = sb("dst_row", [P, 4, B], I32)
        edge = sb("edge", [P, 4, J, F])
        idx = sb("idx0", [P, 4, J], I32)
        e_h, e_l = sb("e_h", [P, 2, C, B], F32R), sb("e_l", [P, 2, C, B], F32R)
        gelu = sb("gelu", [P, 2, J, F])
        msg = sb("msg", [P, 2, J, F])
        same = sb("same", [P, 2, J, P])
        cont = sb("cont", [P, 2, J, P])
        sums = sb("sums", [P, 4, J, F])
        pT = [c.enter_context(nc.psum_tensor(f"pT{n}", [P, C, B], F32)) for n in range(2)]
        pU = c.enter_context(nc.psum_tensor("pU", [P, J, F], F32))
        pS = [c.enter_context(nc.psum_tensor(f"pS{n}", [P, 512], F32)) for n in range(2)]

        attr_full, bases_full, row_full, got_full, stored = (
            [sem(f"e0_{n}{q}") for q in range(4)] for n in ("attr_full", "bases_full", "row_full", "got_full", "stored"))
        idx_ready, past, added, turned, hi_done, lo_done = (sem("e0_idx_ready"), sem("e0_past"), sem("e0_added"),
                                                            sem("e0_turned"), sem("e0_hi"), sem("e0_lo"))
        u_done, gelu_done, msg_done, masks, tile_sum, tile_out = (
            sem("e0_u"), sem("e0_gelu"), sem("e0_msg"), sem("e0_masks"), sem("e0_tile_sum"), sem("e0_tile_out"))
        first_sum, tail_attr, tail_bases = sem("e0_first_sum"), sem("e0_tail_attr"), sem("e0_tail_bases")
        block = c.enter_context(nc.Block())
        LAST = S.EB - 1
        real = batch_of(S.EB)

        def is_last(k):
            return isinstance(k, int) and k == LAST

        def tiles(k):
            return S.tail_tiles if is_last(k) else J

        @block.sync
        def _(sp):
            dst_v = A["dst"][0:LAST * B].rearrange("(b e) -> b e", e=B)

            def load_rows(k, q, buffer, source, full, tail):
                if is_last(k):
                    t, lo = S.tail_tiles - 1, LAST * B
                    sp.dma_start(buffer[0:S.tail_rows, q, t], source[lo + t * P:S.E, :]).then_inc(tail, 16)
                    sp.dma_start(buffer[:, q, 0:t], source[lo:lo + t * P, :].rearrange("(j p) f -> p j f", p=P)).then_inc(full[q], 16)
                else:
                    rows = source[0:LAST * B, :].rearrange("(b j p) f -> b p j f", j=J, p=P)
                    sp.dma_start(buffer[:, q], rows[bass.ds(k, 1)].rearrange("o p j f -> (o p) j f")).then_inc(full[q], 16)

            def load_attr(k, q):
                load_rows(k, q, attr, A["attr"], attr_full, tail_attr)

            def load_bases(k, q):
                load_rows(k, q, bases, A["bases"], bases_full, tail_bases)

            def load_dst(k, q):
                if is_last(k):
                    nodes = A["dst"][LAST * B:S.E].rearrange("(a e) -> a e", a=1)
                    sp.dma_start(dst_row[:, q, 0:S.tail_edges], nodes.to_broadcast([P, S.tail_edges])).then_inc(row_full[q], 16)
                else:
                    sp.dma_start(dst_row[:, q], dst_v[bass.ds(k, 1)].to_broadcast([P, B])).then_inc(row_full[q], 16)

            def at(k):
                return k if isinstance(k, int) else sp.snap(k)

            for q in range(4):
                load_attr(q, q)
                load_bases(q, q)
                load_dst(q, q)

            def step(k, q):
                attr_next, next_k, row = at(k + 7), at(k + 4), at((k - 1) * B)
                if real(k + 7) and real(k + 3):
                    sp.wait_ge(added, k + 4)
                    load_attr(attr_next, (q + 3) % 4)
                if real(k + 4) and real(k):
                    sp.wait_ge(msg_done, k + 1)
                    load_bases(next_k, q)
                    sp.wait_ge(masks, k + 1)
                    load_dst(next_k, q)
                if real(k - 1):
                    n, b = tiles(k - 1), (q - 1) % 4
                    sp.wait_ge(tile_out, J * (k - 1) + n)
                    sp.dma_start(A["sums"][bass.ds(row, n * P), :].rearrange("(j p) f -> p j f", p=P),
                                 sums[:, b, 0:n]).then_inc(stored[b], 16)

            batch_steps(sp, S.EB, step, 8)
            for q in range(4):
                sp.wait_ge(stored[q], 16 * ((LAST - q) // 4 + 1))

        @block.gpsimd
        def _(pool):
            bound = pool.to_reg(S.N - 1)

            def step(k, q):
                if not real(k + 6):
                    return
                b = (q + 2) % 4
                if real(k + 2):
                    pool.wait_ge(turned, k + 3)
                    pool.sem_inc(past, 1)
                pool.tensor_copy(idx[:, b], K.src[:, bass.ds((k + 6) * J, J)]).then_inc(idx_ready, 1)
                pool.wait_ge(idx_ready, k + 7)
                pool.sem_inc(past, 1)
                for j in range(J):
                    pool.indirect_dma_start(
                        out=edge[:, b, j], out_offset=None, in_=A["x"],
                        in_offset=bass.IndirectOffsetOnAxis(ap=idx[:, b, j:j + 1], axis=0),
                        bounds_check=bound, oob_is_err=False).then_inc(got_full[b], 16)

            for k in (-6, -5, -4):
                step(k, k % 4)
            batch_steps(pool, S.EB, step, 7)

        @block.tensor
        def _(pe):
            def turn(k, b, q):
                pe.wait_ge(added, k + 1)
                wait(pe, lo_done, k - 1)
                for cc in range(C):
                    for j in range(J):
                        last = pe.transpose(pT[b][:, cc, j * P:(j + 1) * P], edge[:, q, j, cc * P:(cc + 1) * P], K.ident[:])
                last.then_inc(turned, 1)

            def dense(k, b, j):
                if j == 0:
                    pe.wait_ge(lo_done, k + 1)
                    wait(pe, gelu_done, k)
                pe.matmul(pU[:, j], K.ones[0:1, :], K.rows_h[0:1, 0, :], start=True, stop=False)
                pe.matmul(pU[:, j], K.ones[0:1, :], K.rows_l[0:1, 0, :], start=False, stop=False)
                for cc in range(C):
                    cols = slice(j * P, (j + 1) * P)
                    last = mm3(pe, pU[:, j], (e_h[:, b, cc, cols], e_l[:, b, cc, cols]),
                               (K.w0_h[:, 0, cc], K.w0_l[:, 0, cc]), False, cc == C - 1)
                if j == J - 1:
                    last.then_inc(u_done, 1)

            def segments(k, b, q, j):
                before = (q, j - 1) if j else ((q - 1) % 4, J - 1)
                first = isinstance(k, int) and k == 0
                if j == 0:
                    pe.wait_ge(msg_done, k + 1)
                    pe.wait_ge(masks, k + 1)
                if not (first and j < 2):
                    pe.wait_ge(tile_out, J * k + j - 1)
                pe.matmul(pS[j % 2][:, 0:F], same[:, b, j], msg[:, b, j], start=True, stop=False)
                if first and j == 0:
                    pe.wait_ge(first_sum, 1)
                else:
                    pe.wait_ge(tile_out, J * k + j)
                pe.matmul(pS[j % 2][:, 0:F], cont[96:128, b, j], sums[96:128, before[0], before[1]],
                          start=False, stop=True).then_inc(tile_sum, 1)

            def step(k, q):
                b = q % 2
                if real(k + 2):
                    turn(k + 2, b, (q + 2) % 4)
                for j in range(J):
                    if real(k - 1) and j < tiles(k - 1):
                        segments(k - 1, 1 - b, (q - 1) % 4, j)
                    if real(k + 1):
                        dense(k + 1, 1 - b, j)

            batch_steps(pe, S.EB, step, 3)

        @block.scalar
        def _(act):
            def hi(k, b):
                act.wait_ge(turned, k + 1)
                wait(act, u_done, k - 1)
                act.activation(e_h[:, b], pT[b][:], ACT.Copy).then_inc(hi_done, 1)

            def gelus(k, b):
                act.wait_ge(u_done, k + 1)
                wait(act, msg_done, k - 1)
                act.activation(gelu[:, b], pU[:], ACT.Gelu).then_inc(gelu_done, 1)

            def out(k, q, j):
                act.wait_ge(tile_sum, J * k + j + 1)
                if j == 0:
                    wait(act, stored[q], (k - q) * 4)
                act.activation(sums[:, q, j], pS[j % 2][:, 0:F], ACT.Copy).then_inc(tile_out, 1)

            def step(k, q):
                if real(k):
                    row = k * S.piece if isinstance(k, int) else act.snap(k * S.piece)
                    act.dma_start(A["y"][bass.ds(row, S.piece), :], A["x"][bass.ds(row, S.piece), :]).then_inc(K.copied, 16)
                    gelus(k, q % 2)
                if real(k + 2):
                    hi(k + 2, q % 2)
                if real(k - 1):
                    for j in range(tiles(k - 1)):
                        out(k - 1, (q - 1) % 4, j)

            batch_steps(act, S.EB, step, 3)

        @block.vector
        def _(dve):
            def add(k, q):
                dve.wait_ge(attr_full[q], 4 * (k - q) + 16)
                if is_last(k):
                    dve.wait_ge(tail_attr, 16)
                dve.wait_ge(got_full[q], 16 * (k - q) + 16 * J)
                dve.tensor_tensor(out=edge[:, q], in0=edge[:, q], in1=attr[:, q], op=ALU.add).then_inc(added, 1)

            def message(k, q):
                b = q % 2
                dve.wait_ge(bases_full[q], 4 * (k - q) + 16)
                if is_last(k):
                    dve.wait_ge(tail_bases, 16)
                dve.wait_ge(gelu_done, k + 1)
                wait(dve, tile_out, J * (k - 1))
                dve.tensor_tensor(out=msg[:, b], in0=gelu[:, b], in1=bases[:, q], op=ALU.mult).then_inc(msg_done, 1)

            def lo(k, b):
                dve.wait_ge(hi_done, k + 1)
                dve.tensor_tensor(out=e_l[:, b], in0=pT[b][:], in1=e_h[:, b].bitcast(F32), op=ALU.subtract).then_inc(lo_done, 1)

            def mask(k, q):
                dve.wait_ge(row_full[q], 4 * (k - q) + 16)
                rows = dst_row[:, q].rearrange("p (j e) -> p j e", j=J)
                for out, key in ((same, K.dst_f), (cont, K.prev_row)):
                    cols = key[:, bass.ds(k * J, J)].rearrange("p (j o) -> p j o", o=1).to_broadcast([P, J, P])
                    last = dve.tensor_tensor(out=out[:, q % 2], in0=rows, in1=cols, op=ALU.is_equal)
                last.then_inc(masks, 1)

            def step(k, q):
                if real(k + 3):
                    add(k + 3, (q + 3) % 4)
                if real(k):
                    message(k, q)
                if real(k + 2):
                    lo(k + 2, q % 2)
                if real(k):
                    mask(k, q)

            dve.memset(sums[:, 3, J - 1], 0.0).then_inc(first_sum, 1)
            batch_steps(dve, S.EB, step, 4)


def scatter0(nc, A, K, S):
    with ExitStack() as c:
        used = c.enter_context(stage_semaphores(nc))

        def sem(name):
            used.append(nc.alloc_semaphore(name))
            return used[-1]

        rows = c.enter_context(nc.sbuf_tensor("sc_rows", [P, 4, 2, F], F32))
        idx = c.enter_context(nc.sbuf_tensor("sc_idx", [P, 4, 2], I32))
        full, done = [sem(f"sc_full{q}") for q in range(4)], [sem(f"sc_done{q}") for q in range(4)]
        idx_ready, past = sem("sc_idx_ready"), sem("sc_past")
        block = c.enter_context(nc.Block())
        pairs = S.ET // 2
        real = batch_of(pairs)

        @block.sync
        def _(sp):
            view = A["sums"][0:S.ET * P, :].rearrange("(s j p) f -> s p j f", j=2, p=P)

            def load(s, q):
                sp.dma_start(rows[:, q], view[bass.ds(s, 1)].rearrange("o p j f -> (o p) j f")).then_inc(full[q], 16)

            for q in range(4):
                load(q, q)

            def step(s, q):
                ahead = s + 4 if isinstance(s, int) else sp.snap(s + 4)
                if real(s) and real(s + 4):
                    sp.wait_ge(done[q], 8 * (s - q) + 32)
                    load(ahead, q)

            batch_steps(sp, pairs, step, 4)
            for q in range(4):
                sp.wait_ge(done[q], 32 * ((pairs - 1 - q) // 4 + 1))

        @block.gpsimd
        def _(pool):
            bound = pool.to_reg(S.N - 1)
            pool.wait_ge(K.copied, 16 * (S.EB + 1))

            def step(s, q):
                if not real(s):
                    return
                if not (isinstance(s, int) and s < 4):
                    pool.wait_ge(done[q], 8 * (s - q))
                    pool.sem_inc(past, 1)
                pool.tensor_copy(idx[:, q], K.target[:, bass.ds(s * 2, 2)]).then_inc(idx_ready, 1)
                pool.wait_ge(full[q], 4 * (s - q) + 16)
                pool.sem_inc(past, 1)
                pool.wait_ge(idx_ready, s + 1)
                pool.sem_inc(past, 1)
                for j in range(2):
                    pool.indirect_dma_start(
                        out=A["y"], out_offset=bass.IndirectOffsetOnAxis(ap=idx[:, q, j:j + 1], axis=0),
                        in_=rows[:, q, j], in_offset=None, compute_op=ALU.add,
                        bounds_check=bound, oob_is_err=False).then_inc(done[q], 16)

            batch_steps(pool, pairs, step, 4)


def node_rows(t, S):
    full = t[0:(S.NB - 1) * B, :].rearrange("(n p j) f -> n p (j f)", p=P, j=J)

    def at(k):
        if isinstance(k, int) and k == S.NB - 1:
            return t[S.last_node:S.N, :].rearrange("(p j) f -> p (j f)", j=J)
        return full[bass.ds(k, 1)].rearrange("o p f -> (o p) f")
    return at


def bn_stats_of(dve, out, psum, tail, S):
    if tail:
        psum = psum.rearrange("p (j q) -> p j q", j=J)[:, :, S.dup:P]
    return dve.bn_stats(out, psum)


def bn_coefficients(nc, sem, sb, K, which, stats, name):
    mv, var, rstd, coef, tmp = (sb(f"{name}_mv", [P, C, 2]), sb(f"{name}_var", [P, C]), sb(f"{name}_rstd", [P, C]),
                                sb(f"{name}_coef", [P, 2, C]), sb(f"{name}_tmp", [P, 2, C]))
    step, var_ready, rstd_ready, ready = (sem(f"{name}_step"), sem(f"{name}_var_ready"), sem(f"{name}_rstd_ready"),
                                          sem(f"{name}_ready"))
    b, g, be = (K.bn[:, 3 * which + n] for n in range(3))

    def on_vector(dve):
        for cc in range(C):
            last = dve.bn_aggr(mv[:, cc], stats[:, cc].rearrange("p n s -> p (n s)"))
        last.then_inc(step, 1)
        dve.wait_ge(step, 1)
        dve.tensor_scalar(out=var[:], in0=mv[:, :, 1], scalar1=EPS, scalar2=None, op0=ALU.add).then_inc(var_ready, 1)
        dve.tensor_tensor(out=tmp[:, 0], in0=mv[:, :, 0], in1=b, op=ALU.add).then_inc(step, 1)
        dve.wait_ge(step, 2)
        dve.tensor_tensor(out=tmp[:, 1], in0=b, in1=tmp[:, 0], op=ALU.subtract)
        dve.wait_ge(rstd_ready, 1)
        dve.tensor_tensor(out=coef[:, 0], in0=g, in1=rstd[:], op=ALU.mult).then_inc(step, 1)
        dve.wait_ge(step, 3)
        dve.tensor_tensor(out=tmp[:, 0], in0=tmp[:, 1], in1=coef[:, 0], op=ALU.mult).then_inc(step, 1)
        dve.wait_ge(step, 4)
        dve.tensor_tensor(out=coef[:, 1], in0=tmp[:, 0], in1=be, op=ALU.add).then_inc(ready, 1)

    def on_pool(pool):
        pool.wait_ge(var_ready, 1)
        pool.tensor_tensor(out=rstd[:], in0=var[:], in1=K.minus_half[:, 0:C], op=ALU.pow).then_inc(rstd_ready, 1)

    return coef, ready, on_vector, on_pool


def dense1(nc, A, K, S):
    with ExitStack() as c:
        used = c.enter_context(stage_semaphores(nc))

        def sb(name, shape, dt=F32):
            return c.enter_context(nc.sbuf_tensor(name, shape, dt))

        def sem(name):
            used.append(nc.alloc_semaphore(name))
            return used[-1]

        y = sb("d1_y", [P, 4, J * F])
        y_h, y_l = sb("d1_y_h", [P, 2, C, B], F32R), sb("d1_y_l", [P, 2, C, B], F32R)
        h = sb("d1_h", [P, 4, C * B])
        pT = [c.enter_context(nc.psum_tensor(f"d1_pT{n}", [P, C, B], F32)) for n in range(2)]
        pH = [c.enter_context(nc.psum_tensor(f"d1_pH{n}", [P, C, B], F32)) for n in range(2)]
        full, stored = [sem(f"d1_full{n}") for n in range(4)], [sem(f"d1_stored{n}") for n in range(4)]
        turned, hi_done, lo_done, product, stats_done, h_done, past = (
            sem("d1_turned"), sem("d1_hi"), sem("d1_lo"), sem("d1_product"), sem("d1_stats"), sem("d1_h_done"),
            sem("d1_past"))
        block = c.enter_context(nc.Block())
        loops = (S.NB - 2) // 4
        real = batch_of(S.NB)

        @block.sync
        def _(sp):
            rows = node_rows(A["y"], S)
            for q in range(4):
                sp.dma_start(y[:, q], rows(q)).then_inc(full[q], 16)

            def step(k, q):
                y_next, h_now = (k + 5, k - 1) if isinstance(k, int) else (sp.snap(k + 5), sp.snap(k - 1))
                if real(k + 5) and real(k + 1):
                    sp.wait_ge(turned, k + 2)
                    sp.dma_start(y[:, (q + 1) % 4], rows(y_next)).then_inc(full[(q + 1) % 4], 16)
                if real(k - 1):
                    b = (q - 1) % 4
                    sp.wait_ge(h_done, k + 2)
                    sp.dma_start(A["h1"][bass.ds(h_now, 1)].rearrange("o p f -> (o p) f"), h[:, b]).then_inc(stored[b], 16)

            batch_steps(sp, S.NB, step, 6)
            for q in range(4):
                sp.wait_ge(stored[q], 16 * ((S.NB - 1 - q) // 4 + 1))

        @block.tensor
        def _(pe):
            pe.sem_inc(product, 1)

            def turn(k, q):
                b = q % 2
                pe.wait_ge(full[q], 4 * (k - q) + 16)
                wait(pe, lo_done, k - 1)
                for cc in range(C):
                    for j in range(J):
                        at = j * F + cc * P
                        last = pe.transpose(pT[b][:, cc, j * P:(j + 1) * P], y[:, q, at:at + P], K.ident[:])
                last.then_inc(turned, 1)

            def multiply(k, q):
                b = q % 2
                pe.wait_ge(lo_done, k + 1)
                pe.wait_ge(h_done, k + 1)
                for oc in range(C):
                    for ic in range(C):
                        cols = slice(oc * P, (oc + 1) * P)
                        last = mm3(pe, pH[b][:, oc], (K.w0_h[:, 1, ic, cols], K.w0_l[:, 1, ic, cols]),
                                   (y_h[:, b, ic], y_l[:, b, ic]), ic == 0, ic == C - 1)
                last.then_inc(product, 1)

            turn(0, 0)
            with pe.Fori(0, loops) as i:
                for k, q in quarters(i):
                    turn(k + 1, q + 1 if q < 3 else 0)
                    multiply(k, q)
            k = S.NB - 2
            turn(k + 1, 1)
            multiply(k, 0)
            multiply(k + 1, 1)

        @block.scalar
        def _(act):
            act.sem_inc(h_done, 2)

            def hi(k, b):
                act.wait_ge(turned, k + 1)
                wait(act, product, k)
                act.activation(y_h[:, b], pT[b][:], ACT.Copy).then_inc(hi_done, 1)

            def out(k, q):
                act.wait_ge(stats_done, k + 1)
                wait(act, stored[q], 4 * (k - q))
                act.activation(h[:, q].rearrange("p (c n) -> p c n", c=C), pH[q % 2][:], ACT.Copy).then_inc(h_done, 1)

            hi(0, 0)
            hi(1, 1)
            for k in (1, 2, 3):
                hi(k + 1, (k + 1) % 2)
                out(k - 1, k - 1)
            with act.Fori(1, loops) as i:
                for k, q in quarters(i):
                    hi(k + 1, (q + 1) % 2)
                    out(k - 1, (q - 1) % 4)
            hi(S.NB - 1, 1)
            out(S.NB - 3, 3)
            out(S.NB - 2, 0)
            out(S.NB - 1, 1)

        @block.vector
        def _(dve):
            def lo(k, b):
                dve.wait_ge(hi_done, k + 1)
                dve.tensor_tensor(out=y_l[:, b], in0=pT[b][:], in1=y_h[:, b].bitcast(F32), op=ALU.subtract).then_inc(lo_done, 1)

            def stats(k, b, tail=False):
                dve.wait_ge(product, k + 2)
                dve.sem_inc(past, 1)
                for cc in range(C):
                    out = K.stats[:, cc, bass.ds(k, 1)].rearrange("p o s -> p (o s)")
                    last = bn_stats_of(dve, out, pH[b][:, cc], tail, S)
                last.then_inc(stats_done, 1)

            lo(0, 0)
            lo(1, 1)
            for k in (1, 2, 3):
                stats(k - 1, (k - 1) % 2)
                lo(k + 1, (k + 1) % 2)
            with dve.Fori(1, loops) as i:
                for k, q in quarters(i):
                    stats(k - 1, (q - 1) % 2)
                    lo(k + 1, (q + 1) % 2)
            stats(S.NB - 3, 1)
            lo(S.NB - 1, 1)
            stats(S.NB - 2, 0)
            stats(S.NB - 1, 1, True)


def dense2(nc, A, K, S):
    with ExitStack() as c:
        used = c.enter_context(stage_semaphores(nc))

        def sb(name, shape, dt=F32):
            return c.enter_context(nc.sbuf_tensor(name, shape, dt))

        def sem(name):
            used.append(nc.alloc_semaphore(name))
            return used[-1]

        h1 = sb("d2_h1", [P, 4, C * B])
        r = sb("d2_r", [P, 2, C, B])
        r_h, r_l = sb("d2_r_h", [P, 2, C, B], F32R), sb("d2_r_l", [P, 2, C, B], F32R)
        h = sb("d2_h", [P, 4, C * B])
        sums = sb("d2_sums", [P, 4, F])
        half = sb("d2_half", [P, 4, F])
        idx = sb("d2_idx", [P, 4], I32)
        pH = [c.enter_context(nc.psum_tensor(f"d2_pH{n}", [P, C, B], F32)) for n in range(2)]
        full, stored = [sem(f"d2_full{n}") for n in range(4)], [sem(f"d2_stored{n}") for n in range(4)]
        sum_full, added = [sem(f"d2_sum_full{n}") for n in range(4)], [sem(f"d2_added{n}") for n in range(4)]
        relu_done, hi_done, lo_done, product, stats_done, h_done, dve_past, pool_past, halved = (
            sem("d2_relu"), sem("d2_hi"), sem("d2_lo"), sem("d2_product"), sem("d2_stats"), sem("d2_h_done"),
            sem("d2_dve_past"), sem("d2_pool_past"), sem("d2_halved"))
        coef, coef_ready, coef_vector, coef_pool = bn_coefficients(nc, sem, sb, K, 0, K.stats, "bn1")
        block = c.enter_context(nc.Block())
        loops = (S.NB - 2) // 4
        real = batch_of(S.NB)

        @block.sync
        def _(sp):
            sum_tiles = A["sums"][0:S.ET * P, :].rearrange("(t p) f -> t p f", p=P)

            def load_h1(k, q):
                sp.dma_start(h1[:, q], A["h1"][bass.ds(k, 1)].rearrange("o p f -> (o p) f")).then_inc(full[q], 16)

            def load_sums(k, q):
                sp.dma_start(sums[:, q], sum_tiles[bass.ds(k, 1)].rearrange("o p f -> (o p) f")).then_inc(sum_full[q], 16)

            for q in range(4):
                load_h1(q, q)
            for q in range(4):
                load_sums(q, q)

            def step(k, q):
                h1_next, sums_next, h_now = ((k + 6, k + 4, k - 1) if isinstance(k, int) else
                                             (sp.snap(k + 6), sp.snap(k + 4), sp.snap(k - 1)))
                if real(k + 6) and real(k + 2):
                    sp.wait_ge(relu_done, k + 3)
                    load_h1(h1_next, (q + 2) % 4)
                if real(k + 4) and real(k):
                    sp.wait_ge(halved, k + 1)
                    load_sums(sums_next, q)
                if real(k - 1):
                    b = (q - 1) % 4
                    sp.wait_ge(h_done, k + 2)
                    sp.dma_start(A["h2"][bass.ds(h_now, 1)].rearrange("o p f -> (o p) f"), h[:, b]).then_inc(stored[b], 16)

            batch_steps(sp, S.NB, step, 7)
            for q in range(4):
                sp.wait_ge(stored[q], 16 * ((S.NB - 1 - q) // 4 + 1))

        @block.tensor
        def _(pe):
            pe.sem_inc(product, 1)

            def multiply(k, b):
                pe.wait_ge(lo_done, k + 1)
                pe.wait_ge(h_done, k + 1)
                for oc in range(C):
                    for ic in range(C):
                        cols = slice(oc * P, (oc + 1) * P)
                        last = mm3(pe, pH[b][:, oc], (K.w0_h[:, 2, ic, cols], K.w0_l[:, 2, ic, cols]),
                                   (r_h[:, b, ic], r_l[:, b, ic]), ic == 0, ic == C - 1)
                last.then_inc(product, 1)

            with pe.Fori(0, S.NB // 2) as i:
                for k, b in halves(i):
                    multiply(k, b)

        @block.scalar
        def _(act):
            act.sem_inc(h_done, 2)
            act.wait_ge(coef_ready, 1)

            def relu(k, q):
                act.wait_ge(full[q], 4 * (k - q) + 16)
                wait(act, lo_done, k - 1)
                for cc in range(C):
                    last = act.activation(r[:, q % 2, cc], h1[:, q, cc * B:(cc + 1) * B], ACT.Relu,
                                          bias=coef[:, 1, cc:cc + 1], scale=coef[:, 0, cc:cc + 1])
                last.then_inc(relu_done, 1)

            def out(k, q):
                act.wait_ge(stats_done, k + 1)
                wait(act, stored[q], 4 * (k - q))
                act.activation(h[:, q].rearrange("p (c n) -> p c n", c=C), pH[q % 2][:], ACT.Copy).then_inc(h_done, 1)

            relu(0, 0)
            relu(1, 1)
            relu(2, 2)
            for k in (1, 2, 3):
                relu(k + 2, (k + 2) % 4)
                out(k - 1, k - 1)
            with act.Fori(1, loops) as i:
                for k, q in quarters(i):
                    relu(k + 2, (q + 2) % 4)
                    out(k - 1, (q - 1) % 4)
            out(S.NB - 3, 3)
            out(S.NB - 2, 0)
            out(S.NB - 1, 1)

        @block.gpsimd
        def _(pool):
            coef_pool(pool)
            bound = pool.to_reg(S.N - 1)

            def subtract_half(k, q):
                if not (isinstance(k, int) and k < 4):
                    pool.wait_ge(added[q], 4 * (k - q))
                    pool.sem_inc(pool_past, 1)
                pool.wait_ge(sum_full[q], 4 * (k - q) + 16)
                pool.sem_inc(pool_past, 1)
                pool.tensor_copy(idx[:, q:q + 1], K.target[:, bass.ds(k, 1)])
                pool.tensor_scalar(out=half[:, q], in0=sums[:, q], scalar1=-0.5, scalar2=None, op0=ALU.mult).then_inc(halved, 1)
                pool.wait_ge(halved, k + 1)
                pool.sem_inc(pool_past, 1)
                pool.indirect_dma_start(
                    out=A["y"], out_offset=bass.IndirectOffsetOnAxis(ap=idx[:, q:q + 1], axis=0),
                    in_=half[:, q], in_offset=None, compute_op=ALU.add,
                    bounds_check=bound, oob_is_err=False).then_inc(added[q], 16)

            for k, q in quarters(0):
                subtract_half(k, q)
            with pool.Fori(1, loops) as i:
                for k, q in quarters(i):
                    subtract_half(k, q)
            subtract_half(S.NB - 2, 0)
            subtract_half(S.NB - 1, 1)
            for q in range(4):
                pool.wait_ge(added[q], 16 * ((S.NB - 1 - q) // 4 + 1))

        @block.vector
        def _(dve):
            coef_vector(dve)

            def parts(k, b):
                dve.wait_ge(relu_done, k + 1)
                wait(dve, product, k)
                dve.sem_inc(dve_past, 1)
                dve.tensor_copy(r_h[:, b], r[:, b]).then_inc(hi_done, 1)
                dve.wait_ge(hi_done, k + 1)
                dve.tensor_tensor(out=r_l[:, b], in0=r[:, b], in1=r_h[:, b].bitcast(F32), op=ALU.subtract).then_inc(lo_done, 1)

            def stats(k, b, tail=False):
                dve.wait_ge(product, k + 2)
                dve.sem_inc(dve_past, 1)
                for cc in range(C):
                    out = K.stats2[:, cc, bass.ds(k, 1)].rearrange("p o s -> p (o s)")
                    last = bn_stats_of(dve, out, pH[b][:, cc], tail, S)
                last.then_inc(stats_done, 1)

            parts(0, 0)
            parts(1, 1)
            for k in (1, 2, 3):
                stats(k - 1, (k - 1) % 2)
                parts(k + 1, (k + 1) % 2)
            with dve.Fori(1, loops) as i:
                for k, q in quarters(i):
                    stats(k - 1, (q - 1) % 2)
                    parts(k + 1, (q + 1) % 2)
            stats(S.NB - 3, 1)
            parts(S.NB - 1, 1)
            stats(S.NB - 2, 0)
            stats(S.NB - 1, 1, True)


def row_stats(dve, stats, rows, done):
    for j in range(J):
        last = dve.bn_stats(stats[:, j], rows[:, j])
    last.then_inc(done, 1)


def row_moments(dve, mv, stats, past, done):
    dve.sem_inc(past, 1)
    for j in range(J):
        last = dve.bn_aggr(mv[:, j], stats[:, j])
    last.then_inc(done, 1)


def dense3(nc, A, K, S):
    with ExitStack() as c:
        used = c.enter_context(stage_semaphores(nc))

        def sb(name, shape, dt=F32):
            return c.enter_context(nc.sbuf_tensor(name, shape, dt))

        def sem(name):
            used.append(nc.alloc_semaphore(name))
            return used[-1]

        h2 = sb("d3_h2", [P, 4, C * B])
        y = sb("d3_y", [P, 4, J * F])
        r = sb("d3_r", [P, 2, C, B])
        s = sb("d3_s", [P, 2, J, F])
        x1 = sb("d3_x1", [P, 4, J, F])
        u = sb("d3_u", [P, 4, J, F])
        o = sb("d3_o", [P, 4, J, F])
        st1, st2 = sb("d3_st1", [P, 4, J, 6]), sb("d3_st2", [P, 4, J, 6])
        mv, v, rs = sb("d3_mv", [P, 4, 2 * J, 2]), sb("d3_v", [P, 4, 2 * J]), sb("d3_rs", [P, 4, 2 * J])
        nm, nb = sb("d3_nm", [P, 4, J]), sb("d3_nb", [P, 4, J])
        pN = [c.enter_context(nc.psum_tensor(f"d3_pN{n}", [P, J, F], F32)) for n in range(2)]
        h2_full, y_full = [sem(f"d3_h2_full{n}") for n in range(4)], [sem(f"d3_y_full{n}") for n in range(4)]
        x1_out, o_out = ([sem(f"d3_x1_out{n}") for n in range(4)],
                               [sem(f"d3_o_out{n}") for n in range(4)])
        relu_done, turned, s_done, st1_done, st2_done, x1_done, u_done, o_done = (
            sem("d3_relu"), sem("d3_turned"), sem("d3_s_done"), sem("d3_st1_done"), sem("d3_st2_done"),
            sem("d3_x1_done"), sem("d3_u_done"), sem("d3_o_done"))
        mv_done, v_done, rs_done, nb_done, past, dve_past = (
            sem("d3_mv_done"), sem("d3_v_done"), sem("d3_rs_done"), sem("d3_nb_done"), sem("d3_past"), sem("d3_dve_past"))
        coef, coef_ready, coef_vector, coef_pool = bn_coefficients(nc, sem, sb, K, 1, K.stats2, "bn2")
        block = c.enter_context(nc.Block())
        real = batch_of(S.NB)

        def both(k):
            return slice(0 if real(k + 2) else J, 2 * J if real(k) else J)

        @block.sync
        def _(sp):
            rows = node_rows(A["y"], S)
            x1_rows, out_rows = node_rows(A["x1"], S), node_rows(A["out"], S)

            def load_h2(k, q):
                sp.dma_start(h2[:, q], A["h2"][bass.ds(k, 1)].rearrange("o p f -> (o p) f")).then_inc(h2_full[q], 16)

            def load_y(k, q):
                sp.dma_start(y[:, q], rows(k)).then_inc(y_full[q], 16)

            def at(k):
                return k if isinstance(k, int) else sp.snap(k)

            def fresh(k):
                return slice(S.dup, P) if isinstance(k, int) and k == S.NB - 1 else slice(0, P)

            for q in range(4):
                load_h2(q, q)
                load_y(q, q)

            def step(k, q):
                h2_next, y_next, x1_now, o_now = at(k + 7), at(k + 6), at(k + 1), at(k - 1)
                if real(k + 7) and real(k + 3):
                    sp.wait_ge(relu_done, k + 4)
                    load_h2(h2_next, (q + 3) % 4)
                if real(k + 6) and real(k + 2):
                    sp.wait_ge(s_done, k + 3)
                    load_y(y_next, (q + 2) % 4)
                if real(k + 1):
                    sp.wait_ge(x1_done, k + 2)
                    b, some = (q + 1) % 4, fresh(k + 1)
                    sp.dma_start(x1_rows(x1_now)[some], x1[some, b].rearrange("p j f -> p (j f)")).then_inc(x1_out[b], 16)
                if real(k - 1):
                    sp.wait_ge(o_done, k)
                    b, some = (q - 1) % 4, fresh(k - 1)
                    sp.dma_start(out_rows(o_now)[some], o[some, b].rearrange("p j f -> p (j f)")).then_inc(o_out[b], 16)

            batch_steps(sp, S.NB, step, 8)
            for q in range(4):
                sp.wait_ge(x1_out[q], 16 * ((S.NB - 1 - q) // 4 + 1))
                sp.wait_ge(o_out[q], 16 * ((S.NB - 1 - q) // 4 + 1))

        @block.tensor
        def _(pe):
            def turn(k, b):
                pe.wait_ge(relu_done, k + 1)
                wait(pe, s_done, k - 1)
                for j in range(J):
                    for cc in range(C):
                        last = pe.transpose(pN[b][:, j, cc * P:(cc + 1) * P], r[:, b, cc, j * P:(j + 1) * P], K.ident[:])
                last.then_inc(turned, 1)

            turn(0, 0)
            turn(1, 1)
            with pe.Fori(0, (S.NB - 2) // 2) as i:
                for k, b in halves(i):
                    turn(k + 2, b)

        @block.scalar
        def _(act):
            act.wait_ge(coef_ready, 1)

            def relu(k, q):
                act.wait_ge(h2_full[q], 4 * (k - q) + 16)
                wait(act, turned, k - 1)
                for cc in range(C):
                    last = act.activation(r[:, q % 2, cc], h2[:, q, cc * B:(cc + 1) * B], ACT.Relu,
                                          bias=coef[:, 1, cc:cc + 1], scale=coef[:, 0, cc:cc + 1])
                last.then_inc(relu_done, 1)

            def normed(k, q):
                act.wait_ge(nb_done, k + 1)
                wait(act, o_out[q], 4 * (k - q))
                for j in range(J):
                    last = act.activation(o[:, q, j], u[:, q, j], ACT.Identity, bias=nb[:, q, j:j + 1],
                                          scale=rs[:, q, J + j:J + j + 1])
                last.then_inc(o_done, 1)

            def step(k, q):
                if real(k + 3):
                    relu(k + 3, (q + 3) % 4)
                if real(k - 1):
                    normed(k - 1, (q - 1) % 4)

            batch_steps(act, S.NB, step, 4)

        @block.gpsimd
        def _(pool):
            coef_pool(pool)

            def deviations(k, q):
                now = both(k)
                pool.wait_ge(mv_done, k + 3)
                pool.sem_inc(past, 1)
                if real(k):
                    pool.tensor_scalar(out=nm[:, q], in0=mv[:, q, J:2 * J, 0], scalar1=-1.0, scalar2=None, op0=ALU.mult)
                pool.tensor_scalar(out=v[:, q, now], in0=mv[:, q, now, 1], scalar1=EPS, scalar2=None, op0=ALU.add).then_inc(v_done, 1)
                pool.wait_ge(v_done, k + 3)
                pool.tensor_tensor(out=rs[:, q, now], in0=v[:, q, now], in1=K.minus_half[:, now], op=ALU.pow).then_inc(rs_done, 1)
                if real(k):
                    pool.wait_ge(rs_done, k + 3)
                    pool.tensor_tensor(out=nb[:, q], in0=nm[:, q], in1=rs[:, q, J:2 * J], op=ALU.mult).then_inc(nb_done, 1)

            def add_base(k, q):
                pool.wait_ge(x1_done, k + 1)
                wait(pool, o_done, k - 3)
                wide = K.base[:].rearrange("p (o f) -> p o f", o=1).to_broadcast([P, J, F])
                pool.tensor_tensor(out=u[:, q], in0=x1[:, q], in1=wide, op=ALU.add).then_inc(u_done, 1)

            def step(k, q):
                if real(k + 1):
                    add_base(k + 1, (q + 1) % 4)
                if real(k + 2) or real(k):
                    deviations(k, q)

            batch_steps(pool, S.NB, step, 4)

        @block.vector
        def _(dve):
            coef_vector(dve)

            def add(k, q):
                dve.wait_ge(turned, k + 1)
                dve.wait_ge(y_full[q], 4 * (k - q) + 16)
                wait(dve, x1_done, k - 1)
                dve.scalar_tensor_tensor(out=s[:, q % 2], in0=y[:, q].rearrange("p (j f) -> p j f", j=J), scalar=2.0,
                                         in1=pN[q % 2][:], op0=ALU.mult, op1=ALU.add).then_inc(s_done, 1)

            def normed(k, q):
                dve.wait_ge(rs_done, k + 1)
                wait(dve, x1_out[q], 4 * (k - q))
                before = (q - 2) % 4
                for j in range(J):
                    last = dve.tensor_scalar(out=x1[:, q, j], in0=s[:, q % 2, j], scalar1=mv[:, before, j, 0:1],
                                             scalar2=rs[:, before, j:j + 1], op0=ALU.subtract, op1=ALU.mult)
                last.then_inc(x1_done, 1)

            def step(k, q):
                if real(k + 2):
                    add(k + 2, (q + 2) % 4)
                if real(k):
                    dve.wait_ge(u_done, k + 1)
                    row_stats(dve, st2[:, q], u[:, q], st2_done)
                if real(k + 1):
                    normed(k + 1, (q + 1) % 4)
                if real(k + 2):
                    dve.wait_ge(s_done, k + 3)
                    row_stats(dve, st1[:, q], s[:, q % 2], st1_done)
                if real(k + 2) or real(k):
                    if real(k):
                        dve.wait_ge(st2_done, k + 1)
                    if real(k + 2):
                        dve.wait_ge(st1_done, k + 3)
                    dve.sem_inc(dve_past, 1)
                    for j in range(both(k).start, both(k).stop):
                        last = dve.bn_aggr(mv[:, q, j], st1[:, q, j] if j < J else st2[:, q, j - J])
                    last.then_inc(mv_done, 1)

            batch_steps(dve, S.NB, step, 4)


def edges1(nc, A, K, S):
    with ExitStack() as c:
        used = c.enter_context(stage_semaphores(nc))

        def sb(name, shape, dt=F32):
            return c.enter_context(nc.sbuf_tensor(name, shape, dt))

        def sem(name):
            used.append(nc.alloc_semaphore("e1_" + name))
            return used[-1]

        def part(name, shape):
            return sb(name + "_h", shape, F32R), sb(name + "_l", shape, F32R)

        xs, xd = sb("e1_xs", [P, 2, J, F]), sb("e1_xd", [P, 2, J, F])
        idx = sb("e1_idx", [P, 3, 2, J], I32)
        dst_row, rel_row = sb("e1_dst_row", [P, 2, B], I32), sb("e1_rel_row", [P, 2, B], I32)
        has_rel = sb("e1_has_rel", [P, 2, 2, B])
        has_k = sb("e1_has_k", [2, 2, B], F32R)
        same, cont = sb("e1_same", [P, 2, J, P]), sb("e1_cont", [P, 2, J, P])
        xt = part("e1_xt", [P, C, B])
        hid = [sb(f"e1_hid{r}", [P, C, B]) for r in range(2)]
        hidp = [part(f"e1_hidp{r}", [P, C, B]) for r in range(2)]
        msg = sb("e1_msg", [P, J, F])
        agg = sb("e1_agg", [P, C, B])
        aggp = part("e1_aggp", [P, C, B])
        gate = [sb(f"e1_gate{g}", [P, C, B]) for g in range(GATES)]
        cell, cell_t, hn = sb("e1_cell", [P, C, B]), sb("e1_cell_t", [P, C, B]), sb("e1_hn", [P, C, B])
        hnp = part("e1_hnp", [P, C, B])
        m1, m2 = sb("e1_m1", [P, B]), sb("e1_m2", [P, B])
        m1p, m2p = part("e1_m1p", [P, B]), part("e1_m2p", [P, B])
        u = sb("e1_u", [P, J, F])
        st, mv = sb("e1_st", [P, J, 6]), sb("e1_mv", [P, J, 2])
        v, rs = sb("e1_v", [P, J]), sb("e1_rs", [P, J])
        o = sb("e1_o", [P, 2, J, F])
        pX = c.enter_context(nc.psum_tensor("pX", [P, C, B], F32))
        pR = c.enter_context(nc.psum_tensor("pR", [P, C, B], F32))
        pG = c.enter_context(nc.psum_tensor("pG", [P, C, B], F32))
        pM = c.enter_context(nc.psum_tensor("pM", [P, J, F], F32))

        rows_full, xs_full, xd_full, o_out = ([sem(f"{n}{b}") for b in range(2)] for n in
                                              ("rows_full", "xs_full", "xd_full", "o_out"))
        idx_src, idx_dst, idx_out, past, dve_past, agg_clear = (
            sem(n) for n in ("idx_src", "idx_dst", "idx_out", "past", "dve_past", "agg_clear"))
        masked, turned, xt_hi, xt_lo = (sem(n) for n in ("masked", "turned", "xt_hi", "xt_lo"))
        rel_done, relu_done, mult_done, hid_hi, hid_lo = (sem(n) for n in
                                                          ("rel_done", "relu_done", "mult_done", "hid_hi", "hid_lo"))
        m_done, msg_done, sum_done, carried, agg_hi, agg_lo = (
            sem(n) for n in ("m_done", "msg_done", "sum_done", "carried", "agg_hi", "agg_lo"))
        gate_done, gate_on, cell_done, cell_on, hn_done, hn_hi, hn_lo = (
            sem(n) for n in ("gate_done", "gate_on", "cell_done", "cell_on", "hn_done", "hn_hi", "hn_lo"))
        m1_done, m1_on, m1_hi, m1_lo, m2_done, m2_on, m2_hi, m2_lo = (
            sem(n) for n in ("m1_done", "m1_on", "m1_hi", "m1_lo", "m2_done", "m2_on", "m2_hi", "m2_lo"))
        y_done, biased, u_done, st_done, mv_done, v_done, rs_done, o_done = (
            sem(n) for n in ("y_done", "biased", "u_done", "st_done", "mv_done", "v_done", "rs_done", "o_done"))
        block = c.enter_context(nc.Block())
        EB = S.EB

        def real(k):
            return not isinstance(k, int) or 0 <= k < EB

        def steps(engine, step):
            for k in (-2, -1, 0):
                step(k, k % 2)
            with engine.Fori(0, (EB - 3) // 2) as i:
                step(2 * i + 1, 1)
                step(2 * i + 2, 0)
            for k in (EB - 2, EB - 1, EB):
                step(k, k % 2)

        @block.sync
        def _(sp):
            full = (EB - 1) * B

            def load(k, b):
                at = k if isinstance(k, int) else sp.snap(k)
                wait(sp, masked, k - 1)
                for t, src in ((dst_row, "dst"), (rel_row, "rel")):
                    sp.dma_start(t[:, b], A[src][0:full].rearrange("(b e) -> b e", e=B)[bass.ds(at, 1)]
                                 .to_broadcast([P, B])).then_inc(rows_full[b], 16)

            load(0, 0)
            load(1, 1)
            with sp.Fori(1, (EB - 1) // 2) as i:
                for k, b in halves(i):
                    load(k, b)
            sp.wait_ge(masked, EB - 2)
            for t, src in ((dst_row, "dst"), (rel_row, "rel")):
                sp.dma_start(t[:, 0, 0:S.tail_edges], A[src][full:S.E].rearrange("(a e) -> a e", a=1)
                             .to_broadcast([P, S.tail_edges])).then_inc(rows_full[0], 16)

        @block.gpsimd
        def _(pool):
            last_node = pool.to_reg(S.N - 1)

            def fetch(b, into, which, full):
                for j in range(J):
                    pool.indirect_dma_start(
                        out=into[:, b, j], out_offset=None, in_=A["x1"],
                        in_offset=bass.IndirectOffsetOnAxis(ap=idx[:, which, b, j:j + 1], axis=0),
                        bounds_check=last_node, oob_is_err=False).then_inc(full[b], 16)

            def mult(k, b, r):
                pool.wait_ge(relu_done, 2 * k + r + 1)
                wide = has_rel[:, b, r].rearrange("p (o n) -> p o n", o=1).to_broadcast([P, C, B])
                pool.tensor_tensor(out=hid[r][:], in0=hid[r][:], in1=wide, op=ALU.mult).then_inc(mult_done, 1)

            def step(k, b):
                if real(k + 1):
                    pool.wait_ge(masked, k + 2)
                    pool.sem_inc(past, 1)
                    mult(k + 1, 1 - b, 0)
                if real(k - 1):
                    pool.wait_ge(mv_done, k)
                    pool.sem_inc(past, 1)
                    pool.tensor_scalar(out=v[:], in0=mv[:, :, 1], scalar1=EPS, scalar2=None, op0=ALU.add).then_inc(v_done, 1)
                    pool.wait_ge(v_done, k)
                    pool.tensor_tensor(out=rs[:], in0=v[:], in1=K.minus_half[:, 0:J], op=ALU.pow).then_inc(rs_done, 1)
                if real(k + 2):
                    if not (isinstance(k, int) and k < 0):
                        pool.wait_ge(turned, k + 1)
                        pool.sem_inc(past, 1)
                    pool.tensor_copy(idx[:, 0, b], K.src[:, bass.ds((k + 2) * J, J)]).then_inc(idx_src, 1)
                    pool.wait_ge(idx_src, k + 3)
                    pool.sem_inc(past, 1)
                    fetch(b, xs, 0, xs_full)
                if real(k + 1):
                    mult(k + 1, 1 - b, 1)
                    if not (isinstance(k, int) and k < 1):
                        pool.wait_ge(u_done, k)
                        pool.sem_inc(past, 1)
                    pool.tensor_copy(idx[:, 1, 1 - b], K.dst_gather[:, bass.ds((k + 1) * J, J)]).then_inc(idx_dst, 1)
                    pool.wait_ge(idx_dst, k + 2)
                    pool.sem_inc(past, 1)
                    fetch(1 - b, xd, 1, xd_full)
                if real(k - 1):
                    if not (isinstance(k, int) and k < 3):
                        pool.wait_ge(o_out[1 - b], (k - 1 - (1 - b)) * 32)
                        pool.sem_inc(past, 1)
                    pool.tensor_copy(idx[:, 2, 1 - b], K.target[:, bass.ds((k - 1) * J, J)]).then_inc(idx_out, 1)
                    pool.wait_ge(idx_out, k)
                    pool.sem_inc(past, 1)
                    pool.wait_ge(o_done, k)
                    pool.sem_inc(past, 1)
                    for j in range(J):
                        pool.indirect_dma_start(
                            out=A["out"], out_offset=bass.IndirectOffsetOnAxis(ap=idx[:, 2, 1 - b, j:j + 1], axis=0),
                            in_=o[:, 1 - b, j], in_offset=None, bounds_check=last_node,
                            oob_is_err=False).then_inc(o_out[1 - b], 16)
                if real(k):
                    pool.wait_ge(xd_full[b], 32 * (k - b) + 64)
                    pool.sem_inc(past, 1)
                    wide = K.b3[:].rearrange("p (o f) -> p o f", o=1).to_broadcast([P, J, F])
                    pool.tensor_tensor(out=xd[:, b], in0=xd[:, b], in1=wide, op=ALU.add).then_inc(biased, 1)

            steps(pool, step)
            for b in range(2):
                pool.wait_ge(o_out[b], 64 * ((EB - 1 - b) // 2 + 1))

        @block.tensor
        def _(pe):
            def turn(k, b):
                pe.wait_ge(xs_full[b], 32 * (k - b) + 64)
                wait(pe, carried, (k - 1) * J)
                for cc in range(C):
                    for j in range(J):
                        last = pe.transpose(pX[:, cc, j * P:(j + 1) * P], xs[:, b, j, cc * P:(cc + 1) * P], K.ident[:])
                last.then_inc(turned, 1)

            def relation(k, r):
                pe.wait_ge(xt_lo, k + 1)
                wait(pe, relu_done, 2 * k + r)
                for oc in range(C):
                    for ic in range(C):
                        blk = REL + (r * C + ic) * C + oc
                        last = mm3(pe, pR[:, oc], (K.wl_h[:, blk], K.wl_l[:, blk]), (xt[0][:, ic], xt[1][:, ic]),
                                   ic == 0, ic == C - 1)
                last.then_inc(rel_done, 1)

            def second_layer(k, b):
                pe.wait_ge(hid_lo, 2 * k + 2)
                wait(pe, u_done, k - 1)
                for j in range(J):
                    cols = slice(j * P, (j + 1) * P)
                    pe.matmul(pM[:, j], has_k[:, b, cols], K.rows_h[:, 1], start=True, stop=False)
                    pe.matmul(pM[:, j], has_k[:, b, cols], K.rows_l[:, 1], start=False, stop=False)
                    for r in range(2):
                        for ic in range(C):
                            last = mm3(pe, pM[:, j], (hidp[r][0][:, ic, cols], hidp[r][1][:, ic, cols]),
                                       (rel_w(K.wl_h, r, ic), rel_w(K.wl_l, r, ic)), False, r == 1 and ic == C - 1)
                last.then_inc(m_done, 1)

            def segment_sums(k, b):
                pe.wait_ge(msg_done, k + 1)
                pe.wait_ge(xt_lo, min(k + 2, EB) if isinstance(k, int) else k + 2)
                for j in range(J):
                    for cc in range(C):
                        last = pe.matmul(pX[:, cc, j * P:(j + 1) * P], msg[:, j, cc * P:(cc + 1) * P], same[:, b, j],
                                         start=True, stop=True)
                last.then_inc(sum_done, 1)

            def gates(k, g):
                pe.wait_ge(agg_lo, k + 1)
                if g == 0:
                    wait(pe, m2_on, k)
                else:
                    pe.wait_ge(gate_on, GATES * k + g)
                for oc in range(C):
                    for ic in range(C):
                        blk = IH + ic * GATES * C + g * C + oc
                        last = mm3(pe, pG[:, oc], (K.wl_h[:, blk], K.wl_l[:, blk]), (aggp[0][:, ic], aggp[1][:, ic]),
                                   ic == 0, ic == C - 1)
                last.then_inc(gate_done, 1)

            def mlp1(k):
                pe.wait_ge(hn_lo, k + 1)
                pe.wait_ge(gate_on, GATES * k + GATES)
                for ic in range(C):
                    last = mm3(pe, pG[:, 0], (K.wl_h[:, M1 + ic], K.wl_l[:, M1 + ic]), (hnp[0][:, ic], hnp[1][:, ic]),
                               ic == 0, ic == C - 1)
                last.then_inc(m1_done, 1)

            def mlp2(k):
                pe.wait_ge(m1_lo, k + 1)
                mm3(pe, pG[:, 1], (K.wl_h[:, M2], K.wl_l[:, M2]), (m1p[0][:], m1p[1][:]), True, True).then_inc(m2_done, 1)

            def mlp3(k):
                pe.wait_ge(m2_lo, k + 1)
                pe.wait_ge(msg_done, min(k + 2, EB) if isinstance(k, int) else k + 2)
                for j in range(J):
                    cols = slice(j * P, (j + 1) * P)
                    last = mm3(pe, pM[:, j], (m2p[0][:, cols], m2p[1][:, cols]), (w3(K.wl_h), w3(K.wl_l)), True, True)
                last.then_inc(y_done, 1)

            def step(k, b):
                if real(k + 1):
                    relation(k + 1, 0)
                if real(k - 1):
                    mlp3(k - 1)
                if real(k):
                    gates(k, 0)
                if real(k + 1):
                    relation(k + 1, 1)
                if real(k):
                    gates(k, 1)
                if real(k + 2):
                    turn(k + 2, b)
                if real(k):
                    gates(k, 2)
                if real(k + 1):
                    second_layer(k + 1, 1 - b)
                if real(k):
                    mlp1(k)
                if real(k + 1):
                    segment_sums(k + 1, 1 - b)
                if real(k):
                    mlp2(k)

            steps(pe, step)

        @block.scalar
        def _(act):
            def relation(k, r):
                act.wait_ge(rel_done, 2 * k + r + 1)
                wait(act, m_done, k)
                for cc in range(C):
                    last = act.activation(hid[r][:, cc], pR[:, cc], ACT.Relu, bias=K.rel_b[:, r * C + cc:r * C + cc + 1])
                last.then_inc(relu_done, 1)

            def relation_hi(k, r):
                act.wait_ge(mult_done, 2 * k + r + 1)
                act.activation(hidp[r][0][:], hid[r][:], ACT.Copy).then_inc(hid_hi, 1)

            def gates(k, g, func):
                act.wait_ge(gate_done, GATES * k + g + 1)
                for cc in range(C):
                    last = act.activation(gate[g][:, cc], pG[:, cc], func, bias=K.gate_b[:, g * C + cc:g * C + cc + 1])
                last.then_inc(gate_on, 1)

            def step(k, b):
                if real(k + 1):
                    relation(k + 1, 0)
                    relation_hi(k + 1, 0)
                if real(k):
                    gates(k, 0, ACT.Sigmoid)
                if real(k + 1):
                    relation(k + 1, 1)
                if real(k):
                    gates(k, 1, ACT.Tanh)
                if real(k + 1):
                    relation_hi(k + 1, 1)
                if real(k):
                    act.wait_ge(cell_done, k + 1)
                    act.activation(cell_t[:], cell[:], ACT.Tanh).then_inc(cell_on, 1)
                if real(k + 2):
                    act.wait_ge(turned, k + 3)
                    wait(act, rel_done, 2 * k + 4)
                    act.activation(xt[0][:], pX[:], ACT.Copy).then_inc(xt_hi, 1)
                if real(k):
                    gates(k, 2, ACT.Sigmoid)
                    act.wait_ge(hn_done, k + 1)
                    act.activation(hnp[0][:], hn[:], ACT.Copy).then_inc(hn_hi, 1)
                if real(k + 1):
                    act.wait_ge(m_done, k + 2)
                    wait(act, sum_done, k + 1)
                    act.activation(msg[:], pM[:], ACT.Relu).then_inc(msg_done, 1)
                if real(k):
                    act.wait_ge(m1_done, k + 1)
                    act.activation(m1[:], pG[:, 0], ACT.Relu, bias=K.m_b[:, 0:1]).then_inc(m1_on, 1)
                    act.wait_ge(m1_on, k + 1)
                    act.activation(m1p[0][:], m1[:], ACT.Copy).then_inc(m1_hi, 1)
                    act.wait_ge(m2_done, k + 1)
                    wait(act, y_done, k)
                    act.activation(m2[:], pG[:, 1], ACT.Relu, bias=K.m_b[:, 1:2]).then_inc(m2_on, 1)
                    act.wait_ge(m2_on, k + 1)
                    act.activation(m2p[0][:], m2[:], ACT.Copy).then_inc(m2_hi, 1)
                if real(k + 1):
                    act.wait_ge(carried, J * k + 2 * J)
                    act.activation(aggp[0][:], agg[:], ACT.Copy).then_inc(agg_hi, 1)

            steps(act, step)

        @block.vector
        def _(dve):
            def low(parts, whole, hi_done, lo_done, count):
                dve.wait_ge(hi_done, count)
                dve.tensor_tensor(out=parts[1][:], in0=whole, in1=parts[0][:].bitcast(F32), op=ALU.subtract).then_inc(lo_done, 1)

            def masks(k, b):
                dve.wait_ge(rows_full[b], 16 * (k - b) + 32)
                wait(dve, mult_done, 2 * k - 2)
                wait(dve, sum_done, k - 1)
                rows = dst_row[:, b].rearrange("p (j e) -> p j e", j=J)
                for out, key in ((same, K.dst_f), (cont, K.prev)):
                    cols = key[:, bass.ds(k * J, J)].rearrange("p (j o) -> p j o", o=1).to_broadcast([P, J, P])
                    dve.tensor_tensor(out=out[:, b], in0=rows, in1=cols, op=ALU.is_equal)
                for r in range(2):
                    dve.tensor_scalar(out=has_rel[:, b, r], in0=rel_row[:, b], scalar1=float(r), scalar2=None, op0=ALU.is_equal)
                dve.tensor_scalar(out=has_k[:, b], in0=rel_row[0:2, b], scalar1=K.part[0:2, 0:1], scalar2=None,
                                  op0=ALU.is_equal).then_inc(masked, 1)

            def carry(k, b):
                dve.wait_ge(sum_done, k + 1)
                wait(dve, agg_lo, k)
                for j in range(J):
                    wait(dve, carried, J * k + j)
                    before = j * P - 1 if j else B - 1
                    for cc in range(C):
                        cols = slice(j * P, (j + 1) * P)
                        last = dve.scalar_tensor_tensor(out=agg[:, cc, cols], in0=cont[:, b, j],
                                                        scalar=agg[:, cc, before:before + 1], in1=pX[:, cc, cols],
                                                        op0=ALU.mult, op1=ALU.add)
                    last.then_inc(carried, 1)

            def step(k, b):
                if real(k - 1):
                    dve.wait_ge(y_done, k)
                    dve.wait_ge(biased, k)
                    wait(dve, o_done, k - 1)
                    dve.tensor_tensor(out=u[:], in0=pM[:], in1=xd[:, 1 - b], op=ALU.add).then_inc(u_done, 1)
                    dve.wait_ge(u_done, k)
                    row_stats(dve, st, u, st_done)
                if real(k + 1):
                    low(hidp[0], hid[0][:], hid_hi, hid_lo, 2 * k + 3)
                if real(k - 1):
                    dve.wait_ge(st_done, k)
                    row_moments(dve, mv, st, dve_past, mv_done)
                if real(k + 2):
                    masks(k + 2, b)
                if real(k - 1):
                    dve.wait_ge(rs_done, k)
                    if not (isinstance(k, int) and k < 3):
                        dve.wait_ge(o_out[1 - b], (k - 1 - (1 - b)) * 32)
                    for j in range(J):
                        last = dve.tensor_scalar(out=o[:, 1 - b, j], in0=u[:, j], scalar1=mv[:, j, 0:1],
                                                 scalar2=rs[:, j:j + 1], op0=ALU.subtract, op1=ALU.mult)
                    last.then_inc(o_done, 1)
                if real(k):
                    dve.wait_ge(gate_on, GATES * k + 2)
                    dve.tensor_tensor(out=cell[:], in0=gate[0][:], in1=gate[1][:], op=ALU.mult).then_inc(cell_done, 1)
                if real(k + 1):
                    low(hidp[1], hid[1][:], hid_hi, hid_lo, 2 * k + 4)
                if real(k + 2):
                    low(xt, pX[:], xt_hi, xt_lo, k + 3)
                if real(k):
                    dve.wait_ge(gate_on, GATES * k + GATES)
                    dve.wait_ge(cell_on, k + 1)
                    dve.tensor_tensor(out=hn[:], in0=gate[2][:], in1=cell_t[:], op=ALU.mult).then_inc(hn_done, 1)
                    low(hnp, hn[:], hn_hi, hn_lo, k + 1)
                    low(m1p, m1[:], m1_hi, m1_lo, k + 1)
                if real(k + 1):
                    carry(k + 1, 1 - b)
                if real(k):
                    low(m2p, m2[:], m2_hi, m2_lo, k + 1)
                if real(k + 1):
                    low(aggp, agg[:], agg_hi, agg_lo, k + 2)

            dve.memset(agg[:], 0.0).then_inc(agg_clear, 1)
            dve.wait_ge(agg_clear, 1)
            steps(dve, step)


class Persistent:

    def __init__(self, nc, c, S):
        def sb(name, shape, dt=F32):
            return c.enter_context(nc.sbuf_tensor("k_" + name, shape, dt))

        self.ident = sb("ident", [P, P])
        self.ones = sb("ones", [P, P], F32R)
        self.w0_h, self.w0_l = sb("w0_h", [P, 3, C, F], F32R), sb("w0_l", [P, 3, C, F], F32R)
        self.wl_h, self.wl_l = sb("wl_h", [P, NBLK, P], F32R), sb("wl_l", [P, NBLK, P], F32R)
        self.rows_h, self.rows_l = sb("rows_h", [2, 2, F], F32R), sb("rows_l", [2, 2, F], F32R)
        self.src, self.dst_gather = sb("src", [P, S.TC], I32), sb("dst_gather", [P, S.TC], I32)
        self.target = sb("target", [P, S.TC], I32)
        self.dst_f = sb("dst_f", [P, S.TC])
        self.prev, self.prev_row = sb("prev", [P, S.TC]), sb("prev_row", [P, S.TC])
        self.part_i, self.part, self.is_last = sb("part_i", [P, 1], I32), sb("part", [P, 1]), sb("is_last", [P, 1])
        self.minus_half = sb("minus_half", [P, 2 * J])
        self.rel_b, self.m_b, self.gate_b = sb("rel_b", [P, 2 * C]), sb("m_b", [P, 2]), sb("gate_b", [P, GATES * C])
        self.bn = sb("bn", [P, 6, C])
        self.b3, self.base = sb("b3", [P, F]), sb("base", [P, F])
        self.stats, self.stats2 = sb("stats", [P, C, S.NB, 6]), sb("stats2", [P, C, S.NB, 6])
        self.copied = c.enter_context(nc.semaphore("copied"))


def build(nc, A, nodes, edges):
    S = Shapes(nodes, edges)
    for name, shape in (("y", (S.N, F)), ("x1", (S.N, F)), ("sums", (S.TC * P, F)),
                        ("h1", (S.NB, P, C * B)), ("h2", (S.NB, P, C * B))):
        A[name] = nc.dram_tensor(f"scratch_{name}", shape, F32, kind="Internal").ap()
    with ExitStack() as c:
        K = Persistent(nc, c, S)
        for stage in (setup, edges0, scatter0, dense1, dense2, dense3, edges1):
            stage(nc, A, K, S)


_INS = {"x": "x", "src": "src", "dst": "dst", "attr": "edge_attr_256", "bases": "edge_attr_256_n2",
        "rel": "edge_type_2", "W_pre": "L0_gnn_W_pre", "b_pre": "L0_gnn_b_pre", "W1": "L0_gnn_W1", "b1": "L0_gnn_b1",
        "g1": "L0_gnn_g1", "be1": "L0_gnn_be1", "W2": "L0_gnn_W2", "b2": "L0_gnn_b2", "g2": "L0_gnn_g2",
        "be2": "L0_gnn_be2", "W_rel": "L1_gnn_W_rel", "b_rel": "L1_gnn_b_rel", "W_ih": "L1_gnn_W_ih",
        "b_ih": "L1_gnn_b_ih", "b_hh": "L1_gnn_b_hh", "M_W1": "L1_gnn_W1", "M_b1": "L1_gnn_b1", "M_W2": "L1_gnn_W2",
        "M_b2": "L1_gnn_b2", "M_W3": "L1_gnn_W3", "M_b3": "L1_gnn_b3"}


def kernel(**inputs):
    import concourse.bacc as bacc
    from concourse.bass_utils import run_bass_kernel_spmd

    nc = bacc.Bacc("TRN2", target_bir_lowering=False, num_devices=1)
    arrays, A = {}, {}
    for short, name in _INS.items():
        a = np.ascontiguousarray(inputs[name])
        arrays[f"in_{name}"] = a
        A[short] = nc.dram_tensor(f"in_{name}", a.shape, mybir.dt.from_np(a.dtype), kind="ExternalInput").ap()
    nodes, edges = inputs["x"].shape[0], inputs["src"].shape[0]
    A["out"] = nc.dram_tensor("out_0", (nodes, F), F32, kind="ExternalOutput").ap()
    build(nc, A, nodes, edges)
    return run_bass_kernel_spmd(nc, [arrays], core_ids=[0]).results[0]["out_0"]
```

```python
from contextlib import ExitStack, contextmanager

import numpy as np

import concourse.bass as bass
from concourse import mybir

F32 = mybir.dt.float32
F32R = mybir.dt.float32r
I32 = mybir.dt.int32
ALU = mybir.AluOpType
ACT = mybir.ActivationFunctionType

P = 128
F = 256
C = F // P
J = 4
B = J * P
EPS = 1e-5
NO_NODE = -5.0

REL, IH, M1, M2, M3, NBLK = 0, 8, 20, 22, 23, 25
GATES = 3
GATE_ROWS = (0, 2, 3)


class Shapes:
    def __init__(self, nodes, edges):
        self.N, self.E = nodes, edges
        self.NB = -(-nodes // B)
        self.NP = self.NB // 2
        self.last_node = nodes - B
        self.dup = (self.NB * B - nodes) // J
        self.ET = -(-edges // P)
        self.EB = -(-self.ET // J)
        self.tail_tiles = self.ET - J * (self.EB - 1)
        self.tail_edges = edges - (self.EB - 1) * B
        self.tail_rows = edges - (self.ET - 1) * P
        self.TC = J * self.EB
        self.piece = nodes // (self.EB + 3)
        assert self.NB % 2 == 0 and self.NP % 2 == 1 and self.EB % 2 == 1 and self.EB >= 5
        assert self.ET == 2 * self.NP and (self.NB * B - nodes) % J == 0


def mm3(pe, out, lhs, rhs, first, last):
    pe.matmul(out, lhs[0], rhs[0], start=first, stop=False)
    pe.matmul(out, lhs[0], rhs[1], start=False, stop=False)
    return pe.matmul(out, lhs[1], rhs[0], start=False, stop=last)


@contextmanager
def stage_semaphores(nc):
    used = []
    yield used
    nc.clear_and_free_semaphores(used)
    nc.all_engine_barrier()


def wait(engine, semaphore, value):
    if not (isinstance(value, int) and value <= 0):
        engine.wait_ge(semaphore, value)


def halves(i):
    return ((2 * i, 0), (2 * i + 1, 1))


def quarters(i):
    return tuple((4 * i + q, q) for q in range(4))


def batch_steps(engine, n, step, ahead):
    loops = (n - ahead) // 4
    for k in range(-4, 4):
        step(k, k % 4)
    with engine.Fori(1, loops) as i:
        for k, q in quarters(i):
            step(k, q)
    for k in range(4 * loops, n + 1):
        step(k, k % 4)


def batch_of(n):
    return lambda k: not isinstance(k, int) or 0 <= k < n


def setup(nc, A, K, S):
    with ExitStack() as c:
        used = c.enter_context(stage_semaphores(nc))

        def sb(name, shape, dt=F32):
            return c.enter_context(nc.sbuf_tensor(name, shape, dt))

        def sem(name):
            used.append(nc.alloc_semaphore(name))
            return used[-1]

        raw0 = sb("raw0", [P, 3, C, F])
        raw_rel = sb("raw_rel", [P, 2, C, F])
        raw_ih = sb("raw_ih", [P, GATES * C, F])
        raw_m1 = sb("raw_m1", [P, F])
        raw_m2 = sb("raw_m2", [P, P])
        raw_m3 = sb("raw_m3", [P, C, P])
        rows, rows_h, rows_l = sb("rows", [4, 2, F]), sb("rows_h", [4, 2, F], F32R), sb("rows_l", [4, 2, F])
        keep_h, keep_l = sb("keep_h", [4, 1]), sb("keep_l", [4, 1])
        b_ih = sb("b_ih", [P, GATES * C])
        b_hh = sb("b_hh", [P, GATES * C])
        dst_i = sb("dst_i", [P, S.TC], I32)
        nxt_i = sb("nxt_i", [P, S.TC], I32)
        slot = sb("slot", [P, S.TC], I32)
        slot_f = sb("slot_f", [P, S.TC])
        differs = sb("differs", [P, S.TC])
        pick = sb("pick", [P, S.TC])
        last_row = sb("last_row", [P, P])
        gate = sb("gate", [P, GATES, C])
        cell = sb("cell", [P, C])
        cell_t = sb("cell_t", [P, C])
        hid = sb("hid", [P, C])
        hid_h, hid_l = sb("hid_h", [P, C, P], F32R), sb("hid_l", [P, C, P], F32R)
        a1, a1h, a1l = sb("a1", [P, P]), sb("a1h", [P, P], F32R), sb("a1l", [P, P], F32R)
        a2, a2h, a2l = sb("a2", [P, P]), sb("a2h", [P, P], F32R), sb("a2l", [P, P], F32R)
        wt = c.enter_context(nc.psum_tensor("wt", [P, 28, P], F32))
        small = c.enter_context(nc.psum_tensor("small", [P, 512], F32))

        tables_clear, loaded, tables_loaded = sem("tables_clear"), sem("loaded"), sem("tables_loaded")
        zeroed, consts, step, transposed = sem("zeroed"), sem("consts"), sem("step"), sem("transposed")
        gates_on, mlp_done, relu_done, weights_split = (sem("gates_on"), sem("mlp_done"), sem("relu_done"),
                                                        sem("weights_split"))
        product, rows_clear, spilled = sem("product"), sem("rows_clear"), sem("spilled")
        block = c.enter_context(nc.Block())

        loads = []

        @block.sync
        def _(sp):
            def load(dst, src):
                loads.append(sp.dma_start(dst, src).then_inc(loaded, 16))

            for n, name in enumerate(("W_pre", "W1", "W2")):
                load(raw0[:, n], A[name].rearrange("(c p) o -> p c o", p=P))
            load(raw_rel[:], A["W_rel"].rearrange("r (o p) i -> p r o i", p=P))
            for n, g in enumerate(GATE_ROWS):
                load(raw_ih[:, n * C:(n + 1) * C], A["W_ih"][g * F:(g + 1) * F, :].rearrange("(o p) i -> p o i", p=P))
            load(raw_m1[:], A["M_W1"])
            load(raw_m2[:], A["M_W2"])
            load(raw_m3[:], A["M_W3"].rearrange("(o p) i -> p o i", p=P))
            sp.wait_ge(rows_clear, 1)
            for p in (0, 2):
                load(rows[p:p + 1, 0, :], A["b_pre"].rearrange("(a f) -> a f", a=1))
                load(rows[p:p + 2, 1, :], A["b_rel"])
            load(K.b3[:], A["M_b3"].rearrange("(a f) -> a f", a=1).to_broadcast([P, F]))
            with nc.allow_non_contiguous_dma(reason="vectors and indices to columns"):
                for n, g in enumerate(GATE_ROWS):
                    for dst, src in ((b_ih, "b_ih"), (b_hh, "b_hh")):
                        load(dst[:, n * C:(n + 1) * C], A[src][g * F:(g + 1) * F].rearrange("(c p) -> p c", p=P))
                for n in range(2):
                    load(K.rel_b[:, n * C:(n + 1) * C], A["b_rel"][n, :].rearrange("(c p) -> p c", p=P))
                load(K.m_b[:, 0:1], A["M_b1"].rearrange("(c p) -> p c", p=P))
                load(K.m_b[:, 1:2], A["M_b2"].rearrange("(c p) -> p c", p=P))
                for n, name in enumerate(("b1", "g1", "be1", "b2", "g2", "be2")):
                    load(K.bn[:, n], A[name].rearrange("(c p) -> p c", p=P))
                full = (S.ET - 1) * P
                sp.wait_ge(tables_clear, 3)
                for table, src, ahead in ((K.src, "src", 0), (dst_i, "dst", 0), (nxt_i, "dst", 1)):
                    sp.dma_start(table[:, 0:S.ET - 1],
                                 A[src][ahead:full + ahead].rearrange("(t p) -> p t", p=P)).then_inc(tables_loaded, 16)
                    rest = S.tail_rows - ahead
                    sp.dma_start(table[0:rest, S.ET - 1:S.ET],
                                 A[src][full + ahead:S.E].rearrange("(p t) -> p t", t=1)).then_inc(tables_loaded, 16)
            sp.dma_start(A["y"][S.EB * S.piece:S.N, :], A["x"][S.EB * S.piece:S.N, :]).then_inc(K.copied, 16)
            sp.wait_ge(loaded, 16 * len(loads))
            sp.wait_ge(tables_loaded, 96)
            sp.wait_ge(weights_split, 2)
            for name, w in (("wl_h", K.wl_h), ("wl_l", K.wl_l)):
                sp.dma_start(A[name], w[:].rearrange("p b o -> p (b o)").bitcast(F32)).then_inc(spilled, 16)
            sp.wait_ge(spilled, 32)

        n_loads = len(loads)

        @block.gpsimd
        def _(pool):
            pool.memset(rows[:], 0.0).then_inc(rows_clear, 1)
            pool.memset(K.src[:], 0).then_inc(tables_clear, 1)
            pool.memset(dst_i[:], -1).then_inc(tables_clear, 1)
            pool.memset(nxt_i[:], -1).then_inc(tables_clear, 1)
            pool.iota(slot[:], pattern=[[P, S.TC]], base=S.N, channel_multiplier=1).then_inc(consts, 1)
            pool.iota(K.part_i[:], pattern=[[0, 1]], base=0, channel_multiplier=1).then_inc(consts, 1)
            pool.memset(K.minus_half[:], -0.5).then_inc(consts, 1)
            pool.memset(K.ident[:], 0.0).then_inc(zeroed, 1)
            pool.memset(last_row[:], 0.0).then_inc(zeroed, 1)
            pool.wait_ge(zeroed, 2)
            pool.affine_select(out=K.ident[:], in_=K.ident[:], compare_op=ALU.not_equal, fill=1.0, base=0,
                               pattern=[[-1, P]], channel_multiplier=1).then_inc(consts, 1)
            pool.affine_select(out=last_row[:], in_=last_row[:], compare_op=ALU.not_equal, fill=1.0, base=1 - P,
                               pattern=[[0, P]], channel_multiplier=1).then_inc(consts, 1)

        @block.tensor
        def _(pe):
            pe.wait_ge(consts, 5)
            pe.wait_ge(loaded, 16 * n_loads)
            for r in range(2):
                for ic in range(C):
                    for oc in range(C):
                        pe.transpose(wt[:, REL + (r * C + ic) * C + oc], raw_rel[:, r, oc, ic * P:(ic + 1) * P], K.ident[:])
            for ic in range(C):
                for oc in range(GATES * C):
                    pe.transpose(wt[:, IH + ic * GATES * C + oc], raw_ih[:, oc, ic * P:(ic + 1) * P], K.ident[:])
                pe.transpose(wt[:, M1 + ic], raw_m1[:, ic * P:(ic + 1) * P], K.ident[:])
            pe.transpose(wt[:, M2], raw_m2[:], K.ident[:])
            for oc in range(C):
                last = pe.transpose(wt[:, M3 + oc], raw_m3[:, oc], K.ident[:])
            last.then_inc(transposed, 1)
            pe.wait_ge(step, 1)
            pe.matmul(small[:, 0:S.TC - 1], last_row[:], K.dst_f[:, 0:S.TC - 1], start=True, stop=True).then_inc(product, 1)
            pe.wait_ge(step, 5)
            pe.wait_ge(weights_split, 2)
            pe.wait_ge(mlp_done, 1)
            for ic in range(C):
                last = mm3(pe, small[:, 0:P], (K.wl_h[:, M1 + ic], K.wl_l[:, M1 + ic]), (hid_h[:, ic], hid_l[:, ic]),
                           ic == 0, ic == C - 1)
            last.then_inc(product, 1)
            pe.wait_ge(mlp_done, 2)
            mm3(pe, small[:, 0:P], (K.wl_h[:, M2], K.wl_l[:, M2]), (a1h[:], a1l[:]), True, True).then_inc(product, 1)
            pe.wait_ge(mlp_done, 3)
            mm3(pe, small[:, 0:F], (a2h[:], a2l[:]), (w3(K.wl_h), w3(K.wl_l)), True, True).then_inc(product, 1)

        @block.scalar
        def _(act):
            act.wait_ge(step, 3)
            for n, func in ((0, ACT.Sigmoid), (1, ACT.Tanh), (2, ACT.Sigmoid)):
                act.activation(gate[:, n], K.gate_b[:, n * C:(n + 1) * C], func).then_inc(gates_on, 1)
            act.wait_ge(step, 4)
            act.activation(cell_t[:], cell[:], ACT.Tanh).then_inc(gates_on, 1)
            act.wait_ge(product, 2)
            act.activation(a1[:], small[:, 0:P], ACT.Relu, bias=K.m_b[:, 0:1]).then_inc(relu_done, 1)
            act.wait_ge(product, 3)
            act.activation(a2[:], small[:, 0:P], ACT.Relu, bias=K.m_b[:, 1:2]).then_inc(relu_done, 1)

        @block.vector
        def _(dve):
            t = 0
            link = sem("dve_link")

            def then(ins):
                nonlocal t
                t += 1
                ins.then_inc(link, 1)
                dve.wait_ge(link, t)

            dve.wait_ge(consts, 5)
            dve.wait_ge(tables_loaded, 96)
            dve.memset(K.ones[:].bitcast(F32), 1.0)
            dve.memset(K.prev_row[:, 0:1], NO_NODE)
            dve.memset(K.prev[:, 0:1], NO_NODE)
            dve.tensor_copy(K.part[:], K.part_i[:])
            dve.tensor_copy(slot_f[:], slot[:])
            dve.tensor_scalar(out=K.dst_gather[:], in0=dst_i[:], scalar1=0, scalar2=None, op0=ALU.max)
            dve.tensor_copy(K.dst_f[:], dst_i[:]).then_inc(step, 1)
            dve.wait_ge(step, 1)
            then(dve.tensor_tensor(out=differs[:], in0=dst_i[:], in1=nxt_i[:], op=ALU.not_equal))
            then(dve.tensor_tensor(out=pick[:], in0=K.dst_f[:], in1=slot_f[:], op=ALU.subtract))
            then(dve.tensor_tensor(out=pick[:], in0=pick[:], in1=differs[:], op=ALU.mult))
            then(dve.tensor_tensor(out=K.target[:], in0=pick[:], in1=slot_f[:], op=ALU.add))
            dve.wait_ge(product, 1)
            dve.tensor_copy(K.prev[:, 1:S.TC], small[:, 0:S.TC - 1]).then_inc(step, 1)
            then(dve.tensor_scalar(out=K.is_last[:], in0=K.part[:], scalar1=float(P - 1), scalar2=None, op0=ALU.is_equal))
            then(dve.tensor_scalar(out=pick[:, 0:S.TC - 1], in0=K.dst_f[:, 0:S.TC - 1], scalar1=NO_NODE,
                                   scalar2=K.is_last[:, 0:1], op0=ALU.subtract, op1=ALU.mult))
            then(dve.tensor_scalar(out=K.prev_row[:, 1:S.TC], in0=pick[:, 0:S.TC - 1], scalar1=NO_NODE, scalar2=None,
                                   op0=ALU.add))
            dve.wait_ge(loaded, 16 * n_loads)
            dve.tensor_tensor(out=K.gate_b[:], in0=b_ih[:], in1=b_hh[:], op=ALU.add).then_inc(step, 1)
            then(dve.tensor_copy(K.w0_h[:], raw0[:]))
            then(dve.tensor_tensor(out=K.w0_l[:], in0=raw0[:], in1=K.w0_h[:].bitcast(F32), op=ALU.subtract))
            then(dve.tensor_copy(rows_h[:], rows[:]))
            then(dve.tensor_tensor(out=rows_l[:], in0=rows[:], in1=rows_h[:].bitcast(F32), op=ALU.subtract))
            then(dve.tensor_scalar(out=keep_l[:], in0=K.part[0:4], scalar1=2.0, scalar2=None, op0=ALU.is_ge))
            then(dve.tensor_scalar(out=keep_h[:], in0=K.part[0:4], scalar1=2.0, scalar2=None, op0=ALU.is_lt))
            then(dve.tensor_scalar(out=K.row_rel[:], in0=keep_l[:], scalar1=-2.0, scalar2=K.part[0:4, 0:1],
                                   op0=ALU.mult, op1=ALU.add))
            then(dve.tensor_scalar(out=rows_l[:], in0=rows_l[:], scalar1=keep_l[:, 0:1], scalar2=None, op0=ALU.mult))
            for n in range(2):
                then(dve.scalar_tensor_tensor(out=K.rows[:, n], in0=rows_h[:, n].bitcast(F32), scalar=keep_h[:, 0:1],
                                              in1=rows_l[:, n], op0=ALU.mult, op1=ALU.add))
            dve.wait_ge(transposed, 1)
            dve.tensor_copy(K.wl_h[:], wt[:, 0:NBLK]).then_inc(weights_split, 1)
            dve.wait_ge(weights_split, 1)
            dve.tensor_tensor(out=K.wl_l[:], in0=wt[:, 0:NBLK], in1=K.wl_h[:].bitcast(F32), op=ALU.subtract).then_inc(weights_split, 1)
            dve.wait_ge(gates_on, 3)
            dve.tensor_tensor(out=cell[:], in0=gate[:, 0], in1=gate[:, 1], op=ALU.mult).then_inc(step, 1)
            dve.wait_ge(gates_on, 4)
            dve.tensor_tensor(out=hid[:], in0=gate[:, 2], in1=cell_t[:], op=ALU.mult).then_inc(step, 1)
            dve.wait_ge(step, 5)
            wide = hid[:].rearrange("p (c o) -> p c o", o=1).to_broadcast([P, C, P])
            then(dve.tensor_copy(hid_h[:], wide))
            dve.tensor_tensor(out=hid_l[:], in0=wide, in1=hid_h[:].bitcast(F32), op=ALU.subtract).then_inc(mlp_done, 1)
            for n, (a, h, l) in enumerate(((a1, a1h, a1l), (a2, a2h, a2l))):
                dve.wait_ge(relu_done, n + 1)
                then(dve.tensor_copy(h[:], a[:]))
                dve.tensor_tensor(out=l[:], in0=a[:], in1=h[:].bitcast(F32), op=ALU.subtract).then_inc(mlp_done, 1)
            dve.wait_ge(product, 4)
            then(dve.tensor_tensor(out=K.base[:], in0=small[:, 0:F], in1=K.b3[:], op=ALU.add))


def w3(w):
    return w[:, M3:M3 + C].rearrange("p b o -> p (b o)")


def rel_w(w, r, ic):
    return w[:, REL + (r * C + ic) * C:REL + (r * C + ic + 1) * C].rearrange("p b o -> p (b o)")


def edges0(nc, A, K, S):
    with ExitStack() as c:
        used = c.enter_context(stage_semaphores(nc))

        def sb(name, shape, dt=F32):
            return c.enter_context(nc.sbuf_tensor(name, shape, dt))

        def sem(name):
            used.append(nc.alloc_semaphore(name))
            return used[-1]

        attr = sb("attr", [P, 4, J, F])
        bases = sb("bases", [P, 4, J, F])
        dst_row = sb("dst_row", [P, 2, B], I32)
        edge = sb("edge", [P, 4, J, F])
        idx = sb("idx0", [P, 4, J], I32)
        e_h, e_l = sb("e_h", [P, 2, C, B], F32R), sb("e_l", [P, 2, C, B], F32R)
        msg = sb("msg", [P, 2, J, F])
        same = sb("same", [P, 2, J, P])
        cont = sb("cont", [P, 2, J, P])
        carry = sb("carry", [P, 2, F])
        pT = [c.enter_context(nc.psum_tensor(f"pT{n}", [P, C, B], F32)) for n in range(2)]
        pU = c.enter_context(nc.psum_tensor("pU", [P, J, F], F32))
        pS = [c.enter_context(nc.psum_tensor(f"pS{n}", [P, 512], F32)) for n in range(2)]

        attr_full, bases_full, got_full = (
            [sem(f"e0_{n}{q}") for q in range(4)] for n in ("attr_full", "bases_full", "got_full"))
        row_full = [sem(f"e0_row_full{b}") for b in range(2)]
        idx_ready, past, added, turned, hi_done, lo_done = (sem("e0_idx_ready"), sem("e0_past"), sem("e0_added"),
                                                            sem("e0_turned"), sem("e0_hi"), sem("e0_lo"))
        u_done, gelu_done, msg_done, masks, tile_sum, tile_out = (
            sem("e0_u"), sem("e0_gelu"), sem("e0_msg"), sem("e0_masks"), sem("e0_tile_sum"), sem("e0_tile_out"))
        kept = sem("e0_kept")
        first_sum, tail_attr, tail_bases = sem("e0_first_sum"), sem("e0_tail_attr"), sem("e0_tail_bases")
        block = c.enter_context(nc.Block())
        LAST = S.EB - 1
        real = batch_of(S.EB)

        def is_last(k):
            return isinstance(k, int) and k == LAST

        def tiles(k):
            return S.tail_tiles if is_last(k) else J

        @block.sync
        def _(sp):
            dst_v = A["dst"][0:LAST * B].rearrange("(b e) -> b e", e=B)

            def load_rows(k, q, buffer, source, full, tail):
                if is_last(k):
                    t, lo = S.tail_tiles - 1, LAST * B
                    sp.dma_start(buffer[0:S.tail_rows, q, t], source[lo + t * P:S.E, :]).then_inc(tail, 16)
                    sp.dma_start(buffer[:, q, 0:t], source[lo:lo + t * P, :].rearrange("(j p) f -> p j f", p=P)).then_inc(full[q], 16)
                else:
                    rows = source[0:LAST * B, :].rearrange("(b j p) f -> b p j f", j=J, p=P)
                    sp.dma_start(buffer[:, q], rows[bass.ds(k, 1)].rearrange("o p j f -> (o p) j f")).then_inc(full[q], 16)

            def load_attr(k, q):
                load_rows(k, q, attr, A["attr"], attr_full, tail_attr)

            def load_bases(k, q):
                load_rows(k, q, bases, A["bases"], bases_full, tail_bases)

            def load_dst(k, b):
                if is_last(k):
                    nodes = A["dst"][LAST * B:S.E].rearrange("(a e) -> a e", a=1)
                    sp.dma_start(dst_row[:, b, 0:S.tail_edges], nodes.to_broadcast([P, S.tail_edges])).then_inc(row_full[b], 16)
                else:
                    sp.dma_start(dst_row[:, b], dst_v[bass.ds(k, 1)].to_broadcast([P, B])).then_inc(row_full[b], 16)

            def at(k):
                return k if isinstance(k, int) else sp.snap(k)

            for q in range(4):
                load_attr(q, q)
                load_bases(q, q)
                if q < 2:
                    load_dst(q, q)

            def step(k, q):
                attr_next, bases_next, dst_next = at(k + 7), at(k + 4), at(k + 2)
                if real(k + 7) and real(k + 3):
                    sp.wait_ge(added, k + 4)
                    load_attr(attr_next, (q + 3) % 4)
                if real(k + 4) and real(k):
                    sp.wait_ge(msg_done, k + 1)
                    load_bases(bases_next, q)
                if real(k + 2) and real(k):
                    sp.wait_ge(masks, k + 1)
                    load_dst(dst_next, q % 2)

            batch_steps(sp, S.EB, step, 8)

        @block.gpsimd
        def _(pool):
            bound = pool.to_reg(S.N - 1)

            def step(k, q):
                if not real(k + 6):
                    return
                b = (q + 2) % 4
                if real(k + 2):
                    pool.wait_ge(turned, k + 3)
                    pool.sem_inc(past, 1)
                pool.tensor_copy(idx[:, b], K.src[:, bass.ds((k + 6) * J, J)]).then_inc(idx_ready, 1)
                pool.wait_ge(idx_ready, k + 7)
                pool.sem_inc(past, 1)
                for j in range(J):
                    pool.indirect_dma_start(
                        out=edge[:, b, j], out_offset=None, in_=A["x"],
                        in_offset=bass.IndirectOffsetOnAxis(ap=idx[:, b, j:j + 1], axis=0),
                        bounds_check=bound, oob_is_err=False).then_inc(got_full[b], 16)

            for k in (-6, -5):
                step(k, k % 4)
            batch_steps(pool, S.EB, step, 7)

        @block.tensor
        def _(pe):
            def turn(k, b, q):
                pe.wait_ge(added, k + 1)
                wait(pe, lo_done, k - 1)
                for cc in range(C):
                    for j in range(J):
                        last = pe.transpose(pT[b][:, cc, j * P:(j + 1) * P], edge[:, q, j, cc * P:(cc + 1) * P], K.ident[:])
                last.then_inc(turned, 1)

            def dense(k, b, j):
                if j == 0:
                    pe.wait_ge(lo_done, k + 1)
                    wait(pe, gelu_done, k)
                pe.matmul(pU[:, j], K.ones[0:4, :], K.rows[:, 0], start=True, stop=False)
                for cc in range(C):
                    cols = slice(j * P, (j + 1) * P)
                    last = mm3(pe, pU[:, j], (e_h[:, b, cc, cols], e_l[:, b, cc, cols]),
                               (K.w0_h[:, 0, cc], K.w0_l[:, 0, cc]), False, cc == C - 1)
                if j == J - 1:
                    last.then_inc(u_done, 1)

            def segments(k, b, j):
                first = isinstance(k, int) and k == 0
                if j == 0:
                    pe.wait_ge(msg_done, k + 1)
                    pe.wait_ge(masks, k + 1)
                if not (first and j < 2):
                    pe.wait_ge(tile_out, J * k + j - 1)
                pe.matmul(pS[j % 2][:, 0:F], same[:, b, j], msg[:, b, j], start=True, stop=False)
                if first and j == 0:
                    pe.wait_ge(first_sum, 1)
                else:
                    pe.wait_ge(tile_out, J * k + j)
                pe.matmul(pS[j % 2][:, 0:F], cont[96:128, b, j], carry[96:128, 1 - j % 2],
                          start=False, stop=True).then_inc(tile_sum, 1)

            def step(k, q):
                b = q % 2
                if real(k + 2):
                    turn(k + 2, b, (q + 2) % 4)
                for j in range(J):
                    if real(k - 1) and j < tiles(k - 1):
                        segments(k - 1, 1 - b, j)
                    if real(k + 1):
                        dense(k + 1, 1 - b, j)

            batch_steps(pe, S.EB, step, 3)

        @block.scalar
        def _(act):
            def hi(k, b):
                act.wait_ge(turned, k + 1)
                wait(act, u_done, k - 1)
                act.activation(e_h[:, b], pT[b][:], ACT.Copy).then_inc(hi_done, 1)

            def gelus(k, b):
                act.wait_ge(u_done, k + 1)
                wait(act, tile_out, J * (k - 1))
                act.activation(msg[:, b], pU[:], ACT.Gelu).then_inc(gelu_done, 1)

            def out(k, q, j):
                act.wait_ge(tile_sum, J * k + j + 1)
                act.activation(carry[:, j % 2], pS[j % 2][:, 0:F], ACT.Copy).then_inc(tile_out, 1)
                at = K.sums[:, bass.ds(k * J + j, 1)].rearrange("p o f -> p (o f)")
                act.wait_ge(tile_out, J * k + j + 1)
                act.activation(at, carry[:, j % 2], ACT.Copy).then_inc(kept, 1)

            def step(k, q):
                if real(k):
                    row = k * S.piece if isinstance(k, int) else act.snap(k * S.piece)
                    act.dma_start(A["y"][bass.ds(row, S.piece), :], A["x"][bass.ds(row, S.piece), :]).then_inc(K.copied, 16)
                    gelus(k, q % 2)
                if real(k + 2):
                    hi(k + 2, q % 2)
                if real(k - 1):
                    for j in range(tiles(k - 1)):
                        out(k - 1, (q - 1) % 4, j)

            batch_steps(act, S.EB, step, 3)

        @block.vector
        def _(dve):
            def add(k, q):
                dve.wait_ge(attr_full[q], 4 * (k - q) + 16)
                if is_last(k):
                    dve.wait_ge(tail_attr, 16)
                dve.wait_ge(got_full[q], 16 * (k - q) + 16 * J)
                dve.tensor_tensor(out=edge[:, q], in0=edge[:, q], in1=attr[:, q], op=ALU.add).then_inc(added, 1)

            def message(k, q):
                b = q % 2
                dve.wait_ge(bases_full[q], 4 * (k - q) + 16)
                if is_last(k):
                    dve.wait_ge(tail_bases, 16)
                dve.wait_ge(gelu_done, k + 1)
                dve.tensor_tensor(out=msg[:, b], in0=msg[:, b], in1=bases[:, q], op=ALU.mult).then_inc(msg_done, 1)

            def lo(k, b):
                dve.wait_ge(hi_done, k + 1)
                dve.tensor_tensor(out=e_l[:, b], in0=pT[b][:], in1=e_h[:, b].bitcast(F32), op=ALU.subtract).then_inc(lo_done, 1)

            def mask(k, b):
                dve.wait_ge(row_full[b], 8 * (k - b) + 16)
                wait(dve, tile_out, J * (k - 1))
                rows = dst_row[:, b].rearrange("p (j e) -> p j e", j=J)
                for out, key in ((same, K.dst_f), (cont, K.prev_row)):
                    cols = key[:, bass.ds(k * J, J)].rearrange("p (j o) -> p j o", o=1).to_broadcast([P, J, P])
                    last = dve.tensor_tensor(out=out[:, b], in0=rows, in1=cols, op=ALU.is_equal)
                last.then_inc(masks, 1)

            def step(k, q):
                if real(k + 3):
                    add(k + 3, (q + 3) % 4)
                if real(k):
                    message(k, q)
                if real(k + 2):
                    lo(k + 2, q % 2)
                if real(k):
                    mask(k, q % 2)

            dve.memset(carry[:, 1], 0.0).then_inc(first_sum, 1)
            batch_steps(dve, S.EB, step, 4)


def scatter0(nc, A, K, S):
    with ExitStack() as c:
        used = c.enter_context(stage_semaphores(nc))

        def sem(name):
            used.append(nc.alloc_semaphore(name))
            return used[-1]

        rows = c.enter_context(nc.sbuf_tensor("sc_rows", [P, 4, 2, F], F32))
        idx = c.enter_context(nc.sbuf_tensor("sc_idx", [P, 4, 2], I32))
        done = [sem(f"sc_done{q}") for q in range(4)]
        idx_ready, past, full, dve_past = sem("sc_idx_ready"), sem("sc_past"), sem("sc_full"), sem("sc_dve_past")
        halved = sem("sc_halved")
        block = c.enter_context(nc.Block())
        pairs = S.ET // 2
        real = batch_of(pairs)

        @block.scalar
        def _(act):
            def step(s, q):
                if real(s):
                    act.wait_ge(full, s + 1)
                    act.activation(K.sums[:, bass.ds(2 * s, 2)], rows[:, q], ACT.Copy, scale=-0.5).then_inc(halved, 1)

            batch_steps(act, pairs, step, 4)

        @block.vector
        def _(dve):
            def step(s, q):
                if not real(s):
                    return
                if not (isinstance(s, int) and s < 4):
                    dve.wait_ge(done[q], 8 * (s - q))
                    dve.wait_ge(halved, s - 3)
                    dve.sem_inc(dve_past, 1)
                dve.tensor_copy(rows[:, q], K.sums[:, bass.ds(2 * s, 2)]).then_inc(full, 1)

            batch_steps(dve, pairs, step, 4)

        @block.gpsimd
        def _(pool):
            bound = pool.to_reg(S.N - 1)
            pool.wait_ge(K.copied, 16 * (S.EB + 1))

            def step(s, q):
                if not real(s):
                    return
                if not (isinstance(s, int) and s < 4):
                    pool.wait_ge(done[q], 8 * (s - q))
                    pool.sem_inc(past, 1)
                pool.tensor_copy(idx[:, q], K.target[:, bass.ds(s * 2, 2)]).then_inc(idx_ready, 1)
                pool.wait_ge(full, s + 1)
                pool.sem_inc(past, 1)
                pool.wait_ge(idx_ready, s + 1)
                pool.sem_inc(past, 1)
                for j in range(2):
                    pool.indirect_dma_start(
                        out=A["y"], out_offset=bass.IndirectOffsetOnAxis(ap=idx[:, q, j:j + 1], axis=0),
                        in_=rows[:, q, j], in_offset=None, compute_op=ALU.add,
                        bounds_check=bound, oob_is_err=False).then_inc(done[q], 16)

            batch_steps(pool, pairs, step, 4)
            for q in range(4):
                pool.wait_ge(done[q], 32 * ((pairs - 1 - q) // 4 + 1))


def node_rows(t, S):
    full = t[0:(S.NB - 1) * B, :].rearrange("(n p j) f -> n p (j f)", p=P, j=J)

    def at(k):
        if isinstance(k, int) and k == S.NB - 1:
            return t[S.last_node:S.N, :].rearrange("(p j) f -> p (j f)", j=J)
        return full[bass.ds(k, 1)].rearrange("o p f -> (o p) f")
    return at


def bn_stats_of(dve, out, psum, tail, S):
    if tail:
        psum = psum.rearrange("p (j q) -> p j q", j=J)[:, :, S.dup:P]
    return dve.bn_stats(out, psum)


def bn_coefficients(sem, sb, K, which, stats, coef, name):
    mv, var, rstd, tmp = (sb(f"{name}_mv", [P, C, 2]), sb(f"{name}_var", [P, C]), sb(f"{name}_rstd", [P, C]),
                          sb(f"{name}_tmp", [P, 2, C]))
    step, var_ready, rstd_ready, ready = (sem(f"{name}_step"), sem(f"{name}_var_ready"), sem(f"{name}_rstd_ready"),
                                          sem(f"{name}_ready"))
    b, g, be = (K.bn[:, 3 * which + n] for n in range(3))

    def on_vector(dve):
        for cc in range(C):
            last = dve.bn_aggr(mv[:, cc], stats[:, cc].rearrange("p n s -> p (n s)"))
        last.then_inc(step, 1)
        dve.wait_ge(step, 1)
        dve.tensor_scalar(out=var[:], in0=mv[:, :, 1], scalar1=EPS, scalar2=None, op0=ALU.add).then_inc(var_ready, 1)
        dve.tensor_tensor(out=tmp[:, 0], in0=mv[:, :, 0], in1=b, op=ALU.add).then_inc(step, 1)
        dve.wait_ge(step, 2)
        dve.tensor_tensor(out=tmp[:, 1], in0=b, in1=tmp[:, 0], op=ALU.subtract)
        dve.wait_ge(rstd_ready, 1)
        dve.tensor_tensor(out=coef[:, 0], in0=g, in1=rstd[:], op=ALU.mult).then_inc(step, 1)
        dve.wait_ge(step, 3)
        dve.tensor_tensor(out=tmp[:, 0], in0=tmp[:, 1], in1=coef[:, 0], op=ALU.mult).then_inc(step, 1)
        dve.wait_ge(step, 4)
        dve.tensor_tensor(out=coef[:, 1], in0=tmp[:, 0], in1=be, op=ALU.add).then_inc(ready, 1)

    def on_pool(pool):
        pool.wait_ge(var_ready, 1)
        pool.tensor_tensor(out=rstd[:], in0=var[:], in1=K.minus_half[:, 0:C], op=ALU.pow).then_inc(rstd_ready, 1)

    return ready, on_vector, on_pool


def dense1(nc, A, K, S):
    with ExitStack() as c:
        used = c.enter_context(stage_semaphores(nc))

        def sb(name, shape, dt=F32):
            return c.enter_context(nc.sbuf_tensor(name, shape, dt))

        def sem(name):
            used.append(nc.alloc_semaphore(name))
            return used[-1]

        y = sb("d1_y", [P, 4, J * F])
        y_h, y_l = sb("d1_y_h", [P, 2, C, B], F32R), sb("d1_y_l", [P, 2, C, B], F32R)
        h = sb("d1_h", [P, 4, C * B])
        pT = [c.enter_context(nc.psum_tensor(f"d1_pT{n}", [P, C, B], F32)) for n in range(2)]
        pH = [c.enter_context(nc.psum_tensor(f"d1_pH{n}", [P, C, B], F32)) for n in range(2)]
        full, stored = [sem(f"d1_full{n}") for n in range(4)], [sem(f"d1_stored{n}") for n in range(4)]
        turned, hi_done, lo_done, product, stats_done, h_done, past = (
            sem("d1_turned"), sem("d1_hi"), sem("d1_lo"), sem("d1_product"), sem("d1_stats"), sem("d1_h_done"),
            sem("d1_past"))
        block = c.enter_context(nc.Block())
        loops = (S.NB - 2) // 4
        real = batch_of(S.NB)

        @block.sync
        def _(sp):
            rows = node_rows(A["y"], S)
            for q in range(4):
                sp.dma_start(y[:, q], rows(q)).then_inc(full[q], 16)

            def step(k, q):
                y_next, h_now = (k + 5, k - 1) if isinstance(k, int) else (sp.snap(k + 5), sp.snap(k - 1))
                if real(k + 5) and real(k + 1):
                    sp.wait_ge(turned, k + 2)
                    sp.dma_start(y[:, (q + 1) % 4], rows(y_next)).then_inc(full[(q + 1) % 4], 16)
                if real(k - 1):
                    b = (q - 1) % 4
                    sp.wait_ge(h_done, k + 2)
                    sp.dma_start(A["h1"][bass.ds(h_now, 1)].rearrange("o p f -> (o p) f"), h[:, b]).then_inc(stored[b], 16)

            batch_steps(sp, S.NB, step, 6)
            for q in range(4):
                sp.wait_ge(stored[q], 16 * ((S.NB - 1 - q) // 4 + 1))

        @block.tensor
        def _(pe):
            pe.sem_inc(product, 1)

            def turn(k, q):
                b = q % 2
                pe.wait_ge(full[q], 4 * (k - q) + 16)
                wait(pe, lo_done, k - 1)
                for cc in range(C):
                    for j in range(J):
                        at = j * F + cc * P
                        last = pe.transpose(pT[b][:, cc, j * P:(j + 1) * P], y[:, q, at:at + P], K.ident[:])
                last.then_inc(turned, 1)

            def multiply(k, q):
                b = q % 2
                pe.wait_ge(lo_done, k + 1)
                pe.wait_ge(h_done, k + 1)
                for oc in range(C):
                    for ic in range(C):
                        cols = slice(oc * P, (oc + 1) * P)
                        last = mm3(pe, pH[b][:, oc], (K.w0_h[:, 1, ic, cols], K.w0_l[:, 1, ic, cols]),
                                   (y_h[:, b, ic], y_l[:, b, ic]), ic == 0, ic == C - 1)
                last.then_inc(product, 1)

            turn(0, 0)
            with pe.Fori(0, loops) as i:
                for k, q in quarters(i):
                    turn(k + 1, q + 1 if q < 3 else 0)
                    multiply(k, q)
            k = S.NB - 2
            turn(k + 1, 1)
            multiply(k, 0)
            multiply(k + 1, 1)

        @block.scalar
        def _(act):
            act.sem_inc(h_done, 2)

            def hi(k, b):
                act.wait_ge(turned, k + 1)
                wait(act, product, k)
                act.activation(y_h[:, b], pT[b][:], ACT.Copy).then_inc(hi_done, 1)

            def out(k, q):
                act.wait_ge(stats_done, k + 1)
                wait(act, stored[q], 4 * (k - q))
                act.activation(h[:, q].rearrange("p (c n) -> p c n", c=C), pH[q % 2][:], ACT.Copy).then_inc(h_done, 1)

            hi(0, 0)
            hi(1, 1)
            for k in (1, 2, 3):
                hi(k + 1, (k + 1) % 2)
                out(k - 1, k - 1)
            with act.Fori(1, loops) as i:
                for k, q in quarters(i):
                    hi(k + 1, (q + 1) % 2)
                    out(k - 1, (q - 1) % 4)
            hi(S.NB - 1, 1)
            out(S.NB - 3, 3)
            out(S.NB - 2, 0)
            out(S.NB - 1, 1)

        @block.vector
        def _(dve):
            def lo(k, b):
                dve.wait_ge(hi_done, k + 1)
                dve.tensor_tensor(out=y_l[:, b], in0=pT[b][:], in1=y_h[:, b].bitcast(F32), op=ALU.subtract).then_inc(lo_done, 1)

            def stats(k, b, tail=False):
                dve.wait_ge(product, k + 2)
                dve.sem_inc(past, 1)
                for cc in range(C):
                    out = K.stats[:, cc, bass.ds(k, 1)].rearrange("p o s -> p (o s)")
                    last = bn_stats_of(dve, out, pH[b][:, cc], tail, S)
                last.then_inc(stats_done, 1)

            lo(0, 0)
            lo(1, 1)
            for k in (1, 2, 3):
                stats(k - 1, (k - 1) % 2)
                lo(k + 1, (k + 1) % 2)
            with dve.Fori(1, loops) as i:
                for k, q in quarters(i):
                    stats(k - 1, (q - 1) % 2)
                    lo(k + 1, (q + 1) % 2)
            stats(S.NB - 3, 1)
            lo(S.NB - 1, 1)
            stats(S.NB - 2, 0)
            stats(S.NB - 1, 1, True)


def dense2(nc, A, K, S):
    with ExitStack() as c:
        used = c.enter_context(stage_semaphores(nc))

        def sb(name, shape, dt=F32):
            return c.enter_context(nc.sbuf_tensor(name, shape, dt))

        def sem(name):
            used.append(nc.alloc_semaphore(name))
            return used[-1]

        h1 = sb("d2_h1", [P, 4, C * B])
        r = sb("d2_r", [P, 2, C, B])
        r_h, r_l = sb("d2_r_h", [P, 2, C, B], F32R), sb("d2_r_l", [P, 2, C, B], F32R)
        h = sb("d2_h", [P, 4, C * B])
        half = sb("d2_half", [P, 4, F])
        idx = sb("d2_idx", [P, 4], I32)
        pH = [c.enter_context(nc.psum_tensor(f"d2_pH{n}", [P, C, B], F32)) for n in range(2)]
        full, stored = [sem(f"d2_full{n}") for n in range(4)], [sem(f"d2_stored{n}") for n in range(4)]
        added = [sem(f"d2_added{n}") for n in range(4)]
        relu_done, hi_done, lo_done, product, stats_done, h_done, dve_past, pool_past, halved = (
            sem("d2_relu"), sem("d2_hi"), sem("d2_lo"), sem("d2_product"), sem("d2_stats"), sem("d2_h_done"),
            sem("d2_dve_past"), sem("d2_pool_past"), sem("d2_halved"))
        coef = sb("d2_coef", [P, 2, C])
        coef_ready, coef_vector, coef_pool = bn_coefficients(sem, sb, K, 0, K.stats, coef, "bn1")
        _, coef2_vector, coef2_pool = bn_coefficients(sem, sb, K, 1, K.stats2, K.coef2, "bn2")
        block = c.enter_context(nc.Block())
        loops = (S.NB - 2) // 4
        real = batch_of(S.NB)

        @block.sync
        def _(sp):
            def load_h1(k, q):
                sp.dma_start(h1[:, q], A["h1"][bass.ds(k, 1)].rearrange("o p f -> (o p) f")).then_inc(full[q], 16)

            for q in range(4):
                load_h1(q, q)

            def step(k, q):
                h1_next, h_now = (k + 6, k - 1) if isinstance(k, int) else (sp.snap(k + 6), sp.snap(k - 1))
                if real(k + 6) and real(k + 2):
                    sp.wait_ge(relu_done, k + 3)
                    load_h1(h1_next, (q + 2) % 4)
                if real(k - 1):
                    b = (q - 1) % 4
                    sp.wait_ge(h_done, k + 2)
                    sp.dma_start(A["h2"][bass.ds(h_now, 1)].rearrange("o p f -> (o p) f"), h[:, b]).then_inc(stored[b], 16)

            batch_steps(sp, S.NB, step, 7)
            for q in range(4):
                sp.wait_ge(stored[q], 16 * ((S.NB - 1 - q) // 4 + 1))

        @block.tensor
        def _(pe):
            pe.sem_inc(product, 1)

            def multiply(k, b):
                pe.wait_ge(lo_done, k + 1)
                pe.wait_ge(h_done, k + 1)
                for oc in range(C):
                    for ic in range(C):
                        cols = slice(oc * P, (oc + 1) * P)
                        last = mm3(pe, pH[b][:, oc], (K.w0_h[:, 2, ic, cols], K.w0_l[:, 2, ic, cols]),
                                   (r_h[:, b, ic], r_l[:, b, ic]), ic == 0, ic == C - 1)
                last.then_inc(product, 1)

            with pe.Fori(0, S.NB // 2) as i:
                for k, b in halves(i):
                    multiply(k, b)

        @block.scalar
        def _(act):
            act.sem_inc(h_done, 2)
            act.wait_ge(coef_ready, 1)

            def relu(k, q):
                act.wait_ge(full[q], 4 * (k - q) + 16)
                wait(act, lo_done, k - 1)
                for cc in range(C):
                    last = act.activation(r[:, q % 2, cc], h1[:, q, cc * B:(cc + 1) * B], ACT.Relu,
                                          bias=coef[:, 1, cc:cc + 1], scale=coef[:, 0, cc:cc + 1])
                last.then_inc(relu_done, 1)

            def out(k, q):
                act.wait_ge(stats_done, k + 1)
                wait(act, stored[q], 4 * (k - q))
                act.activation(h[:, q].rearrange("p (c n) -> p c n", c=C), pH[q % 2][:], ACT.Copy).then_inc(h_done, 1)

            relu(0, 0)
            relu(1, 1)
            relu(2, 2)
            for k in (1, 2, 3):
                relu(k + 2, (k + 2) % 4)
                out(k - 1, k - 1)
            with act.Fori(1, loops) as i:
                for k, q in quarters(i):
                    relu(k + 2, (q + 2) % 4)
                    out(k - 1, (q - 1) % 4)
            out(S.NB - 3, 3)
            out(S.NB - 2, 0)
            out(S.NB - 1, 1)

        @block.gpsimd
        def _(pool):
            coef_pool(pool)
            bound = pool.to_reg(S.N - 1)

            def subtract_half(k, q):
                if not (isinstance(k, int) and k < 4):
                    pool.wait_ge(added[q], 4 * (k - q))
                    pool.sem_inc(pool_past, 1)
                pool.tensor_copy(idx[:, q:q + 1], K.target[:, bass.ds(k, 1)])
                pool.tensor_copy(half[:, q], K.sums[:, bass.ds(k, 1)].rearrange("p o f -> p (o f)")).then_inc(halved, 1)
                pool.wait_ge(halved, k + 1)
                pool.sem_inc(pool_past, 1)
                pool.indirect_dma_start(
                    out=A["y"], out_offset=bass.IndirectOffsetOnAxis(ap=idx[:, q:q + 1], axis=0),
                    in_=half[:, q], in_offset=None, compute_op=ALU.add,
                    bounds_check=bound, oob_is_err=False).then_inc(added[q], 16)

            for k, q in quarters(0):
                subtract_half(k, q)
            with pool.Fori(1, loops) as i:
                for k, q in quarters(i):
                    subtract_half(k, q)
            subtract_half(S.NB - 2, 0)
            subtract_half(S.NB - 1, 1)
            coef2_pool(pool)
            for q in range(4):
                pool.wait_ge(added[q], 16 * ((S.NB - 1 - q) // 4 + 1))

        @block.vector
        def _(dve):
            coef_vector(dve)

            def parts(k, b):
                dve.wait_ge(relu_done, k + 1)
                wait(dve, product, k)
                dve.sem_inc(dve_past, 1)
                dve.tensor_copy(r_h[:, b], r[:, b]).then_inc(hi_done, 1)
                dve.wait_ge(hi_done, k + 1)
                dve.tensor_tensor(out=r_l[:, b], in0=r[:, b], in1=r_h[:, b].bitcast(F32), op=ALU.subtract).then_inc(lo_done, 1)

            def stats(k, b, tail=False):
                dve.wait_ge(product, k + 2)
                dve.sem_inc(dve_past, 1)
                for cc in range(C):
                    out = K.stats2[:, cc, bass.ds(k, 1)].rearrange("p o s -> p (o s)")
                    last = bn_stats_of(dve, out, pH[b][:, cc], tail, S)
                last.then_inc(stats_done, 1)

            parts(0, 0)
            parts(1, 1)
            for k in (1, 2, 3):
                stats(k - 1, (k - 1) % 2)
                parts(k + 1, (k + 1) % 2)
            with dve.Fori(1, loops) as i:
                for k, q in quarters(i):
                    stats(k - 1, (q - 1) % 2)
                    parts(k + 1, (q + 1) % 2)
            stats(S.NB - 3, 1)
            parts(S.NB - 1, 1)
            stats(S.NB - 2, 0)
            stats(S.NB - 1, 1, True)
            dve.wait_ge(stats_done, S.NB)
            dve.sem_inc(dve_past, 1)
            coef2_vector(dve)


def row_stats(dve, stats, rows, done):
    for j in range(J):
        last = dve.bn_stats(stats[:, j], rows[:, j])
    last.then_inc(done, 1)


def row_moments(dve, mv, stats, past, done):
    dve.sem_inc(past, 1)
    for j in range(J):
        last = dve.bn_aggr(mv[:, j], stats[:, j])
    last.then_inc(done, 1)


def dense3(nc, A, K, S):
    with ExitStack() as c:
        used = c.enter_context(stage_semaphores(nc))

        def sb(name, shape, dt=F32):
            return c.enter_context(nc.sbuf_tensor(name, shape, dt))

        def sem(name):
            used.append(nc.alloc_semaphore(name))
            return used[-1]

        h2 = sb("d3_h2", [P, 4, C * B])
        y = sb("d3_y", [P, 4, J * F])
        r = sb("d3_r", [P, 2, C, B])
        s = sb("d3_s", [P, 4, J, F])
        x1 = sb("d3_x1", [P, 4, J, F])
        u = sb("d3_u", [P, 4, J, F])
        o = sb("d3_o", [P, 4, J, F])
        st1, st2 = sb("d3_st1", [P, 4, J, 6]), sb("d3_st2", [P, 4, J, 6])
        mv, v, rs = sb("d3_mv", [P, 4, 2 * J, 2]), sb("d3_v", [P, 4, 2 * J]), sb("d3_rs", [P, 4, 2 * J])
        nm, nb = sb("d3_nm", [P, 4, 2 * J]), sb("d3_nb", [P, 4, 2 * J])
        pN = [c.enter_context(nc.psum_tensor(f"d3_pN{n}", [P, J, F], F32)) for n in range(2)]
        h2_full, y_full = [sem(f"d3_h2_full{n}") for n in range(4)], [sem(f"d3_y_full{n}") for n in range(4)]
        x1_out, o_out = ([sem(f"d3_x1_out{n}") for n in range(4)],
                               [sem(f"d3_o_out{n}") for n in range(4)])
        relu_done, turned, s_done, st1_done, st2_done, x1_done, x1_rest, u_done, o_done = (
            sem("d3_relu"), sem("d3_turned"), sem("d3_s_done"), sem("d3_st1_done"), sem("d3_st2_done"),
            sem("d3_x1_done"), sem("d3_x1_rest"), sem("d3_u_done"), sem("d3_o_done"))
        mv_done, v_done, rs_done, nb_done, past, dve_past = (
            sem("d3_mv_done"), sem("d3_v_done"), sem("d3_rs_done"), sem("d3_nb_done"), sem("d3_past"), sem("d3_dve_past"))
        block = c.enter_context(nc.Block())
        real = batch_of(S.NB)

        on_vector = J // 2

        def both(k):
            return slice(0 if real(k + 3) else J, 2 * J if real(k) else J)

        @block.sync
        def _(sp):
            rows = node_rows(A["y"], S)
            x1_rows, out_rows = node_rows(A["x1"], S), node_rows(A["out"], S)

            def load_h2(k, q):
                sp.dma_start(h2[:, q], A["h2"][bass.ds(k, 1)].rearrange("o p f -> (o p) f")).then_inc(h2_full[q], 16)

            def load_y(k, q):
                sp.dma_start(y[:, q], rows(k)).then_inc(y_full[q], 16)

            def at(k):
                return k if isinstance(k, int) else sp.snap(k)

            def fresh(k):
                return slice(S.dup, P) if isinstance(k, int) and k == S.NB - 1 else slice(0, P)

            for q in range(4):
                load_h2(q, q)
                load_y(q, q)
            for name, w in (("wl_h", K.wl_h), ("wl_l", K.wl_l)):
                sp.dma_start(w[:].rearrange("p b o -> p (b o)").bitcast(F32), A[name]).then_inc(K.wl_full, 16)

            def step(k, q):
                h2_next, y_next, x1_now, o_now = at(k + 8), at(k + 7), at(k + 1), at(k - 1)
                if real(k + 8) and real(k + 4):
                    sp.wait_ge(relu_done, k + 5)
                    load_h2(h2_next, q)
                if real(k + 7) and real(k + 3):
                    sp.wait_ge(s_done, k + 4)
                    load_y(y_next, (q + 3) % 4)
                if real(k + 1):
                    sp.wait_ge(x1_done, k + 2)
                    sp.wait_ge(x1_rest, k + 2)
                    b, some = (q + 1) % 4, fresh(k + 1)
                    sp.dma_start(x1_rows(x1_now)[some], x1[some, b].rearrange("p j f -> p (j f)")).then_inc(x1_out[b], 16)
                if real(k - 1):
                    sp.wait_ge(o_done, k)
                    b, some = (q - 1) % 4, fresh(k - 1)
                    sp.dma_start(out_rows(o_now)[some], o[some, b].rearrange("p j f -> p (j f)")).then_inc(o_out[b], 16)

            batch_steps(sp, S.NB, step, 8)
            for q in range(4):
                sp.wait_ge(x1_out[q], 16 * ((S.NB - 1 - q) // 4 + 1))
                sp.wait_ge(o_out[q], 16 * ((S.NB - 1 - q) // 4 + 1))

        @block.tensor
        def _(pe):
            def turn(k, b):
                pe.wait_ge(relu_done, k + 1)
                wait(pe, s_done, k - 1)
                for j in range(J):
                    for cc in range(C):
                        last = pe.transpose(pN[b][:, j, cc * P:(cc + 1) * P], r[:, b, cc, j * P:(j + 1) * P], K.ident[:])
                last.then_inc(turned, 1)

            turn(0, 0)
            turn(1, 1)
            with pe.Fori(0, (S.NB - 2) // 2) as i:
                for k, b in halves(i):
                    turn(k + 2, b)

        @block.scalar
        def _(act):
            def relu(k, q):
                act.wait_ge(h2_full[q], 4 * (k - q) + 16)
                wait(act, turned, k - 1)
                for cc in range(C):
                    last = act.activation(r[:, q % 2, cc], h2[:, q, cc * B:(cc + 1) * B], ACT.Relu,
                                          bias=K.coef2[:, 1, cc:cc + 1], scale=K.coef2[:, 0, cc:cc + 1])
                last.then_inc(relu_done, 1)

            def normed(k, q):
                act.wait_ge(nb_done, k + 4)
                wait(act, o_out[q], 4 * (k - q))
                for j in range(J):
                    last = act.activation(o[:, q, j], u[:, q, j], ACT.Identity, bias=nb[:, q, J + j:J + j + 1],
                                          scale=rs[:, q, J + j:J + j + 1])
                last.then_inc(o_done, 1)

            def x1_part(k, q):
                act.wait_ge(nb_done, k + 1)
                wait(act, x1_out[q], 4 * (k - q))
                before = (q - 3) % 4
                for j in range(on_vector, J):
                    last = act.activation(x1[:, q, j], s[:, q, j], ACT.Identity, bias=nb[:, before, j:j + 1],
                                          scale=rs[:, before, j:j + 1])
                last.then_inc(x1_rest, 1)

            def step(k, q):
                if real(k + 1):
                    x1_part(k + 1, (q + 1) % 4)
                if real(k + 4):
                    relu(k + 4, q)
                if real(k - 1):
                    normed(k - 1, (q - 1) % 4)

            batch_steps(act, S.NB, step, 4)

        @block.gpsimd
        def _(pool):
            def deviations(k, q):
                now = both(k)
                pool.wait_ge(mv_done, k + 4)
                pool.sem_inc(past, 1)
                pool.tensor_scalar(out=nm[:, q, now], in0=mv[:, q, now, 0], scalar1=-1.0, scalar2=None, op0=ALU.mult)
                pool.tensor_scalar(out=v[:, q, now], in0=mv[:, q, now, 1], scalar1=EPS, scalar2=None, op0=ALU.add).then_inc(v_done, 1)
                pool.wait_ge(v_done, k + 4)
                pool.tensor_tensor(out=rs[:, q, now], in0=v[:, q, now], in1=K.minus_half[:, now], op=ALU.pow).then_inc(rs_done, 1)
                pool.wait_ge(rs_done, k + 4)
                pool.tensor_tensor(out=nb[:, q, now], in0=nm[:, q, now], in1=rs[:, q, now], op=ALU.mult).then_inc(nb_done, 1)

            def add_base(k, q):
                pool.wait_ge(x1_done, k + 1)
                pool.wait_ge(x1_rest, k + 1)
                wait(pool, o_done, k - 3)
                wide = K.base[:].rearrange("p (o f) -> p o f", o=1).to_broadcast([P, J, F])
                pool.tensor_tensor(out=u[:, q], in0=x1[:, q], in1=wide, op=ALU.add).then_inc(u_done, 1)

            def step(k, q):
                if real(k + 1):
                    add_base(k + 1, (q + 1) % 4)
                if real(k + 3) or real(k):
                    deviations(k, q)

            batch_steps(pool, S.NB, step, 4)

        @block.vector
        def _(dve):
            def add(k, q):
                dve.wait_ge(turned, k + 1)
                dve.wait_ge(y_full[q], 4 * (k - q) + 16)
                wait(dve, x1_done, k - 3)
                wait(dve, x1_rest, k - 3)
                dve.scalar_tensor_tensor(out=s[:, q], in0=y[:, q].rearrange("p (j f) -> p j f", j=J), scalar=2.0,
                                         in1=pN[q % 2][:], op0=ALU.mult, op1=ALU.add).then_inc(s_done, 1)

            def normed(k, q):
                dve.wait_ge(rs_done, k + 1)
                wait(dve, x1_out[q], 4 * (k - q))
                before = (q - 3) % 4
                for j in range(on_vector):
                    last = dve.tensor_scalar(out=x1[:, q, j], in0=s[:, q, j], scalar1=mv[:, before, j, 0:1],
                                             scalar2=rs[:, before, j:j + 1], op0=ALU.subtract, op1=ALU.mult)
                last.then_inc(x1_done, 1)

            def step(k, q):
                if real(k + 3):
                    add(k + 3, (q + 3) % 4)
                if real(k):
                    dve.wait_ge(u_done, k + 1)
                    row_stats(dve, st2[:, q], u[:, q], st2_done)
                if real(k + 1):
                    normed(k + 1, (q + 1) % 4)
                if real(k + 3):
                    dve.wait_ge(s_done, k + 4)
                    row_stats(dve, st1[:, q], s[:, (q + 3) % 4], st1_done)
                if real(k + 3) or real(k):
                    if real(k):
                        dve.wait_ge(st2_done, k + 1)
                    if real(k + 3):
                        dve.wait_ge(st1_done, k + 4)
                    dve.sem_inc(dve_past, 1)
                    for j in range(both(k).start, both(k).stop):
                        last = dve.bn_aggr(mv[:, q, j], st1[:, q, j] if j < J else st2[:, q, j - J])
                    last.then_inc(mv_done, 1)

            batch_steps(dve, S.NB, step, 4)


def edges1(nc, A, K, S):
    with ExitStack() as c:
        used = c.enter_context(stage_semaphores(nc))

        def sb(name, shape, dt=F32):
            return c.enter_context(nc.sbuf_tensor(name, shape, dt))

        def sem(name):
            used.append(nc.alloc_semaphore("e1_" + name))
            return used[-1]

        def part(name, shape):
            return sb(name + "_h", shape, F32R), sb(name + "_l", shape, F32R)

        xs, xd = sb("e1_xs", [P, 2, J, F]), sb("e1_xd", [P, 2, J, F])
        idx = sb("e1_idx", [P, 3, 2, J], I32)
        dst_row, rel_row = sb("e1_dst_row", [P, 2, B], I32), sb("e1_rel_row", [P, 2, B], I32)
        has_rel = sb("e1_has_rel", [P, 2, 2, B])
        has_k = sb("e1_has_k", [4, 2, B], F32R)
        same, cont = sb("e1_same", [P, 2, J, P]), sb("e1_cont", [P, 2, J, P])
        xt = part("e1_xt", [P, C, B])
        hid = [sb(f"e1_hid{r}", [P, C, B]) for r in range(2)]
        hidp = [part(f"e1_hidp{r}", [P, C, B]) for r in range(2)]
        msg = sb("e1_msg", [P, J, F])
        agg = sb("e1_agg", [P, C, B])
        aggp = part("e1_aggp", [P, C, B])
        gate = [sb(f"e1_gate{g}", [P, C, B]) for g in range(GATES)]
        cell, cell_t, hn = sb("e1_cell", [P, C, B]), sb("e1_cell_t", [P, C, B]), sb("e1_hn", [P, C, B])
        hnp = part("e1_hnp", [P, C, B])
        m1, m2 = sb("e1_m1", [P, B]), sb("e1_m2", [P, B])
        m1p, m2p = part("e1_m1p", [P, B]), part("e1_m2p", [P, B])
        u = sb("e1_u", [P, J, F])
        st, mv = sb("e1_st", [P, J, 6]), sb("e1_mv", [P, J, 2])
        v, rs = sb("e1_v", [P, J]), sb("e1_rs", [P, J])
        o = sb("e1_o", [P, 2, J, F])
        pX = c.enter_context(nc.psum_tensor("pX", [P, C, B], F32))
        pR = c.enter_context(nc.psum_tensor("pR", [P, C, B], F32))
        pG = c.enter_context(nc.psum_tensor("pG", [P, C, B], F32))
        pM = c.enter_context(nc.psum_tensor("pM", [P, J, F], F32))

        rows_full, xs_full, xd_full, o_out = ([sem(f"{n}{b}") for b in range(2)] for n in
                                              ("rows_full", "xs_full", "xd_full", "o_out"))
        idx_src, idx_dst, idx_out, past, dve_past, agg_clear = (
            sem(n) for n in ("idx_src", "idx_dst", "idx_out", "past", "dve_past", "agg_clear"))
        masked, turned, xt_hi, xt_lo = (sem(n) for n in ("masked", "turned", "xt_hi", "xt_lo"))
        rel_done, relu_done, mult_done, hid_hi, hid_lo = (sem(n) for n in
                                                          ("rel_done", "relu_done", "mult_done", "hid_hi", "hid_lo"))
        m_done, msg_done, sum_done, carried, agg_hi, agg_lo = (
            sem(n) for n in ("m_done", "msg_done", "sum_done", "carried", "agg_hi", "agg_lo"))
        gate_done, gate_on, cell_done, cell_on, hn_done, hn_hi, hn_lo = (
            sem(n) for n in ("gate_done", "gate_on", "cell_done", "cell_on", "hn_done", "hn_hi", "hn_lo"))
        m1_done, m1_on, m1_hi, m1_lo, m2_done, m2_on, m2_hi, m2_lo = (
            sem(n) for n in ("m1_done", "m1_on", "m1_hi", "m1_lo", "m2_done", "m2_on", "m2_hi", "m2_lo"))
        y_done, biased, u_done, st_done, mv_done, v_done, rs_done, o_done = (
            sem(n) for n in ("y_done", "biased", "u_done", "st_done", "mv_done", "v_done", "rs_done", "o_done"))
        block = c.enter_context(nc.Block())
        EB = S.EB

        def real(k):
            return not isinstance(k, int) or 0 <= k < EB

        def steps(engine, step, ahead=2):
            for k in (-2, -1, 0):
                step(k, k % 2)
            loops = (EB - 1 - ahead) // 2
            with engine.Fori(0, loops) as i:
                step(2 * i + 1, 1)
                step(2 * i + 2, 0)
            for k in range(2 * loops + 1, EB + 1):
                step(k, k % 2)

        @block.sync
        def _(sp):
            full = (EB - 1) * B

            def load(k, b):
                at = k if isinstance(k, int) else sp.snap(k)
                wait(sp, masked, k - 1)
                for t, src in ((dst_row, "dst"), (rel_row, "rel")):
                    sp.dma_start(t[:, b], A[src][0:full].rearrange("(b e) -> b e", e=B)[bass.ds(at, 1)]
                                 .to_broadcast([P, B])).then_inc(rows_full[b], 16)

            load(0, 0)
            load(1, 1)
            with sp.Fori(1, (EB - 1) // 2) as i:
                for k, b in halves(i):
                    load(k, b)
            sp.wait_ge(masked, EB - 2)
            for t, src in ((dst_row, "dst"), (rel_row, "rel")):
                sp.dma_start(t[:, 0, 0:S.tail_edges], A[src][full:S.E].rearrange("(a e) -> a e", a=1)
                             .to_broadcast([P, S.tail_edges])).then_inc(rows_full[0], 16)

        @block.gpsimd
        def _(pool):
            last_node = pool.to_reg(S.N - 1)

            def fetch(b, into, which, full):
                for j in range(J):
                    pool.indirect_dma_start(
                        out=into[:, b, j], out_offset=None, in_=A["x1"],
                        in_offset=bass.IndirectOffsetOnAxis(ap=idx[:, which, b, j:j + 1], axis=0),
                        bounds_check=last_node, oob_is_err=False).then_inc(full[b], 16)

            def mult(k, b, r):
                pool.wait_ge(relu_done, C * (2 * k + r + 1))
                wide = has_rel[:, b, r].rearrange("p (o n) -> p o n", o=1).to_broadcast([P, C, B])
                pool.tensor_tensor(out=hid[r][:], in0=hid[r][:], in1=wide, op=ALU.mult).then_inc(mult_done, 1)

            def step(k, b):
                if real(k + 1):
                    pool.wait_ge(masked, k + 2)
                    pool.sem_inc(past, 1)
                    mult(k + 1, 1 - b, 0)
                if real(k + 1):
                    mult(k + 1, 1 - b, 1)
                if real(k):
                    pool.wait_ge(xd_full[b], 32 * (k - b) + 64)
                    pool.sem_inc(past, 1)
                    wide = K.b3[:].rearrange("p (o f) -> p o f", o=1).to_broadcast([P, J, F])
                    pool.tensor_tensor(out=xd[:, b], in0=xd[:, b], in1=wide, op=ALU.add).then_inc(biased, 1)
                if real(k + 1):
                    if not (isinstance(k, int) and k < 1):
                        pool.wait_ge(u_done, k)
                        pool.sem_inc(past, 1)
                    pool.tensor_copy(idx[:, 1, 1 - b], K.dst_gather[:, bass.ds((k + 1) * J, J)]).then_inc(idx_dst, 1)
                    pool.wait_ge(idx_dst, k + 2)
                    pool.sem_inc(past, 1)
                    fetch(1 - b, xd, 1, xd_full)
                if real(k - 1):
                    pool.wait_ge(mv_done, k)
                    pool.sem_inc(past, 1)
                    pool.tensor_scalar(out=v[:], in0=mv[:, :, 1], scalar1=EPS, scalar2=None, op0=ALU.add).then_inc(v_done, 1)
                    pool.wait_ge(v_done, k)
                    pool.tensor_tensor(out=rs[:], in0=v[:], in1=K.minus_half[:, 0:J], op=ALU.pow).then_inc(rs_done, 1)
                if real(k + 4):
                    pool.wait_ge(turned, k + 3)
                    pool.sem_inc(past, 1)
                    fetch_src(k + 4, b)
                if real(k - 1):
                    if not (isinstance(k, int) and k < 3):
                        pool.wait_ge(o_out[1 - b], (k - 1 - (1 - b)) * 32)
                        pool.sem_inc(past, 1)
                    pool.tensor_copy(idx[:, 2, 1 - b], K.target[:, bass.ds((k - 1) * J, J)]).then_inc(idx_out, 1)
                    pool.wait_ge(idx_out, k)
                    pool.sem_inc(past, 1)
                    pool.wait_ge(o_done, k)
                    pool.sem_inc(past, 1)
                    for j in range(J):
                        pool.indirect_dma_start(
                            out=A["out"], out_offset=bass.IndirectOffsetOnAxis(ap=idx[:, 2, 1 - b, j:j + 1], axis=0),
                            in_=o[:, 1 - b, j], in_offset=None, bounds_check=last_node,
                            oob_is_err=False).then_inc(o_out[1 - b], 16)

            def fetch_src(k, b):
                pool.tensor_copy(idx[:, 0, b], K.src[:, bass.ds(k * J, J)]).then_inc(idx_src, 1)
                pool.wait_ge(idx_src, k + 1)
                pool.sem_inc(past, 1)
                fetch(b, xs, 0, xs_full)

            fetch_src(0, 0)
            fetch_src(1, 1)
            steps(pool, step, 4)
            for b in range(2):
                pool.wait_ge(o_out[b], 64 * ((EB - 1 - b) // 2 + 1))

        @block.tensor
        def _(pe):
            def turn(k, b):
                pe.wait_ge(xs_full[b], 32 * (k - b) + 64)
                wait(pe, carried, (k - 1) * J)
                for cc in range(C):
                    for j in range(J):
                        last = pe.transpose(pX[:, cc, j * P:(j + 1) * P], xs[:, b, j, cc * P:(cc + 1) * P], K.ident[:])
                last.then_inc(turned, 1)

            def relation(k, r):
                if isinstance(k, int) and k == 0:
                    pe.wait_ge(K.wl_full, 32)
                pe.wait_ge(xt_lo, k + 1)
                for oc in range(C):
                    if r or not (isinstance(k, int) and k == 0):
                        pe.wait_ge(relu_done, C * (2 * k + r - 1) + oc + 1)
                    for ic in range(C):
                        blk = REL + (r * C + ic) * C + oc
                        last = mm3(pe, pR[:, oc], (K.wl_h[:, blk], K.wl_l[:, blk]), (xt[0][:, ic], xt[1][:, ic]),
                                   ic == 0, ic == C - 1)
                    last.then_inc(rel_done, 1)

            def second_layer(k, b):
                pe.wait_ge(hid_lo, 2 * k + 2)
                wait(pe, u_done, k - 1)
                for j in range(J):
                    cols = slice(j * P, (j + 1) * P)
                    pe.matmul(pM[:, j], has_k[:, b, cols], K.rows[:, 1], start=True, stop=False)
                    for r in range(2):
                        for ic in range(C):
                            last = mm3(pe, pM[:, j], (hidp[r][0][:, ic, cols], hidp[r][1][:, ic, cols]),
                                       (rel_w(K.wl_h, r, ic), rel_w(K.wl_l, r, ic)), False, r == 1 and ic == C - 1)
                last.then_inc(m_done, 1)

            def segment_sums(k, b):
                pe.wait_ge(msg_done, k + 1)
                pe.wait_ge(xt_lo, min(k + 2, EB) if isinstance(k, int) else k + 2)
                for j in range(J):
                    for cc in range(C):
                        last = pe.matmul(pX[:, cc, j * P:(j + 1) * P], msg[:, j, cc * P:(cc + 1) * P], same[:, b, j],
                                         start=True, stop=True)
                last.then_inc(sum_done, 1)

            def gates(k, g):
                for oc in range(C):
                    if g == 0:
                        wait(pe, (m1_on, m2_on)[oc], k)
                    else:
                        pe.wait_ge(gate_on, C * (GATES * k + g - 1) + oc + 1)
                    for ic in range(C):
                        if g == 0 and oc == 0:
                            pe.wait_ge(agg_lo, C * k + ic + 1)
                        blk = IH + ic * GATES * C + g * C + oc
                        last = mm3(pe, pG[:, oc], (K.wl_h[:, blk], K.wl_l[:, blk]), (aggp[0][:, ic], aggp[1][:, ic]),
                                   ic == 0, ic == C - 1)
                    last.then_inc(gate_done, 1)

            def mlp1(k):
                pe.wait_ge(hn_lo, k + 1)
                pe.wait_ge(gate_on, C * (GATES * k + GATES))
                for ic in range(C):
                    last = mm3(pe, pG[:, 0], (K.wl_h[:, M1 + ic], K.wl_l[:, M1 + ic]), (hnp[0][:, ic], hnp[1][:, ic]),
                               ic == 0, ic == C - 1)
                last.then_inc(m1_done, 1)

            def mlp2(k):
                pe.wait_ge(m1_lo, k + 1)
                mm3(pe, pG[:, 1], (K.wl_h[:, M2], K.wl_l[:, M2]), (m1p[0][:], m1p[1][:]), True, True).then_inc(m2_done, 1)

            def mlp3(k):
                pe.wait_ge(m2_lo, k + 1)
                pe.wait_ge(msg_done, min(k + 2, EB) if isinstance(k, int) else k + 2)
                for j in range(J):
                    cols = slice(j * P, (j + 1) * P)
                    last = mm3(pe, pM[:, j], (m2p[0][:, cols], m2p[1][:, cols]), (w3(K.wl_h), w3(K.wl_l)), True, True)
                last.then_inc(y_done, 1)

            def step(k, b):
                if real(k + 1):
                    relation(k + 1, 0)
                if real(k - 1):
                    mlp2(k - 1)
                if real(k + 1):
                    relation(k + 1, 1)
                if real(k):
                    gates(k, 0)
                if real(k - 1):
                    mlp3(k - 1)
                if real(k):
                    gates(k, 1)
                if real(k + 2):
                    turn(k + 2, b)
                if real(k):
                    gates(k, 2)
                if real(k + 1):
                    second_layer(k + 1, 1 - b)
                if real(k):
                    mlp1(k)
                if real(k + 1):
                    segment_sums(k + 1, 1 - b)

            steps(pe, step)

        @block.scalar
        def _(act):
            def relation(k, r):
                wait(act, m_done, k)
                for cc in range(C):
                    act.wait_ge(rel_done, C * (2 * k + r) + cc + 1)
                    act.activation(hid[r][:, cc], pR[:, cc], ACT.Relu,
                                   bias=K.rel_b[:, r * C + cc:r * C + cc + 1]).then_inc(relu_done, 1)

            def relation_hi(k, r):
                act.wait_ge(mult_done, 2 * k + r + 1)
                act.activation(hidp[r][0][:], hid[r][:], ACT.Copy).then_inc(hid_hi, 1)

            def gates(k, g, func):
                for cc in range(C):
                    act.wait_ge(gate_done, C * (GATES * k + g) + cc + 1)
                    act.activation(gate[g][:, cc], pG[:, cc], func,
                                   bias=K.gate_b[:, g * C + cc:g * C + cc + 1]).then_inc(gate_on, 1)

            def step(k, b):
                if real(k + 1):
                    relation(k + 1, 0)
                if real(k):
                    act.wait_ge(carried, J * k + J)
                    for cc in range(C):
                        act.activation(aggp[0][:, cc], agg[:, cc], ACT.Copy).then_inc(agg_hi, 1)
                if real(k - 1):
                    act.wait_ge(m2_done, k)
                    wait(act, y_done, k - 1)
                    act.activation(m2[:], pG[:, 1], ACT.Relu, bias=K.m_b[:, 1:2]).then_inc(m2_on, 1)
                    act.wait_ge(m2_on, k)
                    act.activation(m2p[0][:], m2[:], ACT.Copy).then_inc(m2_hi, 1)
                if real(k + 1):
                    relation(k + 1, 1)
                if real(k):
                    gates(k, 0, ACT.Sigmoid)
                if real(k + 1):
                    relation_hi(k + 1, 0)
                if real(k):
                    gates(k, 1, ACT.Tanh)
                if real(k + 1):
                    relation_hi(k + 1, 1)
                if real(k + 2):
                    act.wait_ge(turned, k + 3)
                    wait(act, rel_done, C * (2 * k + 4))
                    act.activation(xt[0][:], pX[:], ACT.Copy).then_inc(xt_hi, 1)
                if real(k):
                    act.wait_ge(cell_done, k + 1)
                    act.activation(cell_t[:], cell[:], ACT.Tanh).then_inc(cell_on, 1)
                if real(k):
                    gates(k, 2, ACT.Sigmoid)
                    act.wait_ge(hn_done, k + 1)
                    act.activation(hnp[0][:], hn[:], ACT.Copy).then_inc(hn_hi, 1)
                if real(k + 1):
                    act.wait_ge(m_done, k + 2)
                    wait(act, sum_done, k + 1)
                    act.activation(msg[:], pM[:], ACT.Relu).then_inc(msg_done, 1)
                if real(k):
                    act.wait_ge(m1_done, k + 1)
                    act.activation(m1[:], pG[:, 0], ACT.Relu, bias=K.m_b[:, 0:1]).then_inc(m1_on, 1)
                    act.wait_ge(m1_on, k + 1)
                    act.activation(m1p[0][:], m1[:], ACT.Copy).then_inc(m1_hi, 1)

            steps(act, step)

        @block.vector
        def _(dve):
            def low(parts, whole, hi_done, lo_done, count):
                dve.wait_ge(hi_done, count)
                dve.tensor_tensor(out=parts[1][:], in0=whole, in1=parts[0][:].bitcast(F32), op=ALU.subtract).then_inc(lo_done, 1)

            def masks(k, b):
                dve.wait_ge(rows_full[b], 16 * (k - b) + 32)
                wait(dve, mult_done, 2 * k - 2)
                wait(dve, sum_done, k - 1)
                rows = dst_row[:, b].rearrange("p (j e) -> p j e", j=J)
                for out, key in ((same, K.dst_f), (cont, K.prev)):
                    cols = key[:, bass.ds(k * J, J)].rearrange("p (j o) -> p j o", o=1).to_broadcast([P, J, P])
                    dve.tensor_tensor(out=out[:, b], in0=rows, in1=cols, op=ALU.is_equal)
                for r in range(2):
                    dve.tensor_scalar(out=has_rel[:, b, r], in0=rel_row[:, b], scalar1=float(r), scalar2=None, op0=ALU.is_equal)
                dve.tensor_scalar(out=has_k[:, b], in0=rel_row[0:4, b], scalar1=K.row_rel[:, 0:1], scalar2=None,
                                  op0=ALU.is_equal).then_inc(masked, 1)

            def carry(k, b):
                dve.wait_ge(sum_done, k + 1)
                wait(dve, agg_lo, C * k)
                for j in range(J):
                    wait(dve, carried, J * k + j)
                    before = j * P - 1 if j else B - 1
                    for cc in range(C):
                        cols = slice(j * P, (j + 1) * P)
                        last = dve.scalar_tensor_tensor(out=agg[:, cc, cols], in0=cont[:, b, j],
                                                        scalar=agg[:, cc, before:before + 1], in1=pX[:, cc, cols],
                                                        op0=ALU.mult, op1=ALU.add)
                    last.then_inc(carried, 1)

            def step(k, b):
                if real(k):
                    for cc in range(C):
                        dve.wait_ge(agg_hi, C * k + cc + 1)
                        dve.tensor_tensor(out=aggp[1][:, cc], in0=agg[:, cc], in1=aggp[0][:, cc].bitcast(F32),
                                          op=ALU.subtract).then_inc(agg_lo, 1)
                if real(k - 1):
                    low(m2p, m2[:], m2_hi, m2_lo, k)
                if real(k - 1):
                    dve.wait_ge(y_done, k)
                    dve.wait_ge(biased, k)
                    wait(dve, o_done, k - 1)
                    dve.tensor_tensor(out=u[:], in0=pM[:], in1=xd[:, 1 - b], op=ALU.add).then_inc(u_done, 1)
                if real(k + 1):
                    low(hidp[0], hid[0][:], hid_hi, hid_lo, 2 * k + 3)
                if real(k):
                    dve.wait_ge(gate_on, C * (GATES * k + 2))
                    dve.tensor_tensor(out=cell[:], in0=gate[0][:], in1=gate[1][:], op=ALU.mult).then_inc(cell_done, 1)
                if real(k + 1):
                    low(hidp[1], hid[1][:], hid_hi, hid_lo, 2 * k + 4)
                if real(k - 1):
                    dve.wait_ge(u_done, k)
                    row_stats(dve, st, u, st_done)
                if real(k - 1):
                    dve.wait_ge(st_done, k)
                    row_moments(dve, mv, st, dve_past, mv_done)
                if real(k):
                    dve.wait_ge(gate_on, C * (GATES * k + GATES))
                    dve.wait_ge(cell_on, k + 1)
                    dve.tensor_tensor(out=hn[:], in0=gate[2][:], in1=cell_t[:], op=ALU.mult).then_inc(hn_done, 1)
                if real(k + 2):
                    low(xt, pX[:], xt_hi, xt_lo, k + 3)
                if real(k):
                    low(hnp, hn[:], hn_hi, hn_lo, k + 1)
                if real(k + 2):
                    masks(k + 2, b)
                if real(k - 1):
                    dve.wait_ge(rs_done, k)
                    if not (isinstance(k, int) and k < 3):
                        dve.wait_ge(o_out[1 - b], (k - 1 - (1 - b)) * 32)
                    for j in range(J):
                        last = dve.tensor_scalar(out=o[:, 1 - b, j], in0=u[:, j], scalar1=mv[:, j, 0:1],
                                                 scalar2=rs[:, j:j + 1], op0=ALU.subtract, op1=ALU.mult)
                    last.then_inc(o_done, 1)
                if real(k):
                    low(m1p, m1[:], m1_hi, m1_lo, k + 1)
                if real(k + 1):
                    carry(k + 1, 1 - b)

            dve.memset(agg[:], 0.0).then_inc(agg_clear, 1)
            dve.wait_ge(agg_clear, 1)
            steps(dve, step)


class Persistent:

    def __init__(self, nc, c, S):
        def sb(name, shape, dt=F32):
            return c.enter_context(nc.sbuf_tensor("k_" + name, shape, dt))

        self.ident = sb("ident", [P, P])
        self.ones = sb("ones", [P, P], F32R)
        self.w0_h, self.w0_l = sb("w0_h", [P, 3, C, F], F32R), sb("w0_l", [P, 3, C, F], F32R)
        self.rows, self.row_rel = sb("rows", [4, 2, F], F32R), sb("row_rel", [4, 1])
        self.src, self.dst_gather = sb("src", [P, S.TC], I32), sb("dst_gather", [P, S.TC], I32)
        self.target = sb("target", [P, S.TC], I32)
        self.dst_f = sb("dst_f", [P, S.TC])
        self.prev, self.prev_row = sb("prev", [P, S.TC]), sb("prev_row", [P, S.TC])
        self.part_i, self.part, self.is_last = sb("part_i", [P, 1], I32), sb("part", [P, 1]), sb("is_last", [P, 1])
        self.minus_half = sb("minus_half", [P, 2 * J])
        self.rel_b, self.m_b, self.gate_b = sb("rel_b", [P, 2 * C]), sb("m_b", [P, 2]), sb("gate_b", [P, GATES * C])
        self.bn, self.coef2 = sb("bn", [P, 6, C]), sb("coef2", [P, 2, C])
        self.b3, self.base = sb("b3", [P, F]), sb("base", [P, F])
        self.copied = c.enter_context(nc.semaphore("copied"))
        self.wl_full = c.enter_context(nc.semaphore("wl_full"))


def build(nc, A, nodes, edges):
    S = Shapes(nodes, edges)
    for name, shape in (("y", (S.N, F)), ("x1", (S.N, F)),
                        ("h1", (S.NB, P, C * B)), ("h2", (S.NB, P, C * B))):
        A[name] = nc.dram_tensor(f"scratch_{name}", shape, F32, kind="Internal").ap()
    for name in ("wl_h", "wl_l"):
        A[name] = nc.dram_tensor(f"scratch_{name}", (P, NBLK * P), F32, kind="Internal").ap()
    with ExitStack() as c:
        def sb(name, shape, dt=F32):
            return nc.sbuf_tensor("k_" + name, shape, dt)

        K = Persistent(nc, c, S)
        with sb("wl_h0", [P, NBLK, P], F32R) as K.wl_h, sb("wl_l0", [P, NBLK, P], F32R) as K.wl_l:
            setup(nc, A, K, S)
        with sb("sums", [P, S.TC, F]) as K.sums:
            edges0(nc, A, K, S)
            scatter0(nc, A, K, S)
            with sb("stats", [P, C, S.NB, 6]) as K.stats, sb("stats2", [P, C, S.NB, 6]) as K.stats2:
                dense1(nc, A, K, S)
                dense2(nc, A, K, S)
        with sb("wl_h1", [P, NBLK, P], F32R) as K.wl_h, sb("wl_l1", [P, NBLK, P], F32R) as K.wl_l:
            dense3(nc, A, K, S)
            edges1(nc, A, K, S)


_INS = {"x": "x", "src": "src", "dst": "dst", "attr": "edge_attr_256", "bases": "edge_attr_256_n2",
        "rel": "edge_type_2", "W_pre": "L0_gnn_W_pre", "b_pre": "L0_gnn_b_pre", "W1": "L0_gnn_W1", "b1": "L0_gnn_b1",
        "g1": "L0_gnn_g1", "be1": "L0_gnn_be1", "W2": "L0_gnn_W2", "b2": "L0_gnn_b2", "g2": "L0_gnn_g2",
        "be2": "L0_gnn_be2", "W_rel": "L1_gnn_W_rel", "b_rel": "L1_gnn_b_rel", "W_ih": "L1_gnn_W_ih",
        "b_ih": "L1_gnn_b_ih", "b_hh": "L1_gnn_b_hh", "M_W1": "L1_gnn_W1", "M_b1": "L1_gnn_b1", "M_W2": "L1_gnn_W2",
        "M_b2": "L1_gnn_b2", "M_W3": "L1_gnn_W3", "M_b3": "L1_gnn_b3"}


def kernel(**inputs):
    import concourse.bacc as bacc
    from concourse.bass_utils import run_bass_kernel_spmd

    nc = bacc.Bacc("TRN2", target_bir_lowering=False, num_devices=1)
    arrays, A = {}, {}
    for short, name in _INS.items():
        a = np.ascontiguousarray(inputs[name])
        arrays[f"in_{name}"] = a
        A[short] = nc.dram_tensor(f"in_{name}", a.shape, mybir.dt.from_np(a.dtype), kind="ExternalInput").ap()
    nodes, edges = inputs["x"].shape[0], inputs["src"].shape[0]
    A["out"] = nc.dram_tensor("out_0", (nodes, F), F32, kind="ExternalOutput").ap()
    build(nc, A, nodes, edges)
    return run_bass_kernel_spmd(nc, [arrays], core_ids=[0]).results[0]["out_0"]
```
